# Optimizing a Trainium2 kernel written in Bass

```python
import numpy as np
import jax
import jax.numpy as jnp

def _softmax(x, axis=-1):
    return jax.nn.softmax(x, axis=axis)

def _gelu(x):
    return jax.nn.gelu(x, approximate=True)

def _silu(x):
    return jax.nn.silu(x)

def _sigmoid(x):
    return jax.nn.sigmoid(x)

def _layernorm(x, axis=-1, eps=1e-05):
    m = jnp.mean(x, axis=axis, keepdims=True)
    v = jnp.var(x, axis=axis, keepdims=True)
    return (x - m) / jnp.sqrt(v + eps)

def _scatter_add(tgt, idx, src, axis=0):
    return tgt.at[idx].add(src)

def _segment_sum(src, seg, n):
    return jax.ops.segment_sum(src, seg, n)
kernel_name = 'mk_conv_attn_hybrid_d2_conv_nchw256_r4_436eb7'

def setup_inputs(seed: int=0):
    np.random.seed(seed)
    _w = jnp.asarray

    def _rec_inputs():
        import jax
        import jax.numpy as jnp
        _gk = jax.random.key(seed)
        x = -0.0003929 + 0.9999 * jax.random.normal(jax.random.fold_in(_gk, 1), (16, 64, 16, 16), jnp.float32)
        return x
    x = _rec_inputs()

    def _L0_conv_setup():
        import jax, jax.numpy as jnp
        import numpy as np
        B, D, LP, P = (16, 64, 16, 16)
        N = 64
        F = LP * P
        HID = 128
        NODE_SLICES = {'A': (0, 32), 'B': (32, 48), 'C': (48, 64)}
        EDGE_TYPES = [('A', 'B'), ('B', 'A'), ('A', 'C'), ('C', 'A'), ('B', 'C'), ('C', 'B'), ('A', 'A'), ('B', 'B'), ('C', 'C')]
        E = len(EDGE_TYPES)
        ks = jax.random.split(jax.random.key(seed), 8)
        s = lambda fan: 1.0 / np.sqrt(fan)
        return {'x': jax.random.normal(ks[0], (B, D, LP, P), jnp.float32), 'W1': jax.random.normal(ks[1], (D, N), jnp.float32) * s(D), 'b1': jnp.zeros((N,), jnp.float32), 'Wl': jax.random.normal(ks[2], (E, F, HID), jnp.float32) * s(F), 'bl': jnp.zeros((E, HID), jnp.float32), 'Wr': jax.random.normal(ks[3], (E, F, HID), jnp.float32) * s(F), 'Wf': jax.random.normal(ks[4], (HID, F), jnp.float32) * s(HID), 'bf': jnp.zeros((F,), jnp.float32), 'W2': jax.random.normal(ks[5], (N, D), jnp.float32) * s(N), 'b2': jnp.zeros((D,), jnp.float32), 'period': P}
    _L0_conv_all = _L0_conv_setup()
    _L0_conv_in = {k: v for k, v in _L0_conv_all.items() if k in ('W1', 'b1', 'Wl', 'bl', 'Wr', 'Wf', 'bf', 'W2', 'b2')}
    del _L0_conv_all

    def _L1_attn_setup():
        import jax, jax.numpy as jnp
        import numpy as np
        B, T, D = (4, 1024, 64)
        EXPAND, D_STATE = (2, 16)
        INNER = D * EXPAND
        key = jax.random.key(seed)
        ks = jax.random.split(key, 8)
        s = 0.02
        return {'x': jax.random.normal(ks[0], (B, T, D), jnp.float32), 'W_in': jax.random.normal(ks[1], (D, 2 * INNER), jnp.float32) * s, 'b_in': jnp.zeros((2 * INNER,), jnp.float32), 'W_conv': jax.random.normal(ks[2], (INNER, INNER), jnp.float32) * s, 'b_conv': jnp.zeros((INNER,), jnp.float32), 'A_log': jax.random.normal(ks[3], (INNER, D_STATE), jnp.float32) * 0.01, 'W_bc': jax.random.normal(ks[4], (INNER, 2 * D_STATE), jnp.float32) * s, 'b_bc': jnp.zeros((2 * D_STATE,), jnp.float32), 'W_dt': jax.random.normal(ks[5], (INNER, INNER), jnp.float32) * s, 'b_dt': jnp.zeros((INNER,), jnp.float32), 'W_out': jax.random.normal(ks[6], (INNER, D), jnp.float32) * s, 'b_out': jnp.zeros((D,), jnp.float32)}
    _L1_attn_all = _L1_attn_setup()
    _L1_attn_in = {k: v for k, v in _L1_attn_all.items() if k in ('W_in', 'b_in', 'W_conv', 'b_conv', 'A_log', 'W_bc', 'b_bc', 'W_dt', 'b_dt', 'W_out', 'b_out')}
    del _L1_attn_all

    def _L1_ffn_setup():
        import jax, jax.numpy as jnp
        import numpy as np
        TOP_K = 2
        LN_EPS = 1e-05
        key = jax.random.key(seed)
        ks = jax.random.split(key, 8)
        B, S, D, E, H = (16, 256, 64, 8, 256)
        x = jax.random.normal(ks[0], (B, S, D), dtype=jnp.float32)
        Wr = jax.random.normal(ks[1], (D, E), dtype=jnp.float32) * 0.1
        br = jnp.zeros((E,), dtype=jnp.float32)
        ln_g = jnp.ones((E, D), dtype=jnp.float32)
        ln_b = jnp.zeros((E, D), dtype=jnp.float32)
        W1 = jax.random.normal(ks[2], (E, D, H), dtype=jnp.float32) * (1.0 / np.sqrt(D))
        b1 = jnp.zeros((E, H), dtype=jnp.float32)
        W2 = jax.random.normal(ks[3], (E, H, D), dtype=jnp.float32) * (1.0 / np.sqrt(H))
        b2 = jnp.zeros((E, D), dtype=jnp.float32)
        return {'x': x, 'Wr': Wr, 'br': br, 'ln_g': ln_g, 'ln_b': ln_b, 'W1': W1, 'b1': b1, 'W2': W2, 'b2': b2}
    _L1_ffn_all = _L1_ffn_setup()
    _L1_ffn_in = {k: v for k, v in _L1_ffn_all.items() if k in ('Wr', 'br', 'ln_g', 'ln_b', 'W1', 'b1', 'W2', 'b2')}
    del _L1_ffn_all
    return {'x': x, 'L0_conv_W1': _L0_conv_in['W1'], 'L0_conv_b1': _L0_conv_in['b1'], 'L0_conv_Wl': _L0_conv_in['Wl'], 'L0_conv_bl': _L0_conv_in['bl'], 'L0_conv_Wr': _L0_conv_in['Wr'], 'L0_conv_Wf': _L0_conv_in['Wf'], 'L0_conv_bf': _L0_conv_in['bf'], 'L0_conv_W2': _L0_conv_in['W2'], 'L0_conv_b2': _L0_conv_in['b2'], 'L1_attn_W_in': _L1_attn_in['W_in'], 'L1_attn_b_in': _L1_attn_in['b_in'], 'L1_attn_W_conv': _L1_attn_in['W_conv'], 'L1_attn_b_conv': _L1_attn_in['b_conv'], 'L1_attn_A_log': _L1_attn_in['A_log'], 'L1_attn_W_bc': _L1_attn_in['W_bc'], 'L1_attn_b_bc': _L1_attn_in['b_bc'], 'L1_attn_W_dt': _L1_attn_in['W_dt'], 'L1_attn_b_dt': _L1_attn_in['b_dt'], 'L1_attn_W_out': _L1_attn_in['W_out'], 'L1_attn_b_out': _L1_attn_in['b_out'], 'L1_ffn_Wr': _L1_ffn_in['Wr'], 'L1_ffn_br': _L1_ffn_in['br'], 'L1_ffn_ln_g': _L1_ffn_in['ln_g'], 'L1_ffn_ln_b': _L1_ffn_in['ln_b'], 'L1_ffn_W1': _L1_ffn_in['W1'], 'L1_ffn_b1': _L1_ffn_in['b1'], 'L1_ffn_W2': _L1_ffn_in['W2'], 'L1_ffn_b2': _L1_ffn_in['b2']}

def reference(x, L0_conv_W1, L0_conv_b1, L0_conv_Wl, L0_conv_bl, L0_conv_Wr, L0_conv_Wf, L0_conv_bf, L0_conv_W2, L0_conv_b2, L1_attn_W_in, L1_attn_b_in, L1_attn_W_conv, L1_attn_b_conv, L1_attn_A_log, L1_attn_W_bc, L1_attn_b_bc, L1_attn_W_dt, L1_attn_b_dt, L1_attn_W_out, L1_attn_b_out, L1_ffn_Wr, L1_ffn_br, L1_ffn_ln_g, L1_ffn_ln_b, L1_ffn_W1, L1_ffn_b1, L1_ffn_W2, L1_ffn_b2):
    import jax
    import jax.numpy as jnp

    def _L0_conv_ref(x, W1, b1, Wl, bl, Wr, Wf, bf, W2, b2, period):
        import jax, jax.numpy as jnp
        import numpy as np
        B, D, LP, P = (16, 64, 16, 16)
        N = 64
        F = LP * P
        HID = 128
        NODE_SLICES = {'A': (0, 32), 'B': (32, 48), 'C': (48, 64)}
        EDGE_TYPES = [('A', 'B'), ('B', 'A'), ('A', 'C'), ('C', 'A'), ('B', 'C'), ('C', 'B'), ('A', 'A'), ('B', 'B'), ('C', 'C')]
        E = len(EDGE_TYPES)
        b = x.shape[0]
        h = jnp.einsum('bdlp,dn->bnlp', x, W1) + b1[None, :, None, None]
        hf = h.reshape(b, N, -1)
        xt = {t: hf[:, lo:hi] for t, (lo, hi) in NODE_SLICES.items()}
        mu = {t: v.mean(axis=1) for t, v in xt.items()}
        contribs = {t: [] for t in NODE_SLICES}
        for i, (s_t, d_t) in enumerate(EDGE_TYPES):
            c = (mu[s_t] @ Wl[i] + bl[i])[:, None, :] + jnp.einsum('bnf,fh->bnh', xt[d_t], Wr[i])
            contribs[d_t].append(c)
        outs = []
        for t in ('A', 'B', 'C'):
            o = jnp.mean(jnp.stack(contribs[t]), axis=0)
            o = jax.nn.relu(o) @ Wf + bf
            outs.append(o)
        out = jnp.concatenate(outs, axis=1)
        out = out.reshape(b, N, -1, period)
        y = jnp.einsum('bnlp,nd->bdlp', out, W2) + b2[None, :, None, None]
        return y

    def _L1_attn_ref(x, W_in, b_in, W_conv, b_conv, A_log, W_bc, b_bc, W_dt, b_dt, W_out, b_out):
        import jax, jax.numpy as jnp
        import numpy as np
        B, T, D = (4, 1024, 64)
        EXPAND, D_STATE = (2, 16)
        INNER = D * EXPAND
        x_proj = x @ W_in + b_in
        x_main, x_gate = jnp.split(x_proj, 2, axis=-1)
        x_conv = jax.nn.silu(x_main @ W_conv + b_conv)
        A = -jnp.exp(A_log)
        x_bc = x_conv @ W_bc + b_bc
        B_proj, C_proj = jnp.split(x_bc, 2, axis=-1)
        dt = jax.nn.softplus(x_conv @ W_dt + b_dt)

        def scan_step(h, inputs):
            x_t, dt_t, B_t, C_t = inputs
            A_bar = jnp.exp(dt_t[..., None] * A)
            B_bar = dt_t[..., None] * B_t[:, None, :]
            h_new = A_bar * h + B_bar * x_t[..., None]
            y_t = (h_new * C_t[:, None, :]).sum(axis=-1)
            return (h_new, y_t)
        tm = lambda a: jnp.swapaxes(a, 0, 1)
        h0 = jnp.zeros((x.shape[0], INNER, D_STATE), x_conv.dtype)
        _, y_seq = jax.lax.scan(scan_step, h0, (tm(x_conv), tm(dt), tm(B_proj), tm(C_proj)))
        y = jnp.swapaxes(y_seq, 0, 1)
        y = y * jax.nn.silu(x_gate)
        return y @ W_out + b_out

    def _L1_ffn_ref(x, Wr, br, ln_g, ln_b, W1, b1, W2, b2):
        import jax, jax.numpy as jnp
        import numpy as np
        TOP_K = 2
        LN_EPS = 1e-05
        B, S, D = x.shape
        N = B * S
        xt = x.reshape(N, D)
        logits = xt @ Wr + br
        probs = jax.nn.softmax(logits, axis=-1)
        top_p, top_idx = jax.lax.top_k(probs, TOP_K)
        weights = top_p / top_p.sum(axis=-1, keepdims=True)
        mu = xt.mean(axis=-1, keepdims=True)
        var = ((xt - mu) ** 2).mean(axis=-1, keepdims=True)
        xn = (xt - mu) * jax.lax.rsqrt(var + LN_EPS)
        xe = xn[None, :, :] * ln_g[:, None, :] + ln_b[:, None, :]
        h = jax.nn.gelu(jnp.einsum('end,edh->enh', xe, W1) + b1[:, None, :], approximate=False)
        y = jnp.einsum('enh,ehd->end', h, W2) + b2[:, None, :]
        y_tok = jnp.transpose(y, (1, 0, 2))
        sel = jnp.take_along_axis(y_tok, top_idx[:, :, None], axis=1)
        out = (weights[:, :, None] * sel).sum(axis=1)
        return out.reshape(B, S, D)

    def _gn(v, G=32, eps=1e-05):
        B_, C_, H_, W_ = v.shape
        g = v.reshape(B_, G, C_ // G, H_, W_)
        m = jnp.mean(g, axis=(2, 3, 4), keepdims=True)
        s = jnp.var(g, axis=(2, 3, 4), keepdims=True)
        return ((g - m) / jnp.sqrt(s + eps)).reshape(v.shape)

    def _ln_c(v, eps=1e-06):
        m = jnp.mean(v, axis=1, keepdims=True)
        s = jnp.var(v, axis=1, keepdims=True)
        return (v - m) / jnp.sqrt(s + eps)

    def _ln_t(v, eps=1e-05):
        m = jnp.mean(v, axis=-1, keepdims=True)
        s = jnp.var(v, axis=-1, keepdims=True)
        return (v - m) / jnp.sqrt(s + eps)

    def _to_tokens(v):
        B_, C_, H_, W_ = v.shape
        return v.reshape(B_, C_, H_ * W_).transpose(0, 2, 1)

    def _from_tokens(t, like):
        B_, C_, H_, W_ = like.shape
        return t.transpose(0, 2, 1).reshape(B_, C_, H_, W_)
    x = x + _L0_conv_ref(_gn(x), L0_conv_W1, L0_conv_b1, L0_conv_Wl, L0_conv_bl, L0_conv_Wr, L0_conv_Wf, L0_conv_bf, L0_conv_W2, L0_conv_b2, 16)
    t = _to_tokens(x)
    t = t + _L1_attn_ref(_ln_t(t), L1_attn_W_in, L1_attn_b_in, L1_attn_W_conv, L1_attn_b_conv, L1_attn_A_log, L1_attn_W_bc, L1_attn_b_bc, L1_attn_W_dt, L1_attn_b_dt, L1_attn_W_out, L1_attn_b_out)
    t = t + _L1_ffn_ref(_ln_t(t), L1_ffn_Wr, L1_ffn_br, L1_ffn_ln_g, L1_ffn_ln_b, L1_ffn_W1, L1_ffn_b1, L1_ffn_W2, L1_ffn_b2)
    x = _from_tokens(t, x)
    return x

_drawn_inputs = setup_inputs


def setup_inputs(seed=0):
    import zlib

    import numpy as np

    out = dict(_drawn_inputs(seed))
    spreads = {'L0_conv_b1': (0.0, 0.1),
     'L0_conv_bl': (0.0, 0.1),
     'L0_conv_bf': (0.0, 0.1),
     'L0_conv_b2': (0.0, 0.1),
     'L1_attn_b_in': (0.0, 0.8),
     'L1_attn_b_conv': (0.0, 0.8),
     'L1_attn_b_bc': (0.0, 0.8),
     'L1_attn_b_dt': (0.0, 0.8),
     'L1_attn_b_out': (0.0, 2.0),
     'L1_ffn_br': (0.0, 2.0),
     'L1_ffn_ln_g': (1.0, 0.6),
     'L1_ffn_ln_b': (0.0, 0.8),
     'L1_ffn_b1': (0.0, 2.0),
     'L1_ffn_b2': (0.0, 2.0)}
    factors = {'L1_attn_W_in': 8.0,
     'L1_attn_W_conv': 8.0,
     'L1_attn_A_log': 8.0,
     'L1_attn_W_bc': 8.0,
     'L1_attn_W_dt': 8.0,
     'L1_attn_W_out': 8.0,
     'L1_ffn_Wr': 8.0,
     'L1_ffn_W1': 8.0,
     'L1_ffn_W2': 8.0}
    for name, (base, spread) in spreads.items():
        noise = np.random.default_rng([zlib.crc32(name.encode()), seed]).standard_normal(out[name].shape)
        drawn = base * np.exp(spread * noise) if base else spread * noise
        out[name] = jnp.asarray(drawn.astype(out[name].dtype))
    for name, factor in factors.items():
        out[name] = (out[name] * factor).astype(out[name].dtype)
    return out
```

```python
import concourse.bass as bass
from concourse import mybir
from contextlib import ExitStack

B, D, HW = 16, 64, 256
HALF = B // 2
G = HALF
LOOPS = (G - 4) // 2
T = 2 * HW
HID, NODES, NE = 128, 64, 9
NODE = {"A": (0, 32), "B": (32, 48), "C": (48, 64)}
EDGES = [("A", "B"), ("B", "A"), ("A", "C"), ("C", "A"), ("B", "C"), ("C", "B"), ("A", "A"), ("B", "B"), ("C", "C")]
INNER, ST = 128, 16
BLK = INNER // ST
NBLK = INNER // BLK
SLOTS = NBLK // 2
EXP, FH = 8, 256
KC = FH // 128
NROWS = EXP * KC + NE + 2 + 1 + 1 + 1 + EXP + 1 + EXP + EXP
EPS = 1e-5

R, _at = {}, 0
for _name, _n in (("b1", EXP * KC), ("bl", NE), ("b_in", 2), ("b_conv", 1), ("b_dt", 1),
                  ("b_out", 1), ("b2", EXP), ("cb2", 1), ("ln_g", EXP), ("ln_b", EXP)):
    R[_name] = _at
    _at += _n
assert _at == NROWS

SEMS = """ld_x ld_rows ld_wgn ld_wr ld_wl ld_wf ld_wssm ld_ffn ld_dup
gn_stat gn_agg gn_avg gn_dev gn_dsq gn_var gn_ln gn_rs gn_shift gn_out
k_zero k_ident k_sel k_misc k_dve k_selu k_selw k_mask k_col0 bbx bbcol
ht_mm ht_ev mu_ready wrs_ready o_mm c_mm bls_ready c_ev r_add r_ready out_mm out_ev y_mm res_ready
prep1 cols_ev wmt_ev a_exp a_neg a_selx prep2 wz_hi wz_lo bz b1c wbr ffn_g ffn_h ffn_l selx
cen1 sq1 var1 ln1 rs1 xn1 xh1 xl1 z_mm g_mm xc sg
dtz_mm b_mm c_rep_mm sp_abs sp_exp sp_ln sp_relu bs cs dt u uh ul dt_out dt_in0 dt_in1 dt_in2 dt_in3 aexp
ub bm scan cm ysum
yg po t1 cen2 sq2 var2 ln2 rs2 r2 vq lnq rq tn xn2 xh2 xl2
lg lgb m1 dd ex s1 ms1 o1 e2 m2 s2 s2r ms2 o2 den rden num wt vhi vlo wtr wtc wb_mm wb
f1 gl f2 me acc out_sem""".split()


def rep(ap, axis, n):
    v = ap.unsqueeze(axis)
    return v.broadcast_to([*v.shape[:axis], n, *v.shape[axis + 1:]])


def build(nc, x, cW1, cb1, Wl, bl, Wr, Wf, bf, cW2, cb2, W_in, b_in, W_conv, b_conv, A_log, W_bc, b_bc,
          W_dt, b_dt, W_out, b_out, fWr, fbr, ln_g, ln_b, W1, b1, W2, b2, out):
    fp32, f32r = mybir.dt.float32, mybir.dt.float32r
    ALU = mybir.AluOpType
    ACT = mybir.ActivationFunctionType
    AX = mybir.AxisListType.X

    dt_dram = nc.dram_tensor("dt_scratch", (2, INNER, T), fp32, kind="Internal").ap()

    ctx = ExitStack()
    with ctx:
        def sb(name, shape, dt=fp32):
            return ctx.enter_context(nc.sbuf_tensor(name, shape, dt))

        S = {n: ctx.enter_context(nc.semaphore(n)) for n in SEMS}

        def since(eng, name, count):
            if isinstance(count, int) and count <= 0:
                return
            eng.wait_ge(S[name], count)

        res = sb("res", [128, HALF * HW])
        stats = sb("stats", [128, HALF, 6])
        mv = sb("mv", [128, HALF, 2])
        gdev = sb("gdev", [128, 2, HALF])
        gvar = sb("gvar", [128, HALF])
        gmean = sb("gmean", [128, HALF])
        grs = sb("grs", [128, HALF])
        cW2bd = sb("cW2bd", [128, 128])
        mu = sb("mu", [128, 3, 2, B])
        blsum = sb("blsum", [128, 3])
        cT = sb("cT", [128, 3, B])
        ident = sb("ident", [128, 128])
        cen_m = sb("cen_m", [128, 128])
        avg_m = sb("avg_m", [128, 128])
        pair_m = sb("pair_m", [128, 128])
        gsel = sb("gsel", [128, NBLK])
        mask8 = sb("mask8", [128, BLK])
        selU = sb("selU", [128, NBLK, 128], f32r)
        selS = sb("selS", [128, 4, 32])
        selW = sb("selW", [32, EXP, 128], f32r)
        rank = sb("rank", [128, 4, EXP])
        epst = sb("epst", [128, 1])
        onet = sb("onet", [128, 1])
        cols = sb("cols", [128, NROWS])
        bbc = sb("bbc", [2, ST])
        bbx = sb("bbx", [2, ST, BLK])
        bbcol = sb("bbcol", [128, 2])
        Wins = sb("Wins", [128, 2 * INNER])
        WmT2 = sb("WmT2", [128, 2, 64])
        WzH = sb("WzH", [128, 128], f32r)
        WzL = sb("WzL", [128, 128], f32r)
        WgH = sb("WgH", [128, 128], f32r)
        WgL = sb("WgL", [128, 128], f32r)
        bz = sb("bz", [128, 1])
        Als = sb("Als", [128, ST])
        Aneg = sb("Aneg", [128, NBLK])
        Aexp = sb("Aexp", [128, NBLK])
        Wbcs = sb("Wbcs", [128, 2 * ST])
        Wrep = sb("Wrep", [128, 2, ST, BLK])
        Wdts = sb("Wdts", [128, INNER])
        Wouts = sb("Wouts", [128, D])
        Wrt = sb("Wrt", [128, 2, EXP])
        brs = sb("brs", [128, EXP])
        W1H = sb("W1H", [128, EXP, FH], f32r)
        W1L = sb("W1L", [128, EXP, FH], f32r)
        W2s = sb("W2s", [128, EXP, KC, D])
        b1c = sb("b1c", [128, EXP * KC])
        sq = sb("sq", [128, HW])
        rs = sb("rs", [128, HW])
        xnt = sb("xnt", [64, T])
        Xs = sb("Xs", [128, T], f32r)
        xc = sb("xc", [128, T])
        sg = sb("sg", [128, 2, T])
        sp = sb("sp", [128, T])
        rl = sb("rl", [128, T])
        u = rl
        dts = sb("dts", [128, 2, T])
        uh = sb("uh", [128, 2, T], f32r)
        ul = sb("ul", [128, 2, T], f32r)
        Bs = sb("Bs", [128, 2, T])
        Cs = sb("Cs", [128, 2, T])
        av = sb("av", [128, 2, NBLK, T])
        hs = sb("hs", [128, 4, 2, T])
        ygs = sb("ygs", [128, T])
        t1 = sb("t1s", [128, 2, HW])
        sq2 = sb("sq2s", [128, HW])
        rs2 = sb("rs2s", [128, HW])
        r2s = sb("r2s", [128, HW])
        vqs = sb("vqs", [128, HW])
        rqs = sb("rqs", [128, HW])
        tns = sb("tns", [128, HW])
        xnt2 = sb("xnt2", [64, T])
        X2 = sb("X2", [128, T], f32r)
        rt = sb("rt", [128, 12, 4, EXP])
        rv = sb("rv", [128, 8, 4])
        vv = sb("vv", [128, 2, 2, 2, EXP])
        wT = sb("wT", [32, HW], f32r)
        wbs = sb("wbs", [128, EXP, HW])
        hb = sb("hb", [128, 4, T])
        mes = sb("mes", [128, 2, HW])
        acc = sb("accs", [128, 2, HW])

        def within(buf, at, shape):
            n = 1
            for d in shape:
                n *= d
            names = "abcd"[:len(shape)]
            view = buf[:, at:at + n]
            if len(shape) > 1:
                view = view.rearrange("p (" + " ".join(names) + ") -> p " + " ".join(names), **dict(zip(names[1:], shape[1:])))
            return view, at + n

        gn = hs[:, :, :, :].rearrange("p a b t -> p (a b t)")[:, 0:HALF * HW].rearrange("p (b f) -> p b f", b=HALF)
        buf0 = av[:, 0].rearrange("p m t -> p (m t)")
        buf1 = av[:, 1].rearrange("p m t -> p (m t)")
        Wrs_raw, at = within(buf0, 0, [NE, 2, HID])
        Wls, at = within(buf0, at, [NE, 2, HID])
        hT, at = within(buf0, at, [2, B, NODES])
        W1g, at = within(buf1, 0, [EXP, FH])
        W1r, at = within(buf1, at, [EXP, FH])
        Wrsum, at = within(buf1, at, [3, 2, HID])
        rT, at = within(buf1, at, [B, NODES])
        selWf, at = within(buf1[0:32], at, [EXP, 2, 64])

        Wfs, at = within(buf1, at, [HW])
        bfs, at = within(buf1, at, [HW])
        Wcv, at = within(buf1, at, [INNER])
        Asel, at = within(buf1, at, [ST, BLK])
        cb1s, at = within(buf1, at, [NODES])
        cW1s, at = within(buf1, at, [NODES])
        rows, at = within(buf1[0:NROWS], at, [128])
        assert at <= NBLK * T

        P = ctx.enter_context(nc.psum_tensor("P", [128, 8, 512], fp32))
        XA, XB, XC, YS = 4, 5, 6, 7

        v = nc.vector
        a_ = nc.scalar
        pe = nc.tensor
        gp = nc.gpsimd

        def node_edges(t):
            return [i for i, (_, d) in enumerate(EDGES) if d == t]

        def block_of(m):
            return 4 * (m % 4) + m // 4

        xv = x.rearrange("(h b) d l w -> h d b (l w)", h=2)
        ov = out.rearrange("(h b) d l w -> h d b (l w)", h=2)

        block = ctx.enter_context(nc.Block())

        def sp_dt(sp_, g, p):
            since(sp_, "dt", g + 1)
            sp_.dma_start(dt_dram[p], dts[:, p, :]).then_inc(S["dt_out"], 16)
            sp_.wait_ge(S["dt_out"], 16 * (g + 1))
            since(sp_, "scan", SLOTS * (g - 1))
            if isinstance(g, int) and g < 2:
                sp_.wait_ge(S["k_col0"], g + 1)
            src = dt_dram[p].rearrange("(q k e) (h f) -> k q e h f", k=4, e=BLK, h=2)
            for k in range(4):
                for q in range(4):
                    sp_.dma_start(av[:, p, 4 * k + q, :].rearrange("p (h f) -> p h f", h=2)[:, :, 1:HW],
                                  rep(src[k, q, :, :, 1:HW], 0, ST)).then_inc(S[f"dt_in{k}"], 16)

        def sp_out(sp_, g, p):
            sp_.wait_ge(S["acc"], EXP * (g + 1))
            for h in range(2):
                sp_.dma_start(ov[h, :, bass.ds(g, 1), :], acc[64 * h:64 * h + 64, p:p + 1, :]).then_inc(S["out_sem"], 16)

        @block.sync
        def _(sp_):
            for h in range(2):
                sp_.dma_start(res[64 * h:64 * h + 64, :].rearrange("p (b f) -> p b f", b=HALF), xv[h]).then_inc(S["ld_x"], 16)
            for h in range(2):
                sp_.dma_start(cW1s[64 * h:64 * h + 64, :], cW1).then_inc(S["ld_wgn"], 16)
            sp_.dma_start(cb1s[:, :], rep(cb1, 0, 128)).then_inc(S["ld_wgn"], 16)
            for fh in range(2):
                sp_.dma_start(Wrs_raw[:, :, fh, :], Wr[:, 128 * fh:128 * fh + 128, :].rearrange("i f n -> f i n")).then_inc(S["ld_wr"], 16)
            for fh in range(2):
                sp_.dma_start(Wls[:, :, fh, :], Wl[:, 128 * fh:128 * fh + 128, :].rearrange("i f n -> f i n")).then_inc(S["ld_wl"], 16)
            sp_.dma_start(Wfs[:, :], Wf).then_inc(S["ld_wf"], 16)
            sp_.dma_start(bfs[:, :], rep(bf, 0, 128)).then_inc(S["ld_wf"], 16)
            sp_.wait_ge(S["k_zero"], 8)
            for h in range(2):
                sp_.dma_start(cW2bd[64 * h:64 * h + 64, 64 * h:64 * h + 64], cW2).then_inc(S["ld_wf"], 16)
            for h in range(2):
                sp_.dma_start(W1r[64 * h:64 * h + 64, :, :], W1.rearrange("e d n -> d e n")).then_inc(S["ld_ffn"], 16)
            sp_.dma_start(W2s[:, :, :, :], W2.rearrange("e (k p) d -> p e k d", p=128)).then_inc(S["ld_dup"], 16)
            for h in range(2):
                sp_.dma_start(Wrt[64 * h:64 * h + 64, h, :], fWr).then_inc(S["ld_dup"], 16)
            sp_.dma_start(brs[:, :], rep(fbr, 0, 128)).then_inc(S["ld_dup"], 16)
            for g in range(3):
                sp_dt(sp_, g, g % 2)
            sp_out(sp_, 0, 0)
            with sp_.Fori(0, LOOPS) as it:
                for par in range(2):
                    i = it * 2 + (2 + par)
                    sp_dt(sp_, i + 1, 1 - par)
                    sp_out(sp_, i - 1, 1 - par)
            sp_dt(sp_, G - 1, 1)
            sp_out(sp_, G - 3, 1)
            sp_out(sp_, G - 2, 0)
            sp_out(sp_, G - 1, 1)
            sp_.wait_ge(S["out_sem"], 32 * G)

        def pool_slot(eng, g, p, n):
            eng.wait_ge(S["scan"], SLOTS * g + n + 1)
            if n == 0:
                eng.wait_ge(S["cs"], g + 1)
            gp.tensor_tensor(hs[:, n % 4, :, :], hs[:, n % 4, :, :],
                             rep(Cs[:, p, :], 1, 2), ALU.mult).then_inc(S["cm"], 1)

        def pool_acc(eng, g, p, e):
            eng.wait_ge(S["me"], EXP * g + e + 1)
            if e == 0:
                since(eng, "out_sem", 32 * g)
                prev = t1[:, p, :]
            else:
                eng.wait_ge(S["acc"], EXP * g + e)
                prev = acc[:, p, :]
            gp.tensor_tensor(acc[:, p, :], prev, mes[:, e % 2, :], ALU.add).then_inc(S["acc"], 1)

        @block.gpsimd
        def _(eng):
            def row(name, ap, off=0):
                eng.dma_start(rows[R[name] + off:R[name] + off + ap.shape[0], 0:ap.shape[-1]], ap).then_inc(S["ld_rows"], 16)
            row("b1", b1.rearrange("e (k f) -> (e k) f", f=128))
            row("bl", bl)
            row("b_in", b_in.rearrange("(a f) -> a f", f=128))
            row("b_conv", b_conv.unsqueeze(0))
            row("b_dt", b_dt.unsqueeze(0))
            eng.dma_start(bbc[:, :], b_bc.rearrange("(a s) -> a s", a=2)).then_inc(S["ld_rows"], 16)
            for h in range(2):
                for name, ap in (("b_out", b_out.unsqueeze(0)), ("b2", b2), ("cb2", cb2.unsqueeze(0)), ("ln_g", ln_g), ("ln_b", ln_b)):
                    n = ap.shape[0]
                    eng.dma_start(rows[R[name]:R[name] + n, 64 * h:64 * h + 64], ap).then_inc(S["ld_rows"], 16)
            gp.memset(ident[:, :], 0.0).then_inc(S["k_zero"], 1)
            gp.memset(avg_m[:, :], 0.0).then_inc(S["k_zero"], 1)
            gp.memset(cW2bd[:, :], 0.0).then_inc(S["k_zero"], 1)
            gp.memset(Wrt[:, :, :], 0.0).then_inc(S["k_zero"], 1)
            gp.memset(pair_m[:, :], 0.5).then_inc(S["k_zero"], 1)
            gp.memset(gsel[:, :], 1.0).then_inc(S["k_zero"], 1)
            gp.memset(selWf[:, :, :, :], 0.0).then_inc(S["k_zero"], 1)
            gp.memset(selS[:, :, :], 0.0).then_inc(S["k_zero"], 1)
            eng.wait_ge(S["k_zero"], 8)
            for h in range(2):
                gp.memset(avg_m[64 * h:64 * h + 64, 64 * h:64 * h + 64], 1.0 / D).then_inc(S["k_misc"], 1)
            eng.wait_ge(S["k_misc"], 2)
            gp.affine_select(out=ident[:, :], in_=ident[:, :], compare_op=ALU.not_equal, fill=1.0, base=0,
                             pattern=[[-1, 128]], channel_multiplier=1).then_inc(S["k_ident"], 1)
            pv = pair_m[:, :].rearrange("p (a b) -> p a b", b=2)
            gp.affine_select(out=pv, in_=pv, compare_op=ALU.is_ge, fill=0.0, base=0,
                             pattern=[[-2, 64], [0, 2]], channel_multiplier=1).then_inc(S["k_sel"], 1)
            gp.affine_select(out=gsel[:, :], in_=gsel[:, :], compare_op=ALU.is_ge, fill=0.0, base=0,
                             pattern=[[-BLK, NBLK]], channel_multiplier=1).then_inc(S["k_sel"], 1)
            gp.affine_select(out=selWf[:, :, :, :], in_=selWf[:, :, :, :], compare_op=ALU.not_equal, fill=1.0, base=0,
                             pattern=[[-1, EXP], [-2 * EXP, 2], [0, 64]], channel_multiplier=1).then_inc(S["k_sel"], 1)
            eng.wait_ge(S["k_sel"], 3)
            gp.affine_select(out=pv, in_=pv, compare_op=ALU.is_ge, fill=0.0, base=1,
                             pattern=[[2, 64], [0, 2]], channel_multiplier=-1).then_inc(S["k_sel"], 1)
            gp.affine_select(out=gsel[:, :], in_=gsel[:, :], compare_op=ALU.is_ge, fill=0.0, base=BLK - 1,
                             pattern=[[BLK, NBLK]], channel_multiplier=-1).then_inc(S["k_sel"], 1)
            gp.affine_select(out=selWf[:, :, :, :], in_=selWf[:, :, :, :], compare_op=ALU.not_equal, fill=1.0, base=-EXP,
                             pattern=[[-1, EXP], [-2 * EXP, 2], [0, 64]], channel_multiplier=1).then_inc(S["k_sel"], 1)
            gp.memset(epst[:, :], EPS).then_inc(S["k_misc"], 1)
            gp.memset(onet[:, :], 1.0).then_inc(S["k_misc"], 1)
            for e in range(EXP):
                gp.memset(rank[:, :, e:e + 1], float(EXP - e)).then_inc(S["k_misc"], 1)
            eng.wait_ge(S["k_ident"], 1)
            gp.tensor_tensor(cen_m[:, :], ident[:, :], avg_m[:, :], ALU.subtract).then_inc(S["k_misc"], 1)
            eng.wait_ge(S["ld_wr"], 32)
            for ti, t in enumerate("ABC"):
                e0, e1, e2 = node_edges(t)
                gp.tensor_tensor(Wrsum[:, ti], Wrs_raw[:, e0], Wrs_raw[:, e1], ALU.add).then_inc(S["wrs_ready"], 1)
            eng.wait_ge(S["wrs_ready"], 3)
            for ti, t in enumerate("ABC"):
                gp.tensor_tensor(Wrsum[:, ti], Wrsum[:, ti], Wrs_raw[:, node_edges(t)[2]], ALU.add).then_inc(S["wrs_ready"], 1)
            eng.wait_ge(S["ld_ffn"], 32)
            eng.wait_ge(S["cols_ev"], 1)
            gp.tensor_tensor(W1g[:, :, :], W1r[:, :, :], rep(cols[:, R["ln_g"]:R["ln_g"] + EXP], 2, FH),
                             ALU.mult).then_inc(S["ffn_g"], 1)
            eng.wait_ge(S["ffn_h"], 1)
            gp.tensor_tensor(W1L[:, :, :], W1g[:, :, :], W1H[:, :, :], ALU.subtract).then_inc(S["ffn_l"], 1)

            eng.wait_ge(S["res_ready"], 4)
            gp.memset(av[:, 0, :, :].rearrange("p m (h f) -> p m h f", h=2)[:, :, :, 0:1], 0.0).then_inc(S["k_col0"], 1)
            eng.wait_ge(S["ffn_l"], 1)
            eng.wait_ge(S["prep2"], 3)
            eng.wait_ge(S["k_selw"], 1)
            gp.memset(av[:, 1, :, :].rearrange("p m (h f) -> p m h f", h=2)[:, :, :, 0:1], 0.0).then_inc(S["k_col0"], 1)

            def body(i, p, prev):
                for n in range(SLOTS):
                    pool_slot(eng, i, p, n)
                    if prev is not None and n >= SLOTS // 2:
                        for e in range(2 * n - SLOTS, 2 * n - SLOTS + 2):
                            pool_acc(eng, prev, 1 - p, e)

            body(0, 0, None)
            body(1, 1, 0)
            with eng.Fori(0, LOOPS) as it:
                for par in range(2):
                    i = it * 2 + (2 + par)
                    body(i, par, i - 1)
            body(G - 2, 0, G - 3)
            body(G - 1, 1, G - 2)
            for e in range(EXP):
                pool_acc(eng, G - 1, 1, e)

        def act_lnA1(eng, g):
            eng.wait_ge(S["cen1"], g + 1)
            since(eng, "var1", g)
            a_.activation(sq[:, :], P[:, XA, 0:HW], ACT.Square).then_inc(S["sq1"], 1)

        def act_lnA2(eng, g):
            eng.wait_ge(S["var1"], g + 1)
            since(eng, "xn1", 2 * g)
            a_.activation(rs[:, :], P[:, XA, HW:T], ACT.Ln, bias=epst[:, 0:1]).then_inc(S["ln1"], 1)
            eng.wait_ge(S["ln1"], g + 1)
            a_.activation(rs[:, :], rs[:, :], ACT.Exp, scale=-0.5).then_inc(S["rs1"], 1)

        def act_silu(eng, g, p):
            eng.wait_ge(S["z_mm"], g + 1)
            since(eng, "c_rep_mm", g)
            since(eng, "u", g)
            a_.activation(xc[:, :], P[:, XA, :], ACT.Silu, bias=bz[:, 0:1]).then_inc(S["xc"], 1)
            eng.wait_ge(S["g_mm"], g + 1)
            since(eng, "yg", g - 1)
            a_.activation(sg[:, p, :], P[:, XC, :], ACT.Silu, bias=cols[:, R["b_in"] + 1:R["b_in"] + 2]).then_inc(S["sg"], 1)
            a_.preload_act_table_set("natural_log_exp_and_others")

        def act_softplus(eng, g, p):
            bdt = cols[:, R["b_dt"]:R["b_dt"] + 1]
            eng.wait_ge(S["dtz_mm"], g + 1)
            since(eng, "ul", g)
            a_.activation(sp[:, :], P[:, XA, :], ACT.Abs, bias=bdt).then_inc(S["sp_abs"], 1)
            a_.activation(rl[:, :], P[:, XA, :], ACT.Relu, bias=bdt).then_inc(S["sp_relu"], 1)
            eng.wait_ge(S["sp_abs"], g + 1)
            a_.activation(sp[:, :], sp[:, :], ACT.Exp, scale=-1.0).then_inc(S["sp_exp"], 1)
            eng.wait_ge(S["b_mm"], g + 1)
            since(eng, "bm", SLOTS * (g - 1))
            a_.activation(Bs[:, p, :], P[:, XC, :], ACT.Identity, bias=bbcol[:, 0:1]).then_inc(S["bs"], 1)
            eng.wait_ge(S["sp_exp"], g + 1)
            a_.activation(sp[:, :], sp[:, :], ACT.Ln, bias=onet[:, 0:1]).then_inc(S["sp_ln"], 1)
            eng.wait_ge(S["c_rep_mm"], g + 1)
            since(eng, "cm", SLOTS * (g - 1))
            a_.activation(Cs[:, p, :], P[:, XC, :], ACT.Identity, bias=bbcol[:, 1:2]).then_inc(S["cs"], 1)

        def act_decay(eng, g, p, lo, hi):
            for m in range(lo, hi):
                if m % 4 == 0:
                    eng.wait_ge(S[f"dt_in{m // 4}"], 64 * (g + 1))
                j = block_of(m)
                steps = av[:, p, m, :].rearrange("p (h f) -> p h f", h=2)[:, :, 1:HW]
                a_.activation(steps, steps, ACT.Exp, scale=Aneg[:, j:j + 1]).then_inc(S["aexp"], 1)

        def act_lnF1(eng, g):
            eng.wait_ge(S["cen2"], g + 1)
            since(eng, "var2", g)
            a_.activation(sq2[:, :], P[:, XB, 0:HW], ACT.Square).then_inc(S["sq2"], 1)

        def act_lnF2(eng, g):
            eng.wait_ge(S["var2"], g + 1)
            since(eng, "tn", g)
            since(eng, "r2", g)
            a_.activation(rs2[:, :], P[:, XB, HW:T], ACT.Ln, bias=epst[:, 0:1]).then_inc(S["ln2"], 1)
            eng.wait_ge(S["ln2"], g + 1)
            a_.activation(rs2[:, :], rs2[:, :], ACT.Exp, scale=-0.5).then_inc(S["rs2"], 1)
            eng.wait_ge(S["rs2"], g + 1)
            since(eng, "vq", g)
            a_.activation(r2s[:, :], rs2[:, :], ACT.Square).then_inc(S["r2"], 1)

        def act_lnF3(eng, g):
            eng.wait_ge(S["vq"], g + 1)
            since(eng, "xn2", 2 * g)
            a_.activation(rqs[:, :], vqs[:, :], ACT.Ln, bias=epst[:, 0:1]).then_inc(S["lnq"], 1)
            eng.wait_ge(S["lnq"], g + 1)
            a_.activation(rqs[:, :], rqs[:, :], ACT.Exp, scale=-0.5).then_inc(S["rq"], 1)

        def act_router(eng, g):
            eng.wait_ge(S["dd"], g + 1)
            a_.activation(rt[:, 2], rt[:, 1], ACT.Exp).then_inc(S["ex"], 1)

        def act_wb(eng, g):
            eng.wait_ge(S["wtr"], 2 * (g + 1))
            since(eng, "wb_mm", EXP * g)
            a_.activation(wT[:, :], P[0:32, XB, 0:HW], ACT.Copy).then_inc(S["wtc"], 1)
            for r in range(EXP // 2):
                eng.wait_ge(S["wb_mm"], EXP * g + 2 * r + 2)
                if r == 0:
                    since(eng, "me", EXP * g)
                a_.activation(wbs[:, 2 * r:2 * r + 2, :].rearrange("p e f -> p (e f)"), P[:, (XB, XC)[r % 2], :], ACT.Copy).then_inc(S["wb"], 1)

        def act_gelu(eng, g):
            for r in range(EXP * KC):
                eng.wait_ge(S["f1"], EXP * KC * g + r + 1)
                since(eng, "f2", EXP * KC * g + max(r - 3, 0))
                a_.activation(hb[:, r % 4, :], P[:, (XA, XB)[r % 2], :], ACT.Gelu, bias=b1c[:, r:r + 1]).then_inc(S["gl"], 1)
            a_.preload_act_table_set("natural_log_exp_and_others")

        @block.scalar
        def _(eng):
            for ap, src, sem in ((Wcv[:, :], W_conv, "ld_wssm"), (Als[:, :], A_log, "ld_wssm"), (Wins[0:64, :], W_in, "ld_wssm"),
                                 (Wins[64:128, :], W_in, "ld_wssm"), (Wbcs[:, :], W_bc, "ld_wssm"), (Wdts[:, :], W_dt, "ld_wssm"),
                                 (Wouts[:, :], W_out, "ld_wssm")):
                eng.dma_start(ap, src).then_inc(S[sem], 16)
            a_.preload_act_table_set("natural_log_exp_and_others")
            eng.wait_ge(S["k_misc"], 3)
            eng.wait_ge(S["gn_var"], 1)
            a_.activation(gvar[:, :], P[:, 0, 2 * HALF:3 * HALF], ACT.Ln, bias=epst[:, 0:1]).then_inc(S["gn_ln"], 1)
            eng.wait_ge(S["gn_ln"], 1)
            a_.activation(grs[:, :], gvar[:, :], ACT.Exp, scale=-0.5).then_inc(S["gn_rs"], 1)
            eng.wait_ge(S["prep1"], 4)
            eng.wait_ge(S["wmt_ev"], 2)
            a_.activation(Aexp[:, :], P[:, 7, 192:192 + NBLK], ACT.Exp).then_inc(S["a_exp"], 1)
            eng.wait_ge(S["ffn_g"], 1)
            a_.activation(W1H[:, :, :], W1g[:, :, :], ACT.Copy).then_inc(S["ffn_h"], 1)
            eng.wait_ge(S["r_add"], 3)
            a_.activation(rT[:, :, :], rT[:, :, :], ACT.Relu, scale=1.0 / 3.0).then_inc(S["r_ready"], 1)

            def a_stage(g, p):
                act_lnA1(eng, g); act_lnA2(eng, g); act_silu(eng, g, p); act_softplus(eng, g, p)

            def body(i, p, nxt, prev):
                q = 1 - p
                act_decay(eng, i, p, 4, 6)
                if nxt is not None:
                    act_lnA1(eng, nxt)
                    act_lnA2(eng, nxt)
                act_decay(eng, i, p, 6, 8)
                if prev is not None:
                    act_lnF1(eng, prev)
                    act_lnF2(eng, prev)
                if nxt is not None:
                    act_silu(eng, nxt, q)
                if prev is not None:
                    act_lnF3(eng, prev)
                if nxt is not None:
                    act_softplus(eng, nxt, q)
                act_decay(eng, i, p, 8, 10)
                if prev is not None:
                    act_router(eng, prev)
                act_decay(eng, i, p, 10, NBLK)
                if prev is not None:
                    act_wb(eng, prev)
                    act_gelu(eng, prev)
                if nxt is not None:
                    act_decay(eng, nxt, q, 0, 4)

            a_stage(0, 0)
            act_decay(eng, 0, 0, 0, 4)
            body(0, 0, 1, None)
            body(1, 1, 2, 0)
            with eng.Fori(0, LOOPS) as it:
                for par in range(2):
                    i = it * 2 + (2 + par)
                    body(i, par, i + 1, i - 1)
            body(G - 2, 0, G - 1, G - 3)
            body(G - 1, 1, None, G - 2)
            act_lnF1(eng, G - 1)
            act_lnF2(eng, G - 1)
            act_lnF3(eng, G - 1)
            act_router(eng, G - 1)
            act_wb(eng, G - 1)
            act_gelu(eng, G - 1)

        def dve_bm(eng, g, p, n):
            ub = P[:, 2 * (n % 2):2 * (n % 2) + 2, :]
            eng.wait_ge(S["ub"], SLOTS * g + n + 1)
            if n == 0:
                eng.wait_ge(S["bs"], g + 1)
            v.tensor_tensor(ub, ub, rep(Bs[:, p, :], 1, 2), ALU.mult).then_inc(S["bm"], 1)

        def dve_scan(eng, g, p, n):
            ub = P[:, 2 * (n % 2):2 * (n % 2) + 2, :]
            eng.wait_ge(S["bm"], SLOTS * g + n + 1)
            eng.wait_ge(S["aexp"], NBLK * g + 2 * n + 2)
            since(eng, "ysum", 4 * g + n // 2 - 1)
            v.tensor_tensor_scan(hs[:, n % 4, :, :].rearrange("p a t -> p (a t)"),
                                 av[:, p, 2 * n:2 * n + 2, :].rearrange("p a t -> p (a t)"),
                                 ub.rearrange("p a t -> p (a t)"), 0.0, ALU.mult, ALU.add).then_inc(S["scan"], 1)

        def dve_xn(eng, g):
            eng.wait_ge(S["rs1"], g + 1)
            since(eng, "xl1", g)
            for h in range(2):
                q = slice(64 * h, 64 * h + 64)
                v.tensor_tensor(xnt[:, HW * h:HW * h + HW], P[q, XA, 0:HW], rs[q, :], ALU.mult).then_inc(S["xn1"], 1)
            eng.wait_ge(S["xn1"], 2 * (g + 1))
            since(eng, "g_mm", g)
            v.tensor_copy(Xs[0:64, :], xnt[:, :]).then_inc(S["xh1"], 1)
            eng.wait_ge(S["xh1"], g + 1)
            v.tensor_tensor(Xs[64:128, :], xnt[:, :], Xs[0:64, :], ALU.subtract).then_inc(S["xl1"], 1)

        def dve_u(eng, g, p):
            eng.wait_ge(S["sp_ln"], g + 1)
            eng.wait_ge(S["sp_relu"], g + 1)
            since(eng, "dt_out", 16 * (g - 1))
            v.tensor_tensor(dts[:, p, :], rl[:, :], sp[:, :], ALU.add).then_inc(S["dt"], 1)
            eng.wait_ge(S["dt"], g + 1)
            since(eng, "ul", g)
            v.tensor_tensor(u[:, :], dts[:, p, :], xc[:, :], ALU.mult).then_inc(S["u"], 1)
            eng.wait_ge(S["u"], g + 1)
            since(eng, "ub", SLOTS * (g - 1))
            v.tensor_copy(uh[:, p, :], u[:, :]).then_inc(S["uh"], 1)
            eng.wait_ge(S["uh"], g + 1)
            v.tensor_tensor(ul[:, p, :], u[:, :], uh[:, p, :], ALU.subtract).then_inc(S["ul"], 1)

        def dve_gate(eng, g, p):
            eng.wait_ge(S["ysum"], 4 * (g + 1))
            since(eng, "po", g)
            v.tensor_tensor(ygs[:, :], P[:, YS, :], sg[:, p, :], ALU.mult).then_inc(S["yg"], 1)

        def dve_t1(eng, g, p):
            eng.wait_ge(S["po"], g + 1)
            v.scalar_tensor_tensor(out=t1[:, p, :], in0=P[:, XC, 0:HW], scalar=cols[:, R["b_out"]:R["b_out"] + 1],
                                   in1=res[:, bass.ds(g * HW, HW)], op0=ALU.add, op1=ALU.add).then_inc(S["t1"], 1)

        def dve_lnF(eng, g):
            eng.wait_ge(S["rs2"], g + 1)
            since(eng, "lg", g)
            since(eng, "xn2", 2 * g)
            v.tensor_tensor(tns[:, :], P[:, XB, 0:HW], rs2[:, :], ALU.mult).then_inc(S["tn"], 1)
            eng.wait_ge(S["r2"], g + 1)
            since(eng, "lnq", g)
            v.tensor_tensor(vqs[:, :], P[:, XB, HW:T], r2s[:, :], ALU.mult).then_inc(S["vq"], 1)

        def dve_xn2(eng, g):
            eng.wait_ge(S["rq"], g + 1)
            eng.wait_ge(S["tn"], g + 1)
            since(eng, "xl2", g)
            for h in range(2):
                q = slice(64 * h, 64 * h + 64)
                v.tensor_tensor(xnt2[:, HW * h:HW * h + HW], tns[q, :], rqs[q, :], ALU.mult).then_inc(S["xn2"], 1)
            eng.wait_ge(S["xn2"], 2 * (g + 1))
            since(eng, "f1", EXP * KC * g)
            v.tensor_copy(X2[0:64, :], xnt2[:, :]).then_inc(S["xh2"], 1)
            eng.wait_ge(S["xh2"], g + 1)
            v.tensor_tensor(X2[64:128, :], xnt2[:, :], X2[0:64, :], ALU.subtract).then_inc(S["xl2"], 1)

        def dve_router1(eng, g):
            eng.wait_ge(S["lg"], 2 * (g + 1))
            since(eng, "dd", g)
            v.tensor_tensor(rt[:, 0], P[:, XB, 0:4 * EXP].rearrange("p (c e) -> p c e", e=EXP),
                            rep(brs[:, :], 1, 4), ALU.add).then_inc(S["lgb"], 1)
            eng.wait_ge(S["lgb"], g + 1)
            v.tensor_reduce(rv[:, 0], rt[:, 0], AX, ALU.max).then_inc(S["m1"], 1)
            eng.wait_ge(S["m1"], g + 1)
            since(eng, "ex", g)
            v.tensor_tensor(rt[:, 1], rt[:, 0], rep(rv[:, 0], 2, EXP), ALU.subtract).then_inc(S["dd"], 1)

        def dve_router2(eng, g):
            bc = lambda k: rep(rv[:, k], 2, EXP)
            eng.wait_ge(S["ex"], g + 1)
            v.scalar_tensor_tensor(out=rt[:, 3], in0=rt[:, 2], scalar=1.0, in1=rank[:, :, :], op0=ALU.is_ge, op1=ALU.mult).then_inc(S["s1"], 1)
            eng.wait_ge(S["s1"], g + 1)
            v.tensor_reduce(rv[:, 1], rt[:, 3], AX, ALU.max).then_inc(S["ms1"], 1)
            eng.wait_ge(S["ms1"], g + 1)
            v.tensor_tensor(rt[:, 4], rt[:, 3], bc(1), ALU.is_equal).then_inc(S["o1"], 1)
            eng.wait_ge(S["o1"], g + 1)
            v.scalar_tensor_tensor(out=rt[:, 5], in0=rt[:, 4], scalar=-2.0, in1=rt[:, 2], op0=ALU.mult, op1=ALU.add).then_inc(S["e2"], 1)
            eng.wait_ge(S["e2"], g + 1)
            v.tensor_reduce(rv[:, 2], rt[:, 5], AX, ALU.max).then_inc(S["m2"], 1)
            eng.wait_ge(S["m2"], g + 1)
            v.tensor_tensor(rt[:, 6], rt[:, 5], bc(2), ALU.is_equal).then_inc(S["s2"], 1)
            v.tensor_scalar(rv[:, 4], rv[:, 2], 1.0, None, ALU.add).then_inc(S["den"], 1)
            eng.wait_ge(S["s2"], g + 1)
            v.tensor_tensor(rt[:, 7], rt[:, 6], rank[:, :, :], ALU.mult).then_inc(S["s2r"], 1)
            eng.wait_ge(S["den"], g + 1)
            v.reciprocal(rv[:, 5], rv[:, 4]).then_inc(S["rden"], 1)
            eng.wait_ge(S["s2r"], g + 1)
            v.tensor_reduce(rv[:, 3], rt[:, 7], AX, ALU.max).then_inc(S["ms2"], 1)
            eng.wait_ge(S["ms2"], g + 1)
            v.tensor_tensor(rt[:, 8], rt[:, 7], bc(3), ALU.is_equal).then_inc(S["o2"], 1)
            eng.wait_ge(S["o2"], g + 1)
            v.tensor_tensor(rt[:, 9], rt[:, 8], bc(2), ALU.mult).then_inc(S["num"], 1)
            eng.wait_ge(S["num"], g + 1)
            v.tensor_tensor(rt[:, 10], rt[:, 9], rt[:, 4], ALU.add).then_inc(S["wt"], 1)
            eng.wait_ge(S["wt"], g + 1)
            eng.wait_ge(S["rden"], g + 1)
            v.tensor_tensor(rt[:, 11], rt[:, 10], bc(5), ALU.mult).then_inc(S["vhi"], 1)
            eng.wait_ge(S["vhi"], 2 * g + 1)
            w4 = rt[:, 11].rearrange("p (q h) e -> p q h e", h=2)
            since(eng, "wtr", 2 * g)
            v.tensor_copy(vv[:, :, :, 0, :].bitcast(f32r), w4).then_inc(S["vhi"], 1)
            eng.wait_ge(S["vhi"], 2 * g + 2)
            v.tensor_tensor(vv[:, :, :, 1, :], w4, vv[:, :, :, 0, :], ALU.subtract).then_inc(S["vlo"], 1)

        def dve_expert(eng, g, e):
            if e % 2 == 0:
                eng.wait_ge(S["f2"], EXP * KC * g + 2 * KC * (e // 2 + 1))
                eng.wait_ge(S["wb"], EXP // 2 * g + e // 2 + 1)
            since(eng, "acc", EXP * g + max(e - 1, 0))
            v.scalar_tensor_tensor(out=mes[:, e % 2, :], in0=P[:, XC, HW * (e % 2):HW * (e % 2) + HW],
                                   scalar=cols[:, R["b2"] + e:R["b2"] + e + 1], in1=wbs[:, e, :],
                                   op0=ALU.add, op1=ALU.mult).then_inc(S["me"], 1)

        @block.vector
        def _(eng):
            eng.wait_ge(S["ld_x"], 32)
            rv3 = res[:, :].rearrange("p (b f) -> p b f", b=HALF)
            for b in range(HALF):
                v.bn_stats(stats[:, b, :], rv3[:, b, :]).then_inc(S["gn_stat"], 1)
            eng.wait_ge(S["gn_stat"], HALF)
            for b in range(HALF):
                v.bn_aggr(mv[:, b, :], stats[:, b, :]).then_inc(S["gn_agg"], 1)
            eng.wait_ge(S["gn_agg"], HALF)
            eng.wait_ge(S["gn_avg"], 1)
            v.tensor_copy(gmean[:, :], P[:, 0, 0:HALF]).then_inc(S["gn_dev"], 1)
            eng.wait_ge(S["gn_dev"], 1)
            v.tensor_tensor(gdev[:, 0, :], mv[:, :, 0], gmean[:, :], ALU.subtract).then_inc(S["gn_dev"], 1)
            eng.wait_ge(S["gn_dev"], 2)
            v.tensor_tensor(gdev[:, 0, :], gdev[:, 0, :], gdev[:, 0, :], ALU.mult).then_inc(S["gn_dsq"], 1)
            eng.wait_ge(S["gn_dsq"], 1)
            v.tensor_tensor(gdev[:, 1, :], gdev[:, 0, :], mv[:, :, 1], ALU.add).then_inc(S["gn_dsq"], 1)
            eng.wait_ge(S["gn_rs"], 1)
            for b in range(HALF):
                v.tensor_scalar(gn[:, b, :], rv3[:, b, :], gmean[:, b:b + 1], grs[:, b:b + 1], ALU.subtract, ALU.mult).then_inc(S["gn_out"], 1)
            eng.wait_ge(S["k_ident"], 1)
            v.tensor_reduce(mask8[:, :], ident[:, :].rearrange("p (j e) -> p e j", e=BLK), AX, ALU.add).then_inc(S["k_mask"], 1)
            eng.wait_ge(S["ld_wssm"], 112)
            eng.wait_ge(S["k_mask"], 1)
            v.tensor_tensor(Asel[:, :, :], rep(Als[:, :], 2, BLK), rep(mask8[:, :], 1, ST), ALU.mult).then_inc(S["a_selx"], 1)
            eng.wait_ge(S["ld_rows"], 16 * 16)
            v.tensor_copy(bbx[:, :, :], rep(bbc[:, :], 2, BLK)).then_inc(S["bbx"], 1)
            eng.wait_ge(S["prep1"], 4)
            v.tensor_copy(bbcol[:, :], P[:, 7, 208:210]).then_inc(S["bbcol"], 1)
            v.tensor_copy(cols[:, :], P[:, 7, 0:NROWS]).then_inc(S["cols_ev"], 1)
            for h in range(2):
                v.tensor_copy(WmT2[:, h, :], P[:, 7, 128:192]).then_inc(S["wmt_ev"], 1)
            eng.wait_ge(S["ld_wgn"], 48)
            for h in range(2):
                for fh in range(2):
                    eng.wait_ge(S["ht_mm"], 2 * h + fh + 1)
                    v.tensor_tensor(hT[:, fh, HALF * h:HALF * h + HALF, :], P[:, 2 * h + fh, :].rearrange("p (b n) -> p b n", n=NODES),
                                    rep(cb1s[:, :], 1, HALF), ALU.add).then_inc(S["ht_ev"], 1)
            eng.wait_ge(S["ht_ev"], 4)
            for ti, t in enumerate("ABC"):
                lo, hi = NODE[t]
                for fh in range(2):
                    v.tensor_reduce(mu[:, ti, fh, :], hT[:, fh, :, lo:hi], AX, ALU.add).then_inc(S["mu_ready"], 1)
            eng.wait_ge(S["mu_ready"], 6)
            for ti, t in enumerate("ABC"):
                lo, hi = NODE[t]
                v.tensor_scalar(mu[:, ti], mu[:, ti], 1.0 / (hi - lo), None, ALU.mult).then_inc(S["mu_ready"], 1)
            eng.wait_ge(S["cols_ev"], 1)
            for ti, t in enumerate("ABC"):
                e0, e1, e2 = (R["bl"] + i for i in node_edges(t))
                v.tensor_tensor(blsum[:, ti:ti + 1], cols[:, e0:e0 + 1], cols[:, e1:e1 + 1], ALU.add).then_inc(S["bls_ready"], 1)
            eng.wait_ge(S["bls_ready"], 3)
            for ti, t in enumerate("ABC"):
                e2 = R["bl"] + node_edges(t)[2]
                v.tensor_tensor(blsum[:, ti:ti + 1], blsum[:, ti:ti + 1], cols[:, e2:e2 + 1], ALU.add).then_inc(S["bls_ready"], 1)
            eng.wait_ge(S["bls_ready"], 6)
            eng.wait_ge(S["prep2"], 3)
            v.tensor_copy(WzH[:, :], P[:, 7, 0:128]).then_inc(S["wz_hi"], 1)
            v.tensor_copy(WgH[:, :], Wins[:, INNER:2 * INNER]).then_inc(S["wz_hi"], 1)
            eng.wait_ge(S["wz_hi"], 2)
            v.tensor_tensor(WzL[:, :], P[:, 7, 0:128], WzH[:, :], ALU.subtract).then_inc(S["wz_lo"], 1)
            v.tensor_tensor(WgL[:, :], Wins[:, INNER:2 * INNER], WgH[:, :], ALU.subtract).then_inc(S["wz_lo"], 1)
            v.tensor_tensor(bz[:, :], P[:, 7, 128:129], cols[:, R["b_conv"]:R["b_conv"] + 1], ALU.add).then_inc(S["bz"], 1)
            v.tensor_tensor(b1c[:, :], P[:, 7, 132:132 + EXP * KC], cols[:, R["b1"]:R["b1"] + EXP * KC], ALU.add).then_inc(S["b1c"], 1)
            eng.wait_ge(S["a_exp"], 1)
            v.tensor_scalar(Aneg[:, :], Aexp[:, :], -1.0, None, ALU.mult).then_inc(S["a_neg"], 1)
            for i in range(2):
                v.tensor_copy(Wrep[:, i], rep(Wbcs[:, ST * i:ST * i + ST], 2, BLK)).then_inc(S["wbr"], 1)
            for ti, t in enumerate("ABC"):
                eng.wait_ge(S["c_mm"], 3)
                v.tensor_scalar(cT[:, ti, :], P[:, 6, B * ti:B * ti + B], blsum[:, ti:ti + 1], None, ALU.add).then_inc(S["c_ev"], 1)
            eng.wait_ge(S["c_ev"], 3)
            eng.wait_ge(S["o_mm"], 3)
            for ti, t in enumerate("ABC"):
                lo, hi = NODE[t]
                n = hi - lo
                bank, at = ((4, 0), (5, 0), (5, B * n))[ti]
                v.tensor_tensor(rT[:, :, lo:hi], P[:, bank, at:at + B * n].rearrange("p (b n) -> p b n", n=n),
                                rep(cT[:, ti, :], 2, n), ALU.add).then_inc(S["r_add"], 1)
            v.tensor_copy(selU[:, :, :].rearrange("p j (s e) -> p j s e", e=BLK),
                          rep(ident[:, :].rearrange("p (j e) -> p j e", e=BLK), 2, ST)).then_inc(S["k_selu"], 1)
            eng.wait_ge(S["k_zero"], 8)
            for k in range(4):
                v.tensor_copy(selS[:, k, BLK * k:BLK * k + BLK], mask8[:, :]).then_inc(S["k_selu"], 1)
            eng.wait_ge(S["k_sel"], 6)
            v.tensor_copy(selW[:, :, :], selWf[:, :, :, :].rearrange("p e h d -> p e (h d)")).then_inc(S["k_selw"], 1)
            eng.wait_ge(S["ld_wf"], 64)
            eng.wait_ge(S["ht_mm"], 4)
            for c in range(4):
                eng.wait_ge(S["out_mm"], c + 1)
                v.tensor_tensor(gn[:, 2 * c:2 * c + 2, :], P[:, c, :].rearrange("p (b f) -> p b f", f=HW),
                                rep(bfs[:, :], 1, 2), ALU.add).then_inc(S["out_ev"], 1)
            for c in range(4):
                eng.wait_ge(S["y_mm"], c + 1)
                v.scalar_tensor_tensor(out=res[:, 512 * c:512 * c + 512], in0=P[:, 4 + c, :], scalar=cols[:, R["cb2"]:R["cb2"] + 1],
                                       in1=res[:, 512 * c:512 * c + 512], op0=ALU.add, op1=ALU.add).then_inc(S["res_ready"], 1)
            eng.wait_ge(S["res_ready"], 4)

            def body(i, p, nxt, prev):
                q = 1 - p
                dve_bm(eng, i, p, 0)
                dve_scan(eng, i, p, 0)
                if prev is not None:
                    dve_gate(eng, prev, q)
                dve_bm(eng, i, p, 1)
                if nxt is not None:
                    dve_xn(eng, nxt)
                if prev is not None:
                    dve_t1(eng, prev, q)
                dve_scan(eng, i, p, 1)
                dve_bm(eng, i, p, 2)
                if prev is not None:
                    dve_lnF(eng, prev)
                dve_scan(eng, i, p, 2)
                if prev is not None:
                    dve_router1(eng, prev)
                    dve_xn2(eng, prev)
                dve_bm(eng, i, p, 3)
                if prev is not None:
                    dve_router2(eng, prev)
                dve_scan(eng, i, p, 3)
                if nxt is not None:
                    dve_u(eng, nxt, q)
                dve_bm(eng, i, p, 4)
                dve_scan(eng, i, p, 4)
                for n in range(5, SLOTS):
                    dve_bm(eng, i, p, n)
                    if prev is not None:
                        dve_expert(eng, prev, 2 * (n - 5))
                        dve_expert(eng, prev, 2 * (n - 5) + 1)
                    dve_scan(eng, i, p, n)
                if prev is not None:
                    dve_expert(eng, prev, EXP - 2)
                    dve_expert(eng, prev, EXP - 1)

            dve_xn(eng, 0)
            dve_u(eng, 0, 0)
            body(0, 0, 1, None)
            body(1, 1, 2, 0)
            with eng.Fori(0, LOOPS) as it:
                for par in range(2):
                    i = it * 2 + (2 + par)
                    body(i, par, i + 1, i - 1)
            body(G - 2, 0, G - 1, G - 3)
            body(G - 1, 1, None, G - 2)
            dve_gate(eng, G - 1, 1)
            dve_t1(eng, G - 1, 1)
            dve_lnF(eng, G - 1)
            dve_xn2(eng, G - 1)
            dve_router1(eng, G - 1)
            dve_router2(eng, G - 1)
            for e in range(EXP):
                dve_expert(eng, G - 1, e)

        def pe_ub(eng, g, p, n):
            if n == 0:
                eng.wait_ge(S["ul"], g + 1)
            since(eng, "scan", SLOTS * g + n - 1)
            for a in range(2):
                j = block_of(2 * n + a)
                bank = 2 * (n % 2) + a
                pe.matmul(P[:, bank, :], selU[:, j, :], uh[:, p, :], start=True, stop=False)
                last = pe.matmul(P[:, bank, :], selU[:, j, :], ul[:, p, :], start=False, stop=True)
            last.then_inc(S["ub"], 1)

        def pe_sum(eng, g, k):
            eng.wait_ge(S["cm"], SLOTS * g + 2 * k + 2)
            if k == 0:
                since(eng, "yg", g)
            for q in range(4):
                n = 2 * k + q // 2
                last = pe.matmul(P[32 * q:32 * q + 32, YS, :], selS[:, k, :], hs[:, n % 4, q % 2, :],
                                 start=(k == 0), stop=(k == 3))
            last.then_inc(S["ysum"], 1)

        def pe_cenA(eng, g):
            since(eng, "gl", EXP * KC * (g - 2) )
            since(eng, "sp_relu", g)
            since(eng, "sp_abs", g)
            pe.matmul(P[:, XA, 0:HW], cen_m[:, :], res[:, bass.ds(g * HW, HW)], start=True, stop=True).then_inc(S["cen1"], 1)

        def pe_varA(eng, g):
            eng.wait_ge(S["sq1"], g + 1)
            pe.matmul(P[:, XA, HW:T], avg_m[:, :], sq[:, :], start=True, stop=True).then_inc(S["var1"], 1)

        def pe_projz(eng, g):
            eng.wait_ge(S["xl1"], g + 1)
            pe.matmul(P[:, XA, :], WzH[:, :], Xs[:, :], start=True, stop=False)
            pe.matmul(P[:, XA, :], WzL[:, :], Xs[:, :], start=False, stop=True).then_inc(S["z_mm"], 1)

        def pe_projg(eng, g):
            since(eng, "t1", g - 1)
            since(eng, "me", EXP * (g - 2))
            since(eng, "cs", g)
            pe.matmul(P[:, XC, :], WgH[:, :], Xs[:, :], start=True, stop=False)
            pe.matmul(P[:, XC, :], WgL[:, :], Xs[:, :], start=False, stop=True).then_inc(S["g_mm"], 1)

        def pe_dtbc(eng, g):
            eng.wait_ge(S["xc"], g + 1)
            pe.matmul(P[:, XA, :], Wdts[:, :], xc[:, :], start=True, stop=True).then_inc(S["dtz_mm"], 1)
            eng.wait_ge(S["sg"], g + 1)
            pe.matmul(P[:, XC, :], Wrep[:, 0].rearrange("p s e -> p (s e)"), xc[:, :], start=True, stop=True).then_inc(S["b_mm"], 1)
            eng.wait_ge(S["bs"], g + 1)
            pe.matmul(P[:, XC, :], Wrep[:, 1].rearrange("p s e -> p (s e)"), xc[:, :], start=True, stop=True).then_inc(S["c_rep_mm"], 1)

        def pe_po(eng, g):
            eng.wait_ge(S["yg"], g + 1)
            since(eng, "me", EXP * g)
            since(eng, "cs", g + 1)
            for h in range(2):
                last = pe.matmul(P[64 * h:64 * h + 64, XC, 0:HW], Wouts[:, :], ygs[:, HW * h:HW * h + HW], start=True, stop=True)
            last.then_inc(S["po"], 1)

        def pe_cenF(eng, g, p):
            eng.wait_ge(S["t1"], g + 1)
            since(eng, "gl", EXP * KC * g)
            pe.matmul(P[:, XB, 0:HW], cen_m[:, :], t1[:, p, :], start=True, stop=True).then_inc(S["cen2"], 1)

        def pe_varF(eng, g):
            eng.wait_ge(S["sq2"], g + 1)
            pe.matmul(P[:, XB, HW:T], avg_m[:, :], sq2[:, :], start=True, stop=True).then_inc(S["var2"], 1)

        def pe_router(eng, g):
            eng.wait_ge(S["tn"], g + 1)
            eng.wait_ge(S["vq"], g + 1)
            for q in range(2):
                pe.matmul(P[:, XB, 2 * EXP * q:2 * EXP * q + 2 * EXP], tns[:, 128 * q:128 * q + 128],
                          Wrt[:, :, :].rearrange("p h e -> p (h e)"), start=True, stop=True).then_inc(S["lg"], 1)

        def pe_wb(eng, g):
            eng.wait_ge(S["vlo"], g + 1)
            for q in range(2):
                pe.transpose(P[0:32, XB, 128 * q:128 * q + 128], vv[:, q].rearrange("p h r e -> p (h r e)"), ident[:, :]).then_inc(S["wtr"], 1)
            eng.wait_ge(S["wtc"], g + 1)
            for e in range(EXP):
                r = e // 2
                if e % 2 == 0 and r >= 2:
                    eng.wait_ge(S["wb"], EXP // 2 * g + r - 1)
                if e == 2:
                    eng.wait_ge(S["cs"], min(g + 2, G) if isinstance(g, int) else g + 2)
                pe.matmul(P[:, (XB, XC)[r % 2], HW * (e % 2):HW * (e % 2) + HW], selW[:, e, :], wT[:, :],
                          start=True, stop=True).then_inc(S["wb_mm"], 1)

        def pe_f1(eng, g, r):
            e, k = r // KC, r % KC
            if r == 0:
                eng.wait_ge(S["xl2"], g + 1)
                eng.wait_ge(S["sp_relu"], min(g + 2, G) if isinstance(g, int) else g + 2)
            if r == 1:
                eng.wait_ge(S["wb"], EXP // 2 * (g + 1))
            if r >= 2:
                eng.wait_ge(S["gl"], EXP * KC * g + r - 1)
            bank = (XA, XB)[r % 2]
            pe.matmul(P[:, bank, :], W1H[:, e, 128 * k:128 * k + 128], X2[:, :], start=True, stop=False)
            pe.matmul(P[:, bank, :], W1L[:, e, 128 * k:128 * k + 128], X2[:, :], start=False, stop=True).then_inc(S["f1"], 1)

        def pe_f2(eng, g, r):
            e, k = r // KC, r % KC
            eng.wait_ge(S["gl"], EXP * KC * g + r + 1)
            if r == 0:
                eng.wait_ge(S["wb"], EXP // 2 * (g + 1))
            if r % (2 * KC) == 0:
                since(eng, "me", EXP * g + r // KC)
            for h in range(2):
                last = pe.matmul(P[64 * h:64 * h + 64, XC, HW * (e % 2):HW * (e % 2) + HW], W2s[:, e, k, :],
                                 hb[:, r % 4, HW * h:HW * h + HW], start=(k == 0), stop=(k == KC - 1))
            last.then_inc(S["f2"], 1)

        def pe_ffn(eng, g, lo, hi):
            for r in range(lo, hi):
                if r < EXP * KC:
                    pe_f1(eng, g, r)
                if r >= 2:
                    pe_f2(eng, g, r - 2)

        @block.tensor
        def _(eng):
            eng.wait_ge(S["k_ident"], 1)
            eng.wait_ge(S["ld_rows"], 16 * 16)
            pe.transpose(P[:, 7, 0:NROWS], rows[:, :], ident[0:NROWS, 0:NROWS]).then_inc(S["prep1"], 1)
            eng.wait_ge(S["ld_wssm"], 112)
            pe.transpose(P[:, 7, 128:192], Wins[0:64, 0:128], ident[0:64, 0:64]).then_inc(S["prep1"], 1)
            eng.wait_ge(S["k_sel"], 6)
            eng.wait_ge(S["gn_agg"], HALF)
            pe.matmul(P[:, 0, 0:HALF], pair_m[:, :], mv[:, :, 0], start=True, stop=True).then_inc(S["gn_avg"], 1)
            eng.wait_ge(S["gn_dsq"], 2)
            pe.matmul(P[:, 0, 2 * HALF:3 * HALF], pair_m[:, :], gdev[:, 1, :], start=True, stop=True).then_inc(S["gn_var"], 1)
            eng.wait_ge(S["a_selx"], 1)
            pe.matmul(P[:, 7, 192:192 + NBLK], Asel[:, :, :].rearrange("p s e -> p (s e)"), gsel[:, :], start=True, stop=True).then_inc(S["prep1"], 1)
            eng.wait_ge(S["bbx"], 1)
            pe.transpose(P[:, 7, 208:210], bbx[:, :, :].rearrange("p s e -> p (s e)"), ident[0:2, 0:2]).then_inc(S["prep1"], 1)
            eng.wait_ge(S["ld_wgn"], 48)
            eng.wait_ge(S["gn_ln"], 1)
            eng.wait_ge(S["gn_out"], HALF)
            for h in range(2):
                for fh in range(2):
                    for b in range(HALF):
                        last = pe.matmul(P[:, 2 * h + fh, NODES * b:NODES * b + NODES], gn[64 * h:64 * h + 64, b, 128 * fh:128 * fh + 128],
                                         cW1s[64 * h:64 * h + 64, :], start=True, stop=True)
                    last.then_inc(S["ht_mm"], 1)
            eng.wait_ge(S["wmt_ev"], 2)
            eng.wait_ge(S["a_exp"], 1)
            pe.matmul(P[:, 7, 0:128], WmT2[:, :, :].rearrange("p h d -> p (h d)"), Wcv[:, :], start=True, stop=True).then_inc(S["prep2"], 1)
            pe.matmul(P[:, 7, 128:129], Wcv[:, :], cols[:, R["b_in"]:R["b_in"] + 1], start=True, stop=True).then_inc(S["prep2"], 1)
            eng.wait_ge(S["ld_ffn"], 32)
            eng.wait_ge(S["cols_ev"], 1)
            eng.wait_ge(S["prep2"], 2)
            for e in range(EXP):
                for k in range(KC):
                    last = pe.matmul(P[:, 7, 132 + KC * e + k:133 + KC * e + k], W1r[0:64, e, 128 * k:128 * k + 128],
                                     cols[0:64, R["ln_b"] + e:R["ln_b"] + e + 1], start=True, stop=True)
            last.then_inc(S["prep2"], 1)
            eng.wait_ge(S["wrs_ready"], 6)
            eng.wait_ge(S["ht_ev"], 4)
            for ti, t in enumerate("ABC"):
                lo, hi = NODE[t]
                n = hi - lo
                bank, at = ((4, 0), (5, 0), (5, B * n))[ti]
                for fh in range(2):
                    last = pe.matmul(P[:, bank, at:at + B * n], Wrsum[:, ti, fh, :], hT[:, fh, :, lo:hi], start=(fh == 0), stop=(fh == 1))
                last.then_inc(S["o_mm"], 1)
            eng.wait_ge(S["ld_wl"], 32)
            eng.wait_ge(S["mu_ready"], 9)
            for ti, t in enumerate("ABC"):
                todo = [(i, fh) for i in node_edges(t) for fh in range(2)]
                for n, (i, fh) in enumerate(todo):
                    last = pe.matmul(P[:, 6, B * ti:B * ti + B], Wls[:, i, fh, :], mu[:, "ABC".index(EDGES[i][0]), fh, :],
                                     start=(n == 0), stop=(n == len(todo) - 1))
                last.then_inc(S["c_mm"], 1)
            eng.wait_ge(S["ld_wf"], 64)
            eng.wait_ge(S["r_ready"], 1)
            for c in range(4):
                for b in range(2 * c, 2 * c + 2):
                    for h in range(2):
                        last = pe.matmul(P[64 * h:64 * h + 64, c, HW * (b % 2):HW * (b % 2) + HW], rT[:, HALF * h + b, :], Wfs[:, :],
                                         start=True, stop=True)
                last.then_inc(S["out_mm"], 1)
            eng.wait_ge(S["c_ev"], 3)
            eng.wait_ge(S["r_add"], 3)
            eng.wait_ge(S["b1c"], 1)
            eng.wait_ge(S["wz_lo"], 2)
            eng.wait_ge(S["bz"], 1)
            for c in range(4):
                eng.wait_ge(S["out_ev"], c + 1)
                pe.matmul(P[:, 4 + c, :], cW2bd[:, :], gn[:, 2 * c:2 * c + 2, :].rearrange("p b f -> p (b f)"), start=True, stop=True).then_inc(S["y_mm"], 1)
            eng.wait_ge(S["res_ready"], 4)
            eng.wait_ge(S["k_misc"], 13)
            eng.wait_ge(S["wbr"], 2)

            pe_cenA(eng, 0)
            pe_varA(eng, 0)
            pe_projz(eng, 0)
            pe_projg(eng, 0)
            pe_dtbc(eng, 0)
            eng.wait_ge(S["k_selu"], 5)

            def body(i, p, nxt, prev):
                q = 1 - p
                pe_ub(eng, i, p, 0)
                if nxt is not None:
                    pe_cenA(eng, nxt)
                pe_ub(eng, i, p, 1)
                if nxt is not None:
                    pe_varA(eng, nxt)
                if prev is not None:
                    pe_sum(eng, prev, 3)
                    pe_po(eng, prev)
                if nxt is not None:
                    pe_projz(eng, nxt)
                pe_ub(eng, i, p, 2)
                if prev is not None:
                    pe_cenF(eng, prev, q)
                if nxt is not None:
                    pe_projg(eng, nxt)
                if prev is not None:
                    pe_varF(eng, prev)
                pe_ub(eng, i, p, 3)
                if prev is not None:
                    pe_router(eng, prev)
                if nxt is not None:
                    pe_dtbc(eng, nxt)
                pe_sum(eng, i, 0)
                pe_ub(eng, i, p, 4)
                if prev is not None:
                    pe_wb(eng, prev)
                    pe_ffn(eng, prev, 0, 3)
                pe_ub(eng, i, p, 5)
                if prev is not None:
                    pe_ffn(eng, prev, 3, 6)
                pe_sum(eng, i, 1)
                pe_ub(eng, i, p, 6)
                if prev is not None:
                    pe_ffn(eng, prev, 6, 10)
                pe_ub(eng, i, p, 7)
                pe_sum(eng, i, 2)
                if prev is not None:
                    pe_ffn(eng, prev, 10, 18)

            body(0, 0, 1, None)
            eng.wait_ge(S["k_selw"], 1)
            eng.wait_ge(S["ld_dup"], 64)
            eng.wait_ge(S["ffn_l"], 1)
            body(1, 1, 2, 0)
            with eng.Fori(0, LOOPS) as it:
                for par in range(2):
                    i = it * 2 + (2 + par)
                    body(i, par, i + 1, i - 1)
            body(G - 2, 0, G - 1, G - 3)
            body(G - 1, 1, None, G - 2)
            pe_sum(eng, G - 1, 3)
            pe_po(eng, G - 1)
            pe_cenF(eng, G - 1, 1)
            pe_varF(eng, G - 1)
            pe_router(eng, G - 1)
            pe_wb(eng, G - 1)
            pe_ffn(eng, G - 1, 0, 18)


_INS = [('x', 'x'), ('L0_conv_W1', 'cW1'), ('L0_conv_b1', 'cb1'), ('L0_conv_Wl', 'Wl'), ('L0_conv_bl', 'bl'),
        ('L0_conv_Wr', 'Wr'), ('L0_conv_Wf', 'Wf'), ('L0_conv_bf', 'bf'), ('L0_conv_W2', 'cW2'), ('L0_conv_b2', 'cb2'),
        ('L1_attn_W_in', 'W_in'), ('L1_attn_b_in', 'b_in'), ('L1_attn_W_conv', 'W_conv'), ('L1_attn_b_conv', 'b_conv'),
        ('L1_attn_A_log', 'A_log'), ('L1_attn_W_bc', 'W_bc'), ('L1_attn_b_bc', 'b_bc'), ('L1_attn_W_dt', 'W_dt'),
        ('L1_attn_b_dt', 'b_dt'), ('L1_attn_W_out', 'W_out'), ('L1_attn_b_out', 'b_out'), ('L1_ffn_Wr', 'fWr'),
        ('L1_ffn_br', 'fbr'), ('L1_ffn_ln_g', 'ln_g'), ('L1_ffn_ln_b', 'ln_b'), ('L1_ffn_W1', 'W1'), ('L1_ffn_b1', 'b1'),
        ('L1_ffn_W2', 'W2'), ('L1_ffn_b2', 'b2')]


def kernel(**inputs):
    import numpy as _np
    import concourse.bacc as _bacc
    from concourse import mybir as _mybir
    from concourse.bass_utils import run_bass_kernel_spmd as _run

    nc = _bacc.Bacc("TRN2", target_bir_lowering=False, num_devices=1)
    arrays, args = {}, {}
    for name, short in _INS:
        a = _np.ascontiguousarray(inputs[name])
        arrays[f"in_{name}"] = a
        args[short] = nc.dram_tensor(f"in_{name}", a.shape, _mybir.dt.from_np(a.dtype), kind="ExternalInput").ap()
    args["out"] = nc.dram_tensor("out_0", (B, D, 16, 16), _mybir.dt.float32, kind="ExternalOutput").ap()
    build(nc, **args)
    r = _run(nc, [arrays], core_ids=[0])
    return r.results[0]["out_0"]
```

```python
import concourse.bass as bass
from concourse import mybir
from contextlib import ExitStack

B, D, HW = 16, 64, 256
HALF = B // 2
G = HALF
LOOPS = (G - 4) // 2
T = 2 * HW
HID, NODES, NE = 128, 64, 9
NODE = {"A": (0, 32), "B": (32, 48), "C": (48, 64)}
EDGES = [("A", "B"), ("B", "A"), ("A", "C"), ("C", "A"), ("B", "C"), ("C", "B"), ("A", "A"), ("B", "B"), ("C", "C")]
INNER, ST = 128, 16
BLK = INNER // ST
NBLK = INNER // BLK
SLOTS = NBLK // 2
EXP, FH = 8, 256
KC = FH // 128
NROWS = EXP * KC + NE + 2 + 1 + 1 + 1 + EXP + 1 + EXP + EXP
EPS = 1e-5

R, _at = {}, 0
for _name, _n in (("b1", EXP * KC), ("bl", NE), ("b_in", 2), ("b_conv", 1), ("b_dt", 1),
                  ("b_out", 1), ("b2", EXP), ("cb2", 1), ("ln_g", EXP), ("ln_b", EXP)):
    R[_name] = _at
    _at += _n
assert _at == NROWS

SEMS = """ld_x ld_rows ld_wgn ld_wr ld_wl ld_wf ld_wssm ld_ffn ld_dup
gn_stat gn_agg gn_avg gn_dev gn_dsq gn_var gn_ln gn_rs gn_shift gn_out
k_zero k_ident k_sel k_misc k_dve k_selu k_selw k_mask k_col0 bbx bbcol
ht_mm ht_ev mu_ready wrs_ready o_mm c_mm bls_ready c_ev r_add r_ready out_mm out_ev y_mm res_ready
prep1 cols_ev wmt_ev a_exp a_neg a_selx prep2 wz_hi wz_lo bz b1c wbr ffn_g ffn_h ffn_l selx
cen1 sq1 var1 ln1 rs1 xn1 xh1 xl1 z_mm g_mm xc sg
dtz_mm b_mm c_rep_mm sp_abs sp_exp sp_ln sp_relu bs cs dt u uh ul dt_out dt_in0 dt_in1 dt_in2 dt_in3 aexp
ub bm scan cm ysum
yg po t1 cen2 sq2 var2 ln2 rs2 r2 vq lnq rq tn xn2 xh2 xl2
lg lgb m1 dd ex s1 ms1 o1 e2 m2 s2 s2r ms2 o2 den rden num wt vhi vlo wtr wtc wb_mm wb
f1 gl f2 me acc out_sem""".split()


def rep(ap, axis, n):
    v = ap.unsqueeze(axis)
    return v.broadcast_to([*v.shape[:axis], n, *v.shape[axis + 1:]])


def build(nc, x, cW1, cb1, Wl, bl, Wr, Wf, bf, cW2, cb2, W_in, b_in, W_conv, b_conv, A_log, W_bc, b_bc,
          W_dt, b_dt, W_out, b_out, fWr, fbr, ln_g, ln_b, W1, b1, W2, b2, out):
    fp32, f32r = mybir.dt.float32, mybir.dt.float32r
    ALU = mybir.AluOpType
    ACT = mybir.ActivationFunctionType
    AX = mybir.AxisListType.X

    dt_dram = nc.dram_tensor("dt_scratch", (2, INNER, T), fp32, kind="Internal").ap()

    ctx = ExitStack()
    with ctx:
        def sb(name, shape, dt=fp32):
            return ctx.enter_context(nc.sbuf_tensor(name, shape, dt))

        S = {n: ctx.enter_context(nc.semaphore(n)) for n in SEMS}

        def since(eng, name, count):
            if isinstance(count, int) and count <= 0:
                return
            eng.wait_ge(S[name], count)

        res = sb("res", [128, HALF * HW])
        stats = sb("stats", [128, HALF, 6])
        mv = sb("mv", [128, HALF, 2])
        gdev = sb("gdev", [128, 2, HALF])
        gvar = sb("gvar", [128, HALF])
        gmean = sb("gmean", [128, HALF])
        grs = sb("grs", [128, HALF])
        cW2bd = sb("cW2bd", [128, 128])
        mu = sb("mu", [128, 3, 2, B])
        blsum = sb("blsum", [128, 3])
        cT = sb("cT", [128, 3, B])
        ident = sb("ident", [128, 128])
        cen_m = sb("cen_m", [128, 128])
        avg_m = sb("avg_m", [128, 128])
        pair_m = sb("pair_m", [128, 128])
        gsel = sb("gsel", [128, NBLK])
        mask8 = sb("mask8", [128, BLK])
        selU = sb("selU", [128, NBLK, 128], f32r)
        selS = sb("selS", [128, 4, 32])
        selW = sb("selW", [32, EXP, 128], f32r)
        rank = sb("rank", [128, 4, EXP])
        epst = sb("epst", [128, 1])
        onet = sb("onet", [128, 1])
        cols = sb("cols", [128, NROWS])
        bbc = sb("bbc", [2, ST])
        bbx = sb("bbx", [2, ST, BLK])
        bbcol = sb("bbcol", [128, 2])
        Wins = sb("Wins", [128, 2 * INNER])
        WmT2 = sb("WmT2", [128, 2, 64])
        WzH = sb("WzH", [128, 128], f32r)
        WzL = sb("WzL", [128, 128], f32r)
        WgH = sb("WgH", [128, 128], f32r)
        WgL = sb("WgL", [128, 128], f32r)
        bz = sb("bz", [128, 1])
        Als = sb("Als", [128, ST])
        Aneg = sb("Aneg", [128, NBLK])
        Aexp = sb("Aexp", [128, NBLK])
        Wbcs = sb("Wbcs", [128, 2 * ST])
        Wrep = sb("Wrep", [128, 2, ST, BLK])
        Wdts = sb("Wdts", [128, INNER])
        Wouts = sb("Wouts", [128, D])
        Wrt = sb("Wrt", [128, 2, EXP])
        brs = sb("brs", [128, EXP])
        W1H = sb("W1H", [128, EXP, FH], f32r)
        W1L = sb("W1L", [128, EXP, FH], f32r)
        W2s = sb("W2s", [128, EXP, KC, D])
        b1c = sb("b1c", [128, EXP * KC])
        sq = sb("sq", [128, HW])
        rs = sb("rs", [128, HW])
        xnt = sb("xnt", [64, T])
        Xs = sb("Xs", [128, T], f32r)
        xc = sb("xc", [128, T])
        sg = sb("sg", [128, 2, T])
        sp = sb("sp", [128, T])
        rl = sb("rl", [128, T])
        u = rl
        dts = sb("dts", [128, 2, T])
        uh = sb("uh", [128, 2, T], f32r)
        ul = sb("ul", [128, 2, T], f32r)
        Bs = sb("Bs", [128, 2, T])
        Cs = sb("Cs", [128, 2, T])
        av = sb("av", [128, 2, NBLK, T])
        hs = sb("hs", [128, 4, 2, T])
        ygs = sb("ygs", [128, T])
        t1 = sb("t1s", [128, 2, HW])
        sq2 = sb("sq2s", [128, HW])
        rs2 = sb("rs2s", [128, HW])
        r2s = sb("r2s", [128, HW])
        vqs = sb("vqs", [128, HW])
        rqs = sb("rqs", [128, HW])
        tns = sb("tns", [128, HW])
        xnt2 = sb("xnt2", [64, T])
        X2 = sb("X2", [128, T], f32r)
        rt = sb("rt", [128, 12, 4, EXP])
        rv = sb("rv", [128, 8, 4])
        vv = sb("vv", [128, 2, 2, 2, EXP])
        wT = sb("wT", [32, HW], f32r)
        wbs = sb("wbs", [128, EXP, HW])
        hb = sb("hb", [128, 4, T])
        mes = sb("mes", [128, 4, HW])
        acc = sb("accs", [128, 2, HW])

        def within(buf, at, shape):
            n = 1
            for d in shape:
                n *= d
            names = "abcd"[:len(shape)]
            view = buf[:, at:at + n]
            if len(shape) > 1:
                view = view.rearrange("p (" + " ".join(names) + ") -> p " + " ".join(names), **dict(zip(names[1:], shape[1:])))
            return view, at + n

        gn = hs[:, :, :, :].rearrange("p a b t -> p (a b t)")[:, 0:HALF * HW].rearrange("p (b f) -> p b f", b=HALF)
        buf0 = av[:, 0].rearrange("p m t -> p (m t)")
        buf1 = av[:, 1].rearrange("p m t -> p (m t)")
        Wrs_raw, at = within(buf0, 0, [NE, 2, HID])
        Wls, at = within(buf0, at, [NE, 2, HID])
        hT, at = within(buf0, at, [2, B, NODES])
        W1g, at = within(buf1, 0, [EXP, FH])
        W1r, at = within(buf1, at, [EXP, FH])
        Wrsum, at = within(buf1, at, [3, 2, HID])
        rT, at = within(buf1, at, [B, NODES])
        selWf, at = within(buf1[0:32], at, [EXP, 2, 64])

        Wfs, at = within(buf1, at, [HW])
        bfs, at = within(buf1, at, [HW])
        Wcv, at = within(buf1, at, [INNER])
        Asel, at = within(buf1, at, [ST, BLK])
        cb1s, at = within(buf1, at, [NODES])
        cW1s, at = within(buf1, at, [NODES])
        rows, at = within(buf1[0:NROWS], at, [128])
        assert at <= NBLK * T

        P = ctx.enter_context(nc.psum_tensor("P", [128, 8, 512], fp32))
        UB = 3
        XD, XA, XB, XC, YS = 3, 4, 5, 6, 7

        v = nc.vector
        a_ = nc.scalar
        pe = nc.tensor
        gp = nc.gpsimd

        def node_edges(t):
            return [i for i, (_, d) in enumerate(EDGES) if d == t]

        def block_of(m):
            return 4 * (m % 4) + m // 4

        xv = x.rearrange("(h b) d l w -> h d b (l w)", h=2)
        ov = out.rearrange("(h b) d l w -> h d b (l w)", h=2)

        block = ctx.enter_context(nc.Block())

        def sp_dt(sp_, g, p):
            since(sp_, "dt", g + 1)
            sp_.dma_start(dt_dram[p], dts[:, p, :]).then_inc(S["dt_out"], 16)
            sp_.wait_ge(S["dt_out"], 16 * (g + 1))
            since(sp_, "scan", NBLK * (g - 1))
            if isinstance(g, int) and g < 2:
                sp_.wait_ge(S["k_col0"], g + 1)
            src = dt_dram[p].rearrange("(q k e) (h f) -> k q e h f", k=4, e=BLK, h=2)
            for k in range(4):
                for q in range(4):
                    sp_.dma_start(av[:, p, 4 * k + q, :].rearrange("p (h f) -> p h f", h=2)[:, :, 1:HW],
                                  rep(src[k, q, :, :, 1:HW], 0, ST)).then_inc(S[f"dt_in{k}"], 16)

        def sp_out(sp_, g, p):
            sp_.wait_ge(S["acc"], EXP * (g + 1))
            for h in range(2):
                sp_.dma_start(ov[h, :, bass.ds(g, 1), :], acc[64 * h:64 * h + 64, p:p + 1, :]).then_inc(S["out_sem"], 16)

        @block.sync
        def _(sp_):
            for h in range(2):
                sp_.dma_start(res[64 * h:64 * h + 64, :].rearrange("p (b f) -> p b f", b=HALF), xv[h]).then_inc(S["ld_x"], 16)
            for h in range(2):
                sp_.dma_start(cW1s[64 * h:64 * h + 64, :], cW1).then_inc(S["ld_wgn"], 16)
            sp_.dma_start(cb1s[:, :], rep(cb1, 0, 128)).then_inc(S["ld_wgn"], 16)
            for fh in range(2):
                sp_.dma_start(Wrs_raw[:, :, fh, :], Wr[:, 128 * fh:128 * fh + 128, :].rearrange("i f n -> f i n")).then_inc(S["ld_wr"], 16)
            for fh in range(2):
                sp_.dma_start(Wls[:, :, fh, :], Wl[:, 128 * fh:128 * fh + 128, :].rearrange("i f n -> f i n")).then_inc(S["ld_wl"], 16)
            sp_.dma_start(Wfs[:, :], Wf).then_inc(S["ld_wf"], 16)
            sp_.dma_start(bfs[:, :], rep(bf, 0, 128)).then_inc(S["ld_wf"], 16)
            def row(name, ap, off=0):
                sp_.dma_start(rows[R[name] + off:R[name] + off + ap.shape[0], 0:ap.shape[-1]], ap).then_inc(S["ld_rows"], 16)
            row("b1", b1.rearrange("e (k f) -> (e k) f", f=128))
            row("bl", bl)
            row("b_in", b_in.rearrange("(a f) -> a f", f=128))
            row("b_conv", b_conv.unsqueeze(0))
            row("b_dt", b_dt.unsqueeze(0))
            sp_.dma_start(bbc[:, :], b_bc.rearrange("(a s) -> a s", a=2)).then_inc(S["ld_rows"], 16)
            for h in range(2):
                for name, ap in (("b_out", b_out.unsqueeze(0)), ("b2", b2), ("cb2", cb2.unsqueeze(0)), ("ln_g", ln_g), ("ln_b", ln_b)):
                    n = ap.shape[0]
                    sp_.dma_start(rows[R[name]:R[name] + n, 64 * h:64 * h + 64], ap).then_inc(S["ld_rows"], 16)
            sp_.wait_ge(S["k_zero"], 8)
            for h in range(2):
                sp_.dma_start(cW2bd[64 * h:64 * h + 64, 64 * h:64 * h + 64], cW2).then_inc(S["ld_wf"], 16)
            for h in range(2):
                sp_.dma_start(W1r[64 * h:64 * h + 64, :, :], W1.rearrange("e d n -> d e n")).then_inc(S["ld_ffn"], 16)
            sp_.dma_start(W2s[:, :, :, :], W2.rearrange("e (k p) d -> p e k d", p=128)).then_inc(S["ld_dup"], 16)
            for h in range(2):
                sp_.dma_start(Wrt[64 * h:64 * h + 64, h, :], fWr).then_inc(S["ld_dup"], 16)
            sp_.dma_start(brs[:, :], rep(fbr, 0, 128)).then_inc(S["ld_dup"], 16)
            for g in range(3):
                sp_dt(sp_, g, g % 2)
            sp_out(sp_, 0, 0)
            with sp_.Fori(0, LOOPS) as it:
                for par in range(2):
                    i = it * 2 + (2 + par)
                    sp_dt(sp_, i + 1, 1 - par)
                    sp_out(sp_, i - 1, 1 - par)
            sp_dt(sp_, G - 1, 1)
            sp_out(sp_, G - 3, 1)
            sp_out(sp_, G - 2, 0)
            sp_out(sp_, G - 1, 1)
            sp_.wait_ge(S["out_sem"], 32 * G)

        def pool_slot(eng, g, p, n):
            eng.wait_ge(S["scan"], NBLK * g + 2 * n + 2)
            if n == 0:
                eng.wait_ge(S["cs"], g + 1)
            gp.tensor_tensor(hs[:, n % 4, :, :], hs[:, n % 4, :, :],
                             rep(Cs[:, p, :], 1, 2), ALU.mult).then_inc(S["cm"], 1)

        def pool_acc(eng, g, p, e):
            eng.wait_ge(S["me"], EXP * g + e + 1)
            if e == 0:
                since(eng, "out_sem", 32 * g)
                prev = t1[:, p, :]
            else:
                eng.wait_ge(S["acc"], EXP * g + e)
                prev = acc[:, p, :]
            gp.tensor_tensor(acc[:, p, :], prev, mes[:, e % 4, :], ALU.add).then_inc(S["acc"], 1)

        @block.gpsimd
        def _(eng):
            gp.memset(ident[:, :], 0.0).then_inc(S["k_zero"], 1)
            gp.memset(avg_m[:, :], 0.0).then_inc(S["k_zero"], 1)
            gp.memset(cW2bd[:, :], 0.0).then_inc(S["k_zero"], 1)
            gp.memset(Wrt[:, :, :], 0.0).then_inc(S["k_zero"], 1)
            gp.memset(pair_m[:, :], 0.5).then_inc(S["k_zero"], 1)
            gp.memset(gsel[:, :], 1.0).then_inc(S["k_zero"], 1)
            gp.memset(selWf[:, :, :, :], 0.0).then_inc(S["k_zero"], 1)
            gp.memset(selS[:, :, :], 0.0).then_inc(S["k_zero"], 1)
            eng.wait_ge(S["k_zero"], 8)
            for h in range(2):
                gp.memset(avg_m[64 * h:64 * h + 64, 64 * h:64 * h + 64], 1.0 / D).then_inc(S["k_misc"], 1)
            eng.wait_ge(S["k_misc"], 2)
            gp.affine_select(out=ident[:, :], in_=ident[:, :], compare_op=ALU.not_equal, fill=1.0, base=0,
                             pattern=[[-1, 128]], channel_multiplier=1).then_inc(S["k_ident"], 1)
            pv = pair_m[:, :].rearrange("p (a b) -> p a b", b=2)
            gp.affine_select(out=pv, in_=pv, compare_op=ALU.is_ge, fill=0.0, base=0,
                             pattern=[[-2, 64], [0, 2]], channel_multiplier=1).then_inc(S["k_sel"], 1)
            gp.affine_select(out=gsel[:, :], in_=gsel[:, :], compare_op=ALU.is_ge, fill=0.0, base=0,
                             pattern=[[-BLK, NBLK]], channel_multiplier=1).then_inc(S["k_sel"], 1)
            gp.affine_select(out=selWf[:, :, :, :], in_=selWf[:, :, :, :], compare_op=ALU.not_equal, fill=1.0, base=0,
                             pattern=[[-1, EXP], [-2 * EXP, 2], [0, 64]], channel_multiplier=1).then_inc(S["k_sel"], 1)
            eng.wait_ge(S["k_sel"], 3)
            gp.affine_select(out=pv, in_=pv, compare_op=ALU.is_ge, fill=0.0, base=1,
                             pattern=[[2, 64], [0, 2]], channel_multiplier=-1).then_inc(S["k_sel"], 1)
            gp.affine_select(out=gsel[:, :], in_=gsel[:, :], compare_op=ALU.is_ge, fill=0.0, base=BLK - 1,
                             pattern=[[BLK, NBLK]], channel_multiplier=-1).then_inc(S["k_sel"], 1)
            gp.affine_select(out=selWf[:, :, :, :], in_=selWf[:, :, :, :], compare_op=ALU.not_equal, fill=1.0, base=-EXP,
                             pattern=[[-1, EXP], [-2 * EXP, 2], [0, 64]], channel_multiplier=1).then_inc(S["k_sel"], 1)
            gp.memset(epst[:, :], EPS).then_inc(S["k_misc"], 1)
            gp.memset(onet[:, :], 1.0).then_inc(S["k_misc"], 1)
            for e in range(EXP):
                gp.memset(rank[:, :, e:e + 1], float(EXP - e)).then_inc(S["k_misc"], 1)
            eng.wait_ge(S["k_ident"], 1)
            gp.tensor_tensor(cen_m[:, :], ident[:, :], avg_m[:, :], ALU.subtract).then_inc(S["k_misc"], 1)
            eng.wait_ge(S["ld_wr"], 32)
            for ti, t in enumerate("ABC"):
                e0, e1, e2 = node_edges(t)
                gp.tensor_tensor(Wrsum[:, ti], Wrs_raw[:, e0], Wrs_raw[:, e1], ALU.add).then_inc(S["wrs_ready"], 1)
            eng.wait_ge(S["wrs_ready"], 3)
            for ti, t in enumerate("ABC"):
                gp.tensor_tensor(Wrsum[:, ti], Wrsum[:, ti], Wrs_raw[:, node_edges(t)[2]], ALU.add).then_inc(S["wrs_ready"], 1)
            eng.wait_ge(S["ld_ffn"], 32)
            eng.wait_ge(S["cols_ev"], 1)
            gp.tensor_tensor(W1g[:, :, :], W1r[:, :, :], rep(cols[:, R["ln_g"]:R["ln_g"] + EXP], 2, FH),
                             ALU.mult).then_inc(S["ffn_g"], 1)
            eng.wait_ge(S["ffn_h"], 1)
            gp.tensor_tensor(W1L[:, :, :], W1g[:, :, :], W1H[:, :, :], ALU.subtract).then_inc(S["ffn_l"], 1)

            eng.wait_ge(S["res_ready"], 4)
            gp.memset(av[:, 0, :, :].rearrange("p m (h f) -> p m h f", h=2)[:, :, :, 0:1], 0.0).then_inc(S["k_col0"], 1)
            eng.wait_ge(S["ffn_l"], 1)
            eng.wait_ge(S["prep2"], 3)
            eng.wait_ge(S["k_selw"], 1)
            gp.memset(av[:, 1, :, :].rearrange("p m (h f) -> p m h f", h=2)[:, :, :, 0:1], 0.0).then_inc(S["k_col0"], 1)

            def body(i, p, nxt, prev):
                for n in range(1, SLOTS):
                    pool_slot(eng, i, p, n)
                    if prev is not None and n >= 6:
                        for e in range(4 * (n - 6), 4 * (n - 6) + 4):
                            pool_acc(eng, prev, 1 - p, e)
                if nxt is not None:
                    pool_slot(eng, nxt, 1 - p, 0)

            pool_slot(eng, 0, 0, 0)
            body(0, 0, 1, None)
            body(1, 1, 2, 0)
            with eng.Fori(0, LOOPS) as it:
                for par in range(2):
                    i = it * 2 + (2 + par)
                    body(i, par, i + 1, i - 1)
            body(G - 2, 0, G - 1, G - 3)
            body(G - 1, 1, None, G - 2)
            for e in range(EXP):
                pool_acc(eng, G - 1, 1, e)

        def act_lnA1(eng, g):
            eng.wait_ge(S["cen1"], g + 1)
            since(eng, "var1", g)
            a_.activation(sq[:, :], P[:, XA, 0:HW], ACT.Square).then_inc(S["sq1"], 1)

        def act_lnA2(eng, g):
            eng.wait_ge(S["var1"], g + 1)
            since(eng, "xn1", 2 * g)
            a_.activation(rs[:, :], P[:, XA, HW:T], ACT.Ln, bias=epst[:, 0:1]).then_inc(S["ln1"], 1)
            eng.wait_ge(S["ln1"], g + 1)
            a_.activation(rs[:, :], rs[:, :], ACT.Exp, scale=-0.5).then_inc(S["rs1"], 1)

        def act_siluz(eng, g):
            eng.wait_ge(S["z_mm"], g + 1)
            since(eng, "c_rep_mm", g)
            since(eng, "u", g)
            a_.activation(xc[:, :], P[:, XA, :], ACT.Silu, bias=bz[:, 0:1]).then_inc(S["xc"], 1)

        def act_silug(eng, g, p):
            eng.wait_ge(S["g_mm"], g + 1)
            since(eng, "yg", g - 1)
            a_.activation(sg[:, p, :], P[:, XC, :], ACT.Silu, bias=cols[:, R["b_in"] + 1:R["b_in"] + 2]).then_inc(S["sg"], 1)

        def act_softplus1(eng, g):
            bdt = cols[:, R["b_dt"]:R["b_dt"] + 1]
            eng.wait_ge(S["dtz_mm"], g + 1)
            since(eng, "ul", g)
            a_.activation(sp[:, :], P[:, XA, :], ACT.Abs, bias=bdt).then_inc(S["sp_abs"], 1)
            a_.activation(rl[:, :], P[:, XA, :], ACT.Relu, bias=bdt).then_inc(S["sp_relu"], 1)

        def act_softplus2(eng, g, p):
            eng.wait_ge(S["sp_abs"], g + 1)
            a_.activation(sp[:, :], sp[:, :], ACT.Exp, scale=-1.0).then_inc(S["sp_exp"], 1)
            eng.wait_ge(S["b_mm"], g + 1)
            since(eng, "bm", NBLK * (g - 1))
            a_.activation(Bs[:, p, :], P[:, XC, :], ACT.Identity, bias=bbcol[:, 0:1]).then_inc(S["bs"], 1)
            eng.wait_ge(S["sp_exp"], g + 1)
            a_.activation(sp[:, :], sp[:, :], ACT.Ln, bias=onet[:, 0:1]).then_inc(S["sp_ln"], 1)
            eng.wait_ge(S["c_rep_mm"], g + 1)
            since(eng, "cm", SLOTS * (g - 1))
            a_.activation(Cs[:, p, :], P[:, XC, :], ACT.Identity, bias=bbcol[:, 1:2]).then_inc(S["cs"], 1)

        def act_decay(eng, g, p, lo, hi):
            for m in range(lo, hi):
                if m % 4 == 0:
                    eng.wait_ge(S[f"dt_in{m // 4}"], 64 * (g + 1))
                j = block_of(m)
                steps = av[:, p, m, :].rearrange("p (h f) -> p h f", h=2)[:, :, 1:HW]
                a_.activation(steps, steps, ACT.Exp, scale=Aneg[:, j:j + 1]).then_inc(S["aexp"], 1)

        def act_lnF1(eng, g):
            eng.wait_ge(S["cen2"], g + 1)
            since(eng, "var2", g)
            a_.activation(sq2[:, :], P[:, XB, 0:HW], ACT.Square).then_inc(S["sq2"], 1)

        def act_lnF2(eng, g):
            eng.wait_ge(S["var2"], g + 1)
            since(eng, "tn", g)
            since(eng, "r2", g)
            a_.activation(rs2[:, :], P[:, XB, HW:T], ACT.Ln, bias=epst[:, 0:1]).then_inc(S["ln2"], 1)
            eng.wait_ge(S["ln2"], g + 1)
            a_.activation(rs2[:, :], rs2[:, :], ACT.Exp, scale=-0.5).then_inc(S["rs2"], 1)
            eng.wait_ge(S["rs2"], g + 1)
            since(eng, "vq", g)
            a_.activation(r2s[:, :], rs2[:, :], ACT.Square).then_inc(S["r2"], 1)

        def act_lnF3(eng, g):
            eng.wait_ge(S["vq"], g + 1)
            since(eng, "xn2", 2 * g)
            a_.activation(rqs[:, :], vqs[:, :], ACT.Ln, bias=epst[:, 0:1]).then_inc(S["lnq"], 1)
            eng.wait_ge(S["lnq"], g + 1)
            a_.activation(rqs[:, :], rqs[:, :], ACT.Exp, scale=-0.5).then_inc(S["rq"], 1)

        def act_router(eng, g):
            eng.wait_ge(S["dd"], g + 1)
            a_.activation(rt[:, 2], rt[:, 1], ACT.Exp).then_inc(S["ex"], 1)

        def act_wb(eng, g):
            eng.wait_ge(S["wtr"], 2 * (g + 1))
            since(eng, "wb_mm", EXP * g)
            a_.activation(wT[:, :], P[0:32, XB, 0:HW], ACT.Copy).then_inc(S["wtc"], 1)
            for r in range(EXP // 2):
                eng.wait_ge(S["wb_mm"], EXP * g + 2 * r + 2)
                if r == 0:
                    since(eng, "me", EXP * g)
                a_.activation(wbs[:, 2 * r:2 * r + 2, :].rearrange("p e f -> p (e f)"), P[:, (XB, XD)[r % 2], :], ACT.Copy).then_inc(S["wb"], 1)

        def act_gelu(eng, g):
            for r in range(EXP * KC):
                eng.wait_ge(S["f1"], EXP * KC * g + r + 1)
                since(eng, "f2", EXP * KC * g + max(r - 3, 0))
                a_.activation(hb[:, r % 4, :], P[:, (XA, XB)[r % 2], :], ACT.Gelu, bias=b1c[:, r:r + 1]).then_inc(S["gl"], 1)

        @block.scalar
        def _(eng):
            for ap, src, sem in ((Wcv[:, :], W_conv, "ld_wssm"), (Als[:, :], A_log, "ld_wssm"), (Wins[0:64, :], W_in, "ld_wssm"),
                                 (Wins[64:128, :], W_in, "ld_wssm"), (Wbcs[:, :], W_bc, "ld_wssm"), (Wdts[:, :], W_dt, "ld_wssm"),
                                 (Wouts[:, :], W_out, "ld_wssm")):
                eng.dma_start(ap, src).then_inc(S[sem], 16)
            a_.preload_act_table_set("natural_log_exp_and_others")
            eng.wait_ge(S["k_misc"], 3)
            eng.wait_ge(S["gn_var"], 1)
            a_.activation(gvar[:, :], P[:, 0, 2 * HALF:3 * HALF], ACT.Ln, bias=epst[:, 0:1]).then_inc(S["gn_ln"], 1)
            eng.wait_ge(S["gn_ln"], 1)
            a_.activation(grs[:, :], gvar[:, :], ACT.Exp, scale=-0.5).then_inc(S["gn_rs"], 1)
            eng.wait_ge(S["prep1"], 4)
            eng.wait_ge(S["wmt_ev"], 2)
            a_.activation(Aexp[:, :], P[:, 7, 192:192 + NBLK], ACT.Exp).then_inc(S["a_exp"], 1)
            eng.wait_ge(S["ffn_g"], 1)
            a_.activation(W1H[:, :, :], W1g[:, :, :], ACT.Copy).then_inc(S["ffn_h"], 1)
            eng.wait_ge(S["r_add"], 3)
            a_.activation(rT[:, :, :], rT[:, :, :], ACT.Relu, scale=1.0 / 3.0).then_inc(S["r_ready"], 1)

            def a_stage(g, p):
                act_lnA1(eng, g)
                act_lnA2(eng, g)
                a_.preload_act_table_set("silu_and_others")
                act_siluz(eng, g)
                act_silug(eng, g, p)
                a_.preload_act_table_set("natural_log_exp_and_others")
                act_softplus1(eng, g)
                act_softplus2(eng, g, p)

            def body(i, p, nxt, prev):
                q = 1 - p
                if nxt is not None:
                    act_lnA1(eng, nxt)
                act_decay(eng, i, p, 2, 3)
                if nxt is not None:
                    act_lnA2(eng, nxt)
                act_decay(eng, i, p, 3, 5)
                if prev is not None:
                    act_lnF1(eng, prev)
                act_decay(eng, i, p, 5, 6)
                if prev is not None:
                    act_lnF2(eng, prev)
                act_decay(eng, i, p, 6, 7)
                if prev is not None:
                    act_lnF3(eng, prev)
                act_decay(eng, i, p, 7, 9)
                if prev is not None:
                    act_router(eng, prev)
                if nxt is not None:
                    a_.preload_act_table_set("silu_and_others")
                    act_siluz(eng, nxt)
                    act_silug(eng, nxt, q)
                    a_.preload_act_table_set("natural_log_exp_and_others")
                act_decay(eng, i, p, 9, 10)
                if nxt is not None:
                    act_softplus1(eng, nxt)
                    act_softplus2(eng, nxt, q)
                if prev is not None:
                    act_wb(eng, prev)
                act_decay(eng, i, p, 10, NBLK)
                if prev is not None:
                    a_.preload_act_table_set("gelu_and_others")
                    act_gelu(eng, prev)
                    a_.preload_act_table_set("natural_log_exp_and_others")
                if nxt is not None:
                    act_decay(eng, nxt, q, 0, 2)

            a_stage(0, 0)
            act_decay(eng, 0, 0, 0, 2)
            body(0, 0, 1, None)
            body(1, 1, 2, 0)
            with eng.Fori(0, LOOPS) as it:
                for par in range(2):
                    i = it * 2 + (2 + par)
                    body(i, par, i + 1, i - 1)
            body(G - 2, 0, G - 1, G - 3)
            body(G - 1, 1, None, G - 2)
            act_lnF1(eng, G - 1)
            act_lnF2(eng, G - 1)
            act_lnF3(eng, G - 1)
            act_router(eng, G - 1)
            act_wb(eng, G - 1)
            act_gelu(eng, G - 1)

        def dve_bm(eng, g, p, b):
            ub = P[:, b % UB, :]
            eng.wait_ge(S["ub"], NBLK * g + b + 1)
            if b == 0:
                eng.wait_ge(S["bs"], g + 1)
            v.tensor_tensor(ub, ub, Bs[:, p, :], ALU.mult).then_inc(S["bm"], 1)

        def dve_scan(eng, g, p, b):
            n = b // 2
            eng.wait_ge(S["bm"], NBLK * g + b + 1)
            eng.wait_ge(S["aexp"], NBLK * g + b + 1)
            if b % 2 == 0:
                since(eng, "ysum", 4 * g + n // 2 - 1)
            v.tensor_tensor_scan(hs[:, n % 4, b % 2, :], av[:, p, b, :], P[:, b % UB, :],
                                 0.0, ALU.mult, ALU.add).then_inc(S["scan"], 1)

        def dve_step(eng, g, p, b):
            if b + 1 < NBLK:
                dve_bm(eng, g, p, b + 1)
            dve_scan(eng, g, p, b)

        def dve_xn(eng, g):
            eng.wait_ge(S["rs1"], g + 1)
            since(eng, "xl1", g)
            for h in range(2):
                q = slice(64 * h, 64 * h + 64)
                v.tensor_tensor(xnt[:, HW * h:HW * h + HW], P[q, XA, 0:HW], rs[q, :], ALU.mult).then_inc(S["xn1"], 1)
            eng.wait_ge(S["xn1"], 2 * (g + 1))
            since(eng, "g_mm", g)
            v.tensor_copy(Xs[0:64, :], xnt[:, :]).then_inc(S["xh1"], 1)
            eng.wait_ge(S["xh1"], g + 1)
            v.tensor_tensor(Xs[64:128, :], xnt[:, :], Xs[0:64, :], ALU.subtract).then_inc(S["xl1"], 1)

        def dve_u(eng, g, p):
            eng.wait_ge(S["sp_ln"], g + 1)
            eng.wait_ge(S["sp_relu"], g + 1)
            since(eng, "dt_out", 16 * (g - 1))
            v.tensor_tensor(dts[:, p, :], rl[:, :], sp[:, :], ALU.add).then_inc(S["dt"], 1)
            eng.wait_ge(S["dt"], g + 1)
            since(eng, "ul", g)
            v.tensor_tensor(u[:, :], dts[:, p, :], xc[:, :], ALU.mult).then_inc(S["u"], 1)
            eng.wait_ge(S["u"], g + 1)
            since(eng, "ub", NBLK * (g - 1))
            v.tensor_copy(uh[:, p, :], u[:, :]).then_inc(S["uh"], 1)
            eng.wait_ge(S["uh"], g + 1)
            v.tensor_tensor(ul[:, p, :], u[:, :], uh[:, p, :], ALU.subtract).then_inc(S["ul"], 1)

        def dve_gate(eng, g, p):
            eng.wait_ge(S["ysum"], 4 * (g + 1))
            since(eng, "po", g)
            v.tensor_tensor(ygs[:, :], P[:, YS, :], sg[:, p, :], ALU.mult).then_inc(S["yg"], 1)

        def dve_t1(eng, g, p):
            eng.wait_ge(S["po"], g + 1)
            v.scalar_tensor_tensor(out=t1[:, p, :], in0=P[:, XC, 0:HW], scalar=cols[:, R["b_out"]:R["b_out"] + 1],
                                   in1=res[:, bass.ds(g * HW, HW)], op0=ALU.add, op1=ALU.add).then_inc(S["t1"], 1)

        def dve_lnF(eng, g):
            eng.wait_ge(S["rs2"], g + 1)
            since(eng, "lg", g)
            since(eng, "xn2", 2 * g)
            v.tensor_tensor(tns[:, :], P[:, XB, 0:HW], rs2[:, :], ALU.mult).then_inc(S["tn"], 1)
            eng.wait_ge(S["r2"], g + 1)
            since(eng, "lnq", g)
            v.tensor_tensor(vqs[:, :], P[:, XB, HW:T], r2s[:, :], ALU.mult).then_inc(S["vq"], 1)

        def dve_xn2(eng, g):
            eng.wait_ge(S["rq"], g + 1)
            eng.wait_ge(S["tn"], g + 1)
            since(eng, "xl2", g)
            for h in range(2):
                q = slice(64 * h, 64 * h + 64)
                v.tensor_tensor(xnt2[:, HW * h:HW * h + HW], tns[q, :], rqs[q, :], ALU.mult).then_inc(S["xn2"], 1)
            eng.wait_ge(S["xn2"], 2 * (g + 1))
            since(eng, "f1", EXP * KC * g)
            v.tensor_copy(X2[0:64, :], xnt2[:, :]).then_inc(S["xh2"], 1)
            eng.wait_ge(S["xh2"], g + 1)
            v.tensor_tensor(X2[64:128, :], xnt2[:, :], X2[0:64, :], ALU.subtract).then_inc(S["xl2"], 1)

        def dve_router1(eng, g):
            eng.wait_ge(S["lg"], 2 * (g + 1))
            since(eng, "dd", g)
            v.tensor_tensor(rt[:, 0], P[:, XB, 0:4 * EXP].rearrange("p (c e) -> p c e", e=EXP),
                            rep(brs[:, :], 1, 4), ALU.add).then_inc(S["lgb"], 1)
            eng.wait_ge(S["lgb"], g + 1)
            v.tensor_reduce(rv[:, 0], rt[:, 0], AX, ALU.max).then_inc(S["m1"], 1)
            eng.wait_ge(S["m1"], g + 1)
            since(eng, "ex", g)
            v.tensor_tensor(rt[:, 1], rt[:, 0], rep(rv[:, 0], 2, EXP), ALU.subtract).then_inc(S["dd"], 1)

        def dve_router2(eng, g):
            bc = lambda k: rep(rv[:, k], 2, EXP)
            eng.wait_ge(S["ex"], g + 1)
            v.scalar_tensor_tensor(out=rt[:, 3], in0=rt[:, 2], scalar=1.0, in1=rank[:, :, :], op0=ALU.is_ge, op1=ALU.mult).then_inc(S["s1"], 1)
            eng.wait_ge(S["s1"], g + 1)
            v.tensor_reduce(rv[:, 1], rt[:, 3], AX, ALU.max).then_inc(S["ms1"], 1)
            eng.wait_ge(S["ms1"], g + 1)
            v.tensor_tensor(rt[:, 4], rt[:, 3], bc(1), ALU.is_equal).then_inc(S["o1"], 1)
            eng.wait_ge(S["o1"], g + 1)
            v.scalar_tensor_tensor(out=rt[:, 5], in0=rt[:, 4], scalar=-2.0, in1=rt[:, 2], op0=ALU.mult, op1=ALU.add).then_inc(S["e2"], 1)
            eng.wait_ge(S["e2"], g + 1)
            v.tensor_reduce(rv[:, 2], rt[:, 5], AX, ALU.max).then_inc(S["m2"], 1)
            eng.wait_ge(S["m2"], g + 1)
            v.tensor_tensor(rt[:, 6], rt[:, 5], bc(2), ALU.is_equal).then_inc(S["s2"], 1)
            v.tensor_scalar(rv[:, 4], rv[:, 2], 1.0, None, ALU.add).then_inc(S["den"], 1)
            eng.wait_ge(S["s2"], g + 1)
            v.tensor_tensor(rt[:, 7], rt[:, 6], rank[:, :, :], ALU.mult).then_inc(S["s2r"], 1)
            eng.wait_ge(S["den"], g + 1)
            v.reciprocal(rv[:, 5], rv[:, 4]).then_inc(S["rden"], 1)
            eng.wait_ge(S["s2r"], g + 1)
            v.tensor_reduce(rv[:, 3], rt[:, 7], AX, ALU.max).then_inc(S["ms2"], 1)
            eng.wait_ge(S["ms2"], g + 1)
            v.tensor_tensor(rt[:, 8], rt[:, 7], bc(3), ALU.is_equal).then_inc(S["o2"], 1)
            eng.wait_ge(S["o2"], g + 1)
            v.tensor_tensor(rt[:, 9], rt[:, 8], bc(2), ALU.mult).then_inc(S["num"], 1)
            eng.wait_ge(S["num"], g + 1)
            v.tensor_tensor(rt[:, 10], rt[:, 9], rt[:, 4], ALU.add).then_inc(S["wt"], 1)
            eng.wait_ge(S["wt"], g + 1)
            eng.wait_ge(S["rden"], g + 1)
            v.tensor_tensor(rt[:, 11], rt[:, 10], bc(5), ALU.mult).then_inc(S["vhi"], 1)
            eng.wait_ge(S["vhi"], 2 * g + 1)
            w4 = rt[:, 11].rearrange("p (q h) e -> p q h e", h=2)
            since(eng, "wtr", 2 * g)
            v.tensor_copy(vv[:, :, :, 0, :].bitcast(f32r), w4).then_inc(S["vhi"], 1)
            eng.wait_ge(S["vhi"], 2 * g + 2)
            v.tensor_tensor(vv[:, :, :, 1, :], w4, vv[:, :, :, 0, :], ALU.subtract).then_inc(S["vlo"], 1)

        def dve_expert(eng, g, e):
            if e % 2 == 0:
                eng.wait_ge(S["f2"], EXP * KC * g + 2 * KC * (e // 2 + 1))
                eng.wait_ge(S["wb"], EXP // 2 * g + e // 2 + 1)
            since(eng, "acc", EXP * g + max(e - 3, 0))
            v.scalar_tensor_tensor(out=mes[:, e % 4, :], in0=P[:, (XC, XD)[e // 2 % 2], HW * (e % 2):HW * (e % 2) + HW],
                                   scalar=cols[:, R["b2"] + e:R["b2"] + e + 1], in1=wbs[:, e, :],
                                   op0=ALU.add, op1=ALU.mult).then_inc(S["me"], 1)

        @block.vector
        def _(eng):
            eng.wait_ge(S["ld_x"], 32)
            rv3 = res[:, :].rearrange("p (b f) -> p b f", b=HALF)
            for b in range(HALF):
                v.bn_stats(stats[:, b, :], rv3[:, b, :]).then_inc(S["gn_stat"], 1)
            eng.wait_ge(S["gn_stat"], HALF)
            for b in range(HALF):
                v.bn_aggr(mv[:, b, :], stats[:, b, :]).then_inc(S["gn_agg"], 1)
            eng.wait_ge(S["gn_agg"], HALF)
            eng.wait_ge(S["gn_avg"], 1)
            v.tensor_copy(gmean[:, :], P[:, 0, 0:HALF]).then_inc(S["gn_dev"], 1)
            eng.wait_ge(S["gn_dev"], 1)
            v.tensor_tensor(gdev[:, 0, :], mv[:, :, 0], gmean[:, :], ALU.subtract).then_inc(S["gn_dev"], 1)
            eng.wait_ge(S["gn_dev"], 2)
            v.tensor_tensor(gdev[:, 0, :], gdev[:, 0, :], gdev[:, 0, :], ALU.mult).then_inc(S["gn_dsq"], 1)
            eng.wait_ge(S["gn_dsq"], 1)
            v.tensor_tensor(gdev[:, 1, :], gdev[:, 0, :], mv[:, :, 1], ALU.add).then_inc(S["gn_dsq"], 1)
            eng.wait_ge(S["gn_rs"], 1)
            for b in range(HALF):
                v.tensor_scalar(gn[:, b, :], rv3[:, b, :], gmean[:, b:b + 1], grs[:, b:b + 1], ALU.subtract, ALU.mult).then_inc(S["gn_out"], 1)
            eng.wait_ge(S["k_ident"], 1)
            v.tensor_reduce(mask8[:, :], ident[:, :].rearrange("p (j e) -> p e j", e=BLK), AX, ALU.add).then_inc(S["k_mask"], 1)
            eng.wait_ge(S["ld_wssm"], 112)
            eng.wait_ge(S["k_mask"], 1)
            v.tensor_tensor(Asel[:, :, :], rep(Als[:, :], 2, BLK), rep(mask8[:, :], 1, ST), ALU.mult).then_inc(S["a_selx"], 1)
            eng.wait_ge(S["ld_rows"], 16 * 16)
            v.tensor_copy(bbx[:, :, :], rep(bbc[:, :], 2, BLK)).then_inc(S["bbx"], 1)

            def features(h):
                for fh in range(2):
                    eng.wait_ge(S["ht_mm"], 2 * h + fh + 1)
                    v.tensor_tensor(hT[:, fh, HALF * h:HALF * h + HALF, :], P[:, 2 * h + fh, :].rearrange("p (b n) -> p b n", n=NODES),
                                    rep(cb1s[:, :], 1, HALF), ALU.add).then_inc(S["ht_ev"], 1)

            eng.wait_ge(S["ld_wgn"], 48)
            features(0)
            eng.wait_ge(S["prep1"], 4)
            v.tensor_copy(bbcol[:, :], P[:, 7, 208:210]).then_inc(S["bbcol"], 1)
            v.tensor_copy(cols[:, :], P[:, 7, 0:NROWS]).then_inc(S["cols_ev"], 1)
            for h in range(2):
                v.tensor_copy(WmT2[:, h, :], P[:, 7, 128:192]).then_inc(S["wmt_ev"], 1)
            features(1)
            eng.wait_ge(S["ht_ev"], 4)
            for ti, t in enumerate("ABC"):
                lo, hi = NODE[t]
                for fh in range(2):
                    v.tensor_reduce(mu[:, ti, fh, :], hT[:, fh, :, lo:hi], AX, ALU.add).then_inc(S["mu_ready"], 1)
            eng.wait_ge(S["mu_ready"], 6)
            for ti, t in enumerate("ABC"):
                lo, hi = NODE[t]
                v.tensor_scalar(mu[:, ti], mu[:, ti], 1.0 / (hi - lo), None, ALU.mult).then_inc(S["mu_ready"], 1)
            eng.wait_ge(S["cols_ev"], 1)
            for ti, t in enumerate("ABC"):
                e0, e1, e2 = (R["bl"] + i for i in node_edges(t))
                v.tensor_tensor(blsum[:, ti:ti + 1], cols[:, e0:e0 + 1], cols[:, e1:e1 + 1], ALU.add).then_inc(S["bls_ready"], 1)
            eng.wait_ge(S["bls_ready"], 3)
            for ti, t in enumerate("ABC"):
                e2 = R["bl"] + node_edges(t)[2]
                v.tensor_tensor(blsum[:, ti:ti + 1], blsum[:, ti:ti + 1], cols[:, e2:e2 + 1], ALU.add).then_inc(S["bls_ready"], 1)
            eng.wait_ge(S["bls_ready"], 6)
            eng.wait_ge(S["prep2"], 2)
            v.tensor_copy(WzH[:, :], P[:, 7, 0:128]).then_inc(S["wz_hi"], 1)
            v.tensor_copy(WgH[:, :], Wins[:, INNER:2 * INNER]).then_inc(S["wz_hi"], 1)
            eng.wait_ge(S["wz_hi"], 2)
            v.tensor_tensor(WzL[:, :], P[:, 7, 0:128], WzH[:, :], ALU.subtract).then_inc(S["wz_lo"], 1)
            v.tensor_tensor(WgL[:, :], Wins[:, INNER:2 * INNER], WgH[:, :], ALU.subtract).then_inc(S["wz_lo"], 1)
            v.tensor_tensor(bz[:, :], P[:, 7, 128:129], cols[:, R["b_conv"]:R["b_conv"] + 1], ALU.add).then_inc(S["bz"], 1)
            eng.wait_ge(S["a_exp"], 1)
            v.tensor_scalar(Aneg[:, :], Aexp[:, :], -1.0, None, ALU.mult).then_inc(S["a_neg"], 1)
            for i in range(2):
                v.tensor_copy(Wrep[:, i], rep(Wbcs[:, ST * i:ST * i + ST], 2, BLK)).then_inc(S["wbr"], 1)
            for ti, t in enumerate("ABC"):
                eng.wait_ge(S["c_mm"], 3)
                v.tensor_scalar(cT[:, ti, :], P[:, 6, B * ti:B * ti + B], blsum[:, ti:ti + 1], None, ALU.add).then_inc(S["c_ev"], 1)
            eng.wait_ge(S["c_ev"], 3)
            eng.wait_ge(S["o_mm"], 3)
            for ti, t in enumerate("ABC"):
                lo, hi = NODE[t]
                n = hi - lo
                bank, at = ((4, 0), (5, 0), (5, B * n))[ti]
                v.tensor_tensor(rT[:, :, lo:hi], P[:, bank, at:at + B * n].rearrange("p (b n) -> p b n", n=n),
                                rep(cT[:, ti, :], 2, n), ALU.add).then_inc(S["r_add"], 1)
            v.tensor_copy(selU[:, :, :].rearrange("p j (s e) -> p j s e", e=BLK),
                          rep(ident[:, :].rearrange("p (j e) -> p j e", e=BLK), 2, ST)).then_inc(S["k_selu"], 1)
            eng.wait_ge(S["k_zero"], 8)
            for k in range(4):
                v.tensor_copy(selS[:, k, BLK * k:BLK * k + BLK], mask8[:, :]).then_inc(S["k_selu"], 1)
            eng.wait_ge(S["k_sel"], 6)
            v.tensor_copy(selW[:, :, :], selWf[:, :, :, :].rearrange("p e h d -> p e (h d)")).then_inc(S["k_selw"], 1)
            eng.wait_ge(S["ld_wf"], 64)
            eng.wait_ge(S["ht_mm"], 4)

            def outputs(c):
                eng.wait_ge(S["out_mm"], c + 1)
                v.tensor_tensor(gn[:, 2 * c:2 * c + 2, :], P[:, c, :].rearrange("p (b f) -> p b f", f=HW),
                                rep(bfs[:, :], 1, 2), ALU.add).then_inc(S["out_ev"], 1)

            def residual(c):
                eng.wait_ge(S["y_mm"], c + 1)
                v.scalar_tensor_tensor(out=res[:, 512 * c:512 * c + 512], in0=P[:, 4 + c, :], scalar=cols[:, R["cb2"]:R["cb2"] + 1],
                                       in1=res[:, 512 * c:512 * c + 512], op0=ALU.add, op1=ALU.add).then_inc(S["res_ready"], 1)

            outputs(0)
            outputs(1)
            residual(0)
            outputs(2)
            residual(1)
            outputs(3)
            residual(2)
            residual(3)

            def body(i, p, nxt, prev):
                q = 1 - p
                if prev is not None:
                    dve_gate(eng, prev, q)
                dve_step(eng, i, p, 1)
                if prev is not None:
                    dve_t1(eng, prev, q)
                if nxt is not None:
                    dve_xn(eng, nxt)
                dve_step(eng, i, p, 2)
                if prev is not None:
                    dve_lnF(eng, prev)
                dve_step(eng, i, p, 3)
                if prev is not None:
                    dve_router1(eng, prev)
                dve_step(eng, i, p, 4)
                if prev is not None:
                    dve_router2(eng, prev)
                dve_step(eng, i, p, 5)
                if prev is not None:
                    dve_xn2(eng, prev)
                dve_step(eng, i, p, 6)
                dve_step(eng, i, p, 7)
                if nxt is not None:
                    dve_u(eng, nxt, q)
                for b in range(8, 12):
                    dve_step(eng, i, p, b)
                for b in range(12, NBLK):
                    dve_step(eng, i, p, b)
                    if prev is not None:
                        dve_expert(eng, prev, 2 * (b - 12))
                        dve_expert(eng, prev, 2 * (b - 12) + 1)
                if nxt is not None:
                    dve_bm(eng, nxt, q, 0)
                    dve_step(eng, nxt, q, 0)

            dve_xn(eng, 0)
            dve_u(eng, 0, 0)
            eng.wait_ge(S["prep2"], 3)
            v.tensor_tensor(b1c[:, :], P[:, XD, 0:EXP * KC], cols[:, R["b1"]:R["b1"] + EXP * KC], ALU.add).then_inc(S["b1c"], 1)
            dve_bm(eng, 0, 0, 0)
            dve_step(eng, 0, 0, 0)
            body(0, 0, 1, None)
            body(1, 1, 2, 0)
            with eng.Fori(0, LOOPS) as it:
                for par in range(2):
                    i = it * 2 + (2 + par)
                    body(i, par, i + 1, i - 1)
            body(G - 2, 0, G - 1, G - 3)
            body(G - 1, 1, None, G - 2)
            dve_gate(eng, G - 1, 1)
            dve_t1(eng, G - 1, 1)
            dve_lnF(eng, G - 1)
            dve_xn2(eng, G - 1)
            dve_router1(eng, G - 1)
            dve_router2(eng, G - 1)
            for e in range(EXP):
                dve_expert(eng, G - 1, e)

        def pe_ub(eng, g, p, b):
            if b == 0:
                eng.wait_ge(S["ul"], g + 1)
                since(eng, "scan", NBLK * g)
            if b >= UB:
                eng.wait_ge(S["scan"], NBLK * g + b - UB + 1)
            j = block_of(b)
            pe.matmul(P[:, b % UB, :], selU[:, j, :], uh[:, p, :], start=True, stop=False)
            pe.matmul(P[:, b % UB, :], selU[:, j, :], ul[:, p, :], start=False, stop=True).then_inc(S["ub"], 1)

        def pe_sum(eng, g, k):
            eng.wait_ge(S["cm"], SLOTS * g + 2 * k + 2)
            if k == 0:
                since(eng, "yg", g)
            for q in range(4):
                n = 2 * k + q // 2
                last = pe.matmul(P[32 * q:32 * q + 32, YS, :], selS[:, k, :], hs[:, n % 4, q % 2, :],
                                 start=(k == 0), stop=(k == 3))
            last.then_inc(S["ysum"], 1)

        def pe_cenA(eng, g):
            since(eng, "gl", EXP * KC * (g - 2) )
            since(eng, "sp_relu", g)
            since(eng, "sp_abs", g)
            pe.matmul(P[:, XA, 0:HW], cen_m[:, :], res[:, bass.ds(g * HW, HW)], start=True, stop=True).then_inc(S["cen1"], 1)

        def pe_varA(eng, g):
            eng.wait_ge(S["sq1"], g + 1)
            pe.matmul(P[:, XA, HW:T], avg_m[:, :], sq[:, :], start=True, stop=True).then_inc(S["var1"], 1)

        def pe_projz(eng, g):
            eng.wait_ge(S["xl1"], g + 1)
            pe.matmul(P[:, XA, :], WzH[:, :], Xs[:, :], start=True, stop=False)
            pe.matmul(P[:, XA, :], WzL[:, :], Xs[:, :], start=False, stop=True).then_inc(S["z_mm"], 1)

        def pe_projg(eng, g):
            since(eng, "t1", g - 1)
            since(eng, "me", EXP * (g - 2))
            since(eng, "cs", g)
            pe.matmul(P[:, XC, :], WgH[:, :], Xs[:, :], start=True, stop=False)
            pe.matmul(P[:, XC, :], WgL[:, :], Xs[:, :], start=False, stop=True).then_inc(S["g_mm"], 1)

        def pe_dtb(eng, g):
            eng.wait_ge(S["xc"], g + 1)
            pe.matmul(P[:, XA, :], Wdts[:, :], xc[:, :], start=True, stop=True).then_inc(S["dtz_mm"], 1)
            eng.wait_ge(S["sg"], g + 1)
            pe.matmul(P[:, XC, :], Wrep[:, 0].rearrange("p s e -> p (s e)"), xc[:, :], start=True, stop=True).then_inc(S["b_mm"], 1)

        def pe_c(eng, g):
            eng.wait_ge(S["bs"], g + 1)
            pe.matmul(P[:, XC, :], Wrep[:, 1].rearrange("p s e -> p (s e)"), xc[:, :], start=True, stop=True).then_inc(S["c_rep_mm"], 1)

        def pe_po(eng, g):
            eng.wait_ge(S["yg"], g + 1)
            since(eng, "me", EXP * g)
            since(eng, "cs", g + 1)
            for h in range(2):
                last = pe.matmul(P[64 * h:64 * h + 64, XC, 0:HW], Wouts[:, :], ygs[:, HW * h:HW * h + HW], start=True, stop=True)
            last.then_inc(S["po"], 1)

        def pe_cenF(eng, g, p):
            eng.wait_ge(S["t1"], g + 1)
            since(eng, "gl", EXP * KC * g)
            pe.matmul(P[:, XB, 0:HW], cen_m[:, :], t1[:, p, :], start=True, stop=True).then_inc(S["cen2"], 1)

        def pe_varF(eng, g):
            eng.wait_ge(S["sq2"], g + 1)
            pe.matmul(P[:, XB, HW:T], avg_m[:, :], sq2[:, :], start=True, stop=True).then_inc(S["var2"], 1)

        def pe_router(eng, g):
            eng.wait_ge(S["tn"], g + 1)
            eng.wait_ge(S["vq"], g + 1)
            for q in range(2):
                pe.matmul(P[:, XB, 2 * EXP * q:2 * EXP * q + 2 * EXP], tns[:, 128 * q:128 * q + 128],
                          Wrt[:, :, :].rearrange("p h e -> p (h e)"), start=True, stop=True).then_inc(S["lg"], 1)

        def pe_wb(eng, g):
            eng.wait_ge(S["vlo"], g + 1)
            for q in range(2):
                pe.transpose(P[0:32, XB, 128 * q:128 * q + 128], vv[:, q].rearrange("p h r e -> p (h r e)"), ident[:, :]).then_inc(S["wtr"], 1)
            eng.wait_ge(S["wtc"], g + 1)
            for e in range(EXP):
                r = e // 2
                if e % 2 == 0 and r >= 2:
                    eng.wait_ge(S["wb"], EXP // 2 * g + r - 1)
                if e == 2:
                    since(eng, "me", EXP * g)
                pe.matmul(P[:, (XB, XD)[r % 2], HW * (e % 2):HW * (e % 2) + HW], selW[:, e, :], wT[:, :],
                          start=True, stop=True).then_inc(S["wb_mm"], 1)

        def started(g):
            return min(g + 2, G) if isinstance(g, int) else g + 2

        def pe_f1(eng, g, r):
            e, k = r // KC, r % KC
            if r == 0:
                eng.wait_ge(S["xl2"], g + 1)
                eng.wait_ge(S["sp_relu"], started(g))
            if r == 1:
                eng.wait_ge(S["wb"], EXP // 2 * (g + 1))
            if r >= 2:
                eng.wait_ge(S["gl"], EXP * KC * g + r - 1)
            bank = (XA, XB)[r % 2]
            pe.matmul(P[:, bank, :], W1H[:, e, 128 * k:128 * k + 128], X2[:, :], start=True, stop=False)
            pe.matmul(P[:, bank, :], W1L[:, e, 128 * k:128 * k + 128], X2[:, :], start=False, stop=True).then_inc(S["f1"], 1)

        def pe_f2(eng, g, r):
            e, k = r // KC, r % KC
            eng.wait_ge(S["gl"], EXP * KC * g + r + 1)
            pair = r // (2 * KC)
            if r == 0:
                eng.wait_ge(S["cs"], started(g))
            if r == 2 * KC:
                eng.wait_ge(S["wb"], EXP // 2 * (g + 1))
            if r % (2 * KC) == 0 and pair >= 2:
                eng.wait_ge(S["me"], EXP * g + 2 * (pair - 1))
            for h in range(2):
                last = pe.matmul(P[64 * h:64 * h + 64, (XC, XD)[pair % 2], HW * (e % 2):HW * (e % 2) + HW], W2s[:, e, k, :],
                                 hb[:, r % 4, HW * h:HW * h + HW], start=(k == 0), stop=(k == KC - 1))
            last.then_inc(S["f2"], 1)

        def pe_ffn(eng, g, lo, hi):
            for r in range(lo, hi):
                if r < EXP * KC:
                    pe_f1(eng, g, r)
                if r >= 2:
                    pe_f2(eng, g, r - 2)

        @block.tensor
        def _(eng):
            eng.wait_ge(S["k_sel"], 6)
            eng.wait_ge(S["gn_agg"], HALF)
            pe.matmul(P[:, 0, 0:HALF], pair_m[:, :], mv[:, :, 0], start=True, stop=True).then_inc(S["gn_avg"], 1)
            eng.wait_ge(S["gn_dsq"], 2)
            pe.matmul(P[:, 0, 2 * HALF:3 * HALF], pair_m[:, :], gdev[:, 1, :], start=True, stop=True).then_inc(S["gn_var"], 1)
            eng.wait_ge(S["ld_wgn"], 48)
            eng.wait_ge(S["gn_ln"], 1)

            def features(h):
                for fh in range(2):
                    for b in range(HALF):
                        if h == 0 and fh == 0:
                            eng.wait_ge(S["gn_out"], b + 1)
                        last = pe.matmul(P[:, 2 * h + fh, NODES * b:NODES * b + NODES], gn[64 * h:64 * h + 64, b, 128 * fh:128 * fh + 128],
                                         cW1s[64 * h:64 * h + 64, :], start=True, stop=True)
                    last.then_inc(S["ht_mm"], 1)

            features(0)
            eng.wait_ge(S["k_ident"], 1)
            eng.wait_ge(S["ld_rows"], 16 * 16)
            pe.transpose(P[:, 7, 0:NROWS], rows[:, :], ident[0:NROWS, 0:NROWS]).then_inc(S["prep1"], 1)
            eng.wait_ge(S["ld_wssm"], 112)
            pe.transpose(P[:, 7, 128:192], Wins[0:64, 0:128], ident[0:64, 0:64]).then_inc(S["prep1"], 1)
            eng.wait_ge(S["a_selx"], 1)
            pe.matmul(P[:, 7, 192:192 + NBLK], Asel[:, :, :].rearrange("p s e -> p (s e)"), gsel[:, :], start=True, stop=True).then_inc(S["prep1"], 1)
            eng.wait_ge(S["bbx"], 1)
            pe.transpose(P[:, 7, 208:210], bbx[:, :, :].rearrange("p s e -> p (s e)"), ident[0:2, 0:2]).then_inc(S["prep1"], 1)
            features(1)
            eng.wait_ge(S["wmt_ev"], 2)
            eng.wait_ge(S["a_exp"], 1)
            pe.matmul(P[:, 7, 0:128], WmT2[:, :, :].rearrange("p h d -> p (h d)"), Wcv[:, :], start=True, stop=True).then_inc(S["prep2"], 1)
            pe.matmul(P[:, 7, 128:129], Wcv[:, :], cols[:, R["b_in"]:R["b_in"] + 1], start=True, stop=True).then_inc(S["prep2"], 1)
            eng.wait_ge(S["wrs_ready"], 6)
            eng.wait_ge(S["ht_ev"], 4)
            for ti, t in enumerate("ABC"):
                lo, hi = NODE[t]
                n = hi - lo
                bank, at = ((4, 0), (5, 0), (5, B * n))[ti]
                for fh in range(2):
                    last = pe.matmul(P[:, bank, at:at + B * n], Wrsum[:, ti, fh, :], hT[:, fh, :, lo:hi], start=(fh == 0), stop=(fh == 1))
                last.then_inc(S["o_mm"], 1)
            eng.wait_ge(S["ld_wl"], 32)
            eng.wait_ge(S["mu_ready"], 9)
            for ti, t in enumerate("ABC"):
                todo = [(i, fh) for i in node_edges(t) for fh in range(2)]
                for n, (i, fh) in enumerate(todo):
                    last = pe.matmul(P[:, 6, B * ti:B * ti + B], Wls[:, i, fh, :], mu[:, "ABC".index(EDGES[i][0]), fh, :],
                                     start=(n == 0), stop=(n == len(todo) - 1))
                last.then_inc(S["c_mm"], 1)
            eng.wait_ge(S["ld_wf"], 64)
            eng.wait_ge(S["r_ready"], 1)

            def outputs(c):
                for b in range(2 * c, 2 * c + 2):
                    for h in range(2):
                        last = pe.matmul(P[64 * h:64 * h + 64, c, HW * (b % 2):HW * (b % 2) + HW], rT[:, HALF * h + b, :], Wfs[:, :],
                                         start=True, stop=True)
                last.then_inc(S["out_mm"], 1)

            def mixed(c):
                eng.wait_ge(S["out_ev"], c + 1)
                pe.matmul(P[:, 4 + c, :], cW2bd[:, :], gn[:, 2 * c:2 * c + 2, :].rearrange("p b f -> p (b f)"), start=True, stop=True).then_inc(S["y_mm"], 1)

            outputs(0)
            outputs(1)
            eng.wait_ge(S["c_ev"], 3)
            eng.wait_ge(S["r_add"], 3)
            eng.wait_ge(S["wz_lo"], 2)
            eng.wait_ge(S["bz"], 1)
            mixed(0)
            outputs(2)
            mixed(1)
            outputs(3)
            eng.wait_ge(S["k_misc"], 13)
            eng.wait_ge(S["res_ready"], 1)
            pe_cenA(eng, 0)
            mixed(2)
            mixed(3)
            pe_varA(eng, 0)
            pe_projz(eng, 0)
            eng.wait_ge(S["res_ready"], 4)
            eng.wait_ge(S["wbr"], 2)
            pe_projg(eng, 0)
            pe_dtb(eng, 0)
            eng.wait_ge(S["ld_ffn"], 32)
            for e in range(EXP):
                for k in range(KC):
                    last = pe.matmul(P[:, XD, KC * e + k:KC * e + k + 1], W1r[0:64, e, 128 * k:128 * k + 128],
                                     cols[0:64, R["ln_b"] + e:R["ln_b"] + e + 1], start=True, stop=True)
            last.then_inc(S["prep2"], 1)
            pe_c(eng, 0)
            eng.wait_ge(S["k_selu"], 5)

            def body(i, p, nxt, prev):
                q = 1 - p
                if nxt is not None:
                    pe_cenA(eng, nxt)
                    pe_varA(eng, nxt)
                if prev is not None:
                    pe_po(eng, prev)
                pe_ub(eng, i, p, 3)
                if prev is not None:
                    pe_cenF(eng, prev, q)
                pe_ub(eng, i, p, 4)
                if prev is not None:
                    pe_varF(eng, prev)
                if nxt is not None:
                    pe_projz(eng, nxt)
                    pe_projg(eng, nxt)
                pe_ub(eng, i, p, 5)
                if prev is not None:
                    pe_router(eng, prev)
                pe_ub(eng, i, p, 6)
                pe_ub(eng, i, p, 7)
                if nxt is not None:
                    pe_dtb(eng, nxt)
                pe_sum(eng, i, 0)
                if nxt is not None:
                    pe_c(eng, nxt)
                pe_ub(eng, i, p, 8)
                if prev is not None:
                    pe_wb(eng, prev)
                pe_ub(eng, i, p, 9)
                pe_ub(eng, i, p, 10)
                pe_sum(eng, i, 1)
                if prev is not None:
                    pe_ffn(eng, prev, 0, 2)
                pe_ub(eng, i, p, 11)
                if prev is not None:
                    pe_ffn(eng, prev, 2, 3)
                pe_ub(eng, i, p, 12)
                if prev is not None:
                    pe_ffn(eng, prev, 3, 5)
                pe_ub(eng, i, p, 13)
                if prev is not None:
                    pe_ffn(eng, prev, 5, 8)
                pe_ub(eng, i, p, 14)
                if prev is not None:
                    pe_ffn(eng, prev, 8, 11)
                pe_ub(eng, i, p, 15)
                pe_sum(eng, i, 2)
                if prev is not None:
                    pe_ffn(eng, prev, 11, 16)
                if nxt is not None:
                    for b in range(UB):
                        pe_ub(eng, nxt, q, b)
                if prev is not None:
                    pe_ffn(eng, prev, 16, 18)
                pe_sum(eng, i, 3)

            for b in range(UB):
                pe_ub(eng, 0, 0, b)
            body(0, 0, 1, None)
            eng.wait_ge(S["k_selw"], 1)
            eng.wait_ge(S["ld_dup"], 64)
            eng.wait_ge(S["ffn_l"], 1)
            eng.wait_ge(S["b1c"], 1)
            body(1, 1, 2, 0)
            with eng.Fori(0, LOOPS) as it:
                for par in range(2):
                    i = it * 2 + (2 + par)
                    body(i, par, i + 1, i - 1)
            body(G - 2, 0, G - 1, G - 3)
            body(G - 1, 1, None, G - 2)
            pe_po(eng, G - 1)
            pe_cenF(eng, G - 1, 1)
            pe_varF(eng, G - 1)
            pe_router(eng, G - 1)
            pe_wb(eng, G - 1)
            pe_ffn(eng, G - 1, 0, 18)


_INS = [('x', 'x'), ('L0_conv_W1', 'cW1'), ('L0_conv_b1', 'cb1'), ('L0_conv_Wl', 'Wl'), ('L0_conv_bl', 'bl'),
        ('L0_conv_Wr', 'Wr'), ('L0_conv_Wf', 'Wf'), ('L0_conv_bf', 'bf'), ('L0_conv_W2', 'cW2'), ('L0_conv_b2', 'cb2'),
        ('L1_attn_W_in', 'W_in'), ('L1_attn_b_in', 'b_in'), ('L1_attn_W_conv', 'W_conv'), ('L1_attn_b_conv', 'b_conv'),
        ('L1_attn_A_log', 'A_log'), ('L1_attn_W_bc', 'W_bc'), ('L1_attn_b_bc', 'b_bc'), ('L1_attn_W_dt', 'W_dt'),
        ('L1_attn_b_dt', 'b_dt'), ('L1_attn_W_out', 'W_out'), ('L1_attn_b_out', 'b_out'), ('L1_ffn_Wr', 'fWr'),
        ('L1_ffn_br', 'fbr'), ('L1_ffn_ln_g', 'ln_g'), ('L1_ffn_ln_b', 'ln_b'), ('L1_ffn_W1', 'W1'), ('L1_ffn_b1', 'b1'),
        ('L1_ffn_W2', 'W2'), ('L1_ffn_b2', 'b2')]


def kernel(**inputs):
    import numpy as _np
    import concourse.bacc as _bacc
    from concourse import mybir as _mybir
    from concourse.bass_utils import run_bass_kernel_spmd as _run

    nc = _bacc.Bacc("TRN2", target_bir_lowering=False, num_devices=1)
    arrays, args = {}, {}
    for name, short in _INS:
        a = _np.ascontiguousarray(inputs[name])
        arrays[f"in_{name}"] = a
        args[short] = nc.dram_tensor(f"in_{name}", a.shape, _mybir.dt.from_np(a.dtype), kind="ExternalInput").ap()
    args["out"] = nc.dram_tensor("out_0", (B, D, 16, 16), _mybir.dt.float32, kind="ExternalOutput").ap()
    build(nc, **args)
    r = _run(nc, [arrays], core_ids=[0])
    return r.results[0]["out_0"]
```

```python
import concourse.bass as bass
from concourse import mybir
from contextlib import ExitStack

B, D, HW = 16, 64, 256
HALF = B // 2
G = HALF
LOOPS = (G - 4) // 2
T = 2 * HW
HID, NODES, NE = 128, 64, 9
NODE = {"A": (0, 32), "B": (32, 48), "C": (48, 64)}
EDGES = [("A", "B"), ("B", "A"), ("A", "C"), ("C", "A"), ("B", "C"), ("C", "B"), ("A", "A"), ("B", "B"), ("C", "C")]
INNER, ST = 128, 16
BLK = INNER // ST
NBLK = INNER // BLK
SLOTS = NBLK // 2
EXP, FH = 8, 256
KC = FH // 128
NROWS = EXP * KC + NE + 2 + 1 + 1 + 1 + EXP + 1 + EXP + EXP
EPS = 1e-5

R, _at = {}, 0
for _name, _n in (("b1", EXP * KC), ("bl", NE), ("b_in", 2), ("b_conv", 1), ("b_dt", 1),
                  ("b_out", 1), ("b2", EXP), ("cb2", 1), ("ln_g", EXP), ("ln_b", EXP)):
    R[_name] = _at
    _at += _n
assert _at == NROWS

SEMS = """ld_x0 ld_x1 ld_rows ld_wgn ld_wr ld_wl ld_wf ld_wssm ld_ffn ld_dup
gn_stat gn_agg gn_avg gn_dev gn_dsq gn_var gn_ln gn_rs gn_out
k_zero k_ident k_sel k_misc k_selu k_selw k_mask k_col0 k_cw1 bbx bbcol
ht_mm ht_ev mu_ready wrs_ready o_mm c_mm bls_ready c_ev r_add r_ready out_mm out_ev y_mm res_ready
prep1 cols_ev wmt_ev a_exp a_neg a_selx prep2 wz_hi wz_lo bz b1c wbr ffn_g ffn_h ffn_l
cen1 sq1 var1 ln1 rs1 xn1 xh1 xl1 z_mm g_mm xc sg sgc
dtz_mm b_mm c_rep_mm sp_abs sp_exp sp_ln sp_relu bs cs dt u uh ul dt_out dt_in0 dt_in1 dt_in2 dt_in3 aexp
ub bm scan cm ysum
yg po t1 cen2 sq2 var2 ln2 rs2 r2 vq lnq rq tn xn2 xh2 xl2
lg lgb m1 dd ex s1 ms1 o1 e2 m2 s2 s2r ms2 o2 den rden num wt vhi vlo wtr wtc wb_mm wb
f1 gl f2 me acc out_sem""".split()


def rep(ap, axis, n):
    v = ap.unsqueeze(axis)
    return v.broadcast_to([*v.shape[:axis], n, *v.shape[axis + 1:]])


def build(nc, x, cW1, cb1, Wl, bl, Wr, Wf, bf, cW2, cb2, W_in, b_in, W_conv, b_conv, A_log, W_bc, b_bc,
          W_dt, b_dt, W_out, b_out, fWr, fbr, ln_g, ln_b, W1, b1, W2, b2, out):
    fp32, f32r = mybir.dt.float32, mybir.dt.float32r
    ALU = mybir.AluOpType
    ACT = mybir.ActivationFunctionType
    AX = mybir.AxisListType.X

    dt_dram = nc.dram_tensor("dt_scratch", (2, INNER, T), fp32, kind="Internal").ap()

    ctx = ExitStack()
    with ctx:
        def sb(name, shape, dt=fp32):
            return ctx.enter_context(nc.sbuf_tensor(name, shape, dt))

        S = {n: ctx.enter_context(nc.semaphore(n)) for n in SEMS}

        def since(eng, name, count):
            if isinstance(count, int) and count <= 0:
                return
            eng.wait_ge(S[name], count)

        def so_far(g, ahead):
            return min(g + ahead, G) if isinstance(g, int) else g + ahead

        res = sb("res", [128, HALF * HW])
        stats = sb("stats", [128, HALF, 6])
        mv = sb("mv", [128, HALF, 2])
        gdev = sb("gdev", [128, 2, HALF])
        gvar = sb("gvar", [128, HALF])
        gmean = sb("gmean", [128, HALF])
        grs = sb("grs", [128, HALF])
        cW2bd = sb("cW2bd", [128, 128])
        mu = sb("mu", [128, 3, 2, B])
        blsum = sb("blsum", [128, 3])
        cT = sb("cT", [128, 3, B])
        ident = sb("ident", [128, 128])
        cen_m = sb("cen_m", [128, 128])
        avg_m = sb("avg_m", [128, 128])
        pair_m = sb("pair_m", [128, 128])
        gsel = sb("gsel", [128, NBLK])
        mask8 = sb("mask8", [128, BLK])
        selU = sb("selU", [128, NBLK // 2, 128], f32r)
        selS = sb("selS", [128, 4, 32])
        selW = sb("selW", [32, EXP, 128], f32r)
        rank = sb("rank", [128, 4, EXP])
        epst = sb("epst", [128, 1])
        onet = sb("onet", [128, 1])
        cols = sb("cols", [128, NROWS])
        bbc = sb("bbc", [2, ST])
        bbx = sb("bbx", [2, ST, BLK])
        bbcol = sb("bbcol", [128, 2])
        Wins = sb("Wins", [128, 2 * INNER])
        WmT2 = sb("WmT2", [128, 2, 64])
        WzH = sb("WzH", [128, 128], f32r)
        WzL = sb("WzL", [128, 128], f32r)
        WgH = sb("WgH", [128, 128], f32r)
        WgL = sb("WgL", [128, 128], f32r)
        bz = sb("bz", [128, 1])
        Als = sb("Als", [128, ST])
        Aneg = sb("Aneg", [128, NBLK])
        Aexp = sb("Aexp", [128, NBLK])
        Wbcs = sb("Wbcs", [128, 2 * ST])
        Wrep = sb("Wrep", [128, 2, ST, BLK])
        Wdts = sb("Wdts", [128, INNER])
        Wouts = sb("Wouts", [128, D])
        Wrt = sb("Wrt", [128, 2, EXP])
        brs = sb("brs", [128, EXP])
        W1H = sb("W1H", [128, EXP, FH], f32r)
        W1L = sb("W1L", [128, EXP, FH], f32r)
        W2s = sb("W2s", [128, EXP, KC, D])
        b1c = sb("b1c", [128, EXP * KC])
        sq = sb("sq", [128, HW])
        rs = sb("rs", [128, HW])
        xnt = sb("xnt", [64, T])
        Xs = sb("Xs", [128, T], f32r)
        xc = sb("xc", [128, T])
        sg0 = sb("sg0", [128, T])
        sg = sb("sg", [128, 2, T])
        sp = sb("sp", [128, T])
        rl = sb("rl", [128, T])
        u = rl
        dts = sb("dts", [128, 2, T])
        us = sb("us", [128, 2, 2, T], f32r)
        Bs = sb("Bs", [128, 2, T])
        Cs = sb("Cs", [128, 2, T])
        av = sb("av", [128, 2, NBLK, T])
        hs = sb("hs", [128, 4, 2, T])
        ygs = sb("ygs", [128, T])
        t1 = sb("t1s", [128, 2, HW])
        sq2 = sb("sq2s", [128, HW])
        rs2 = sb("rs2s", [128, HW])
        r2s = sb("r2s", [128, HW])
        vqs = sb("vqs", [128, HW])
        rqs = sb("rqs", [128, HW])
        tns = sb("tns", [128, HW])
        xnt2 = sb("xnt2", [64, T])
        X2 = sb("X2", [128, T], f32r)
        rt = sb("rt", [128, 12, 4, EXP])
        rv = sb("rv", [128, 8, 4])
        vv = sb("vv", [128, 2, 2, 2, EXP])
        wT = sb("wT", [32, HW], f32r)
        wbs = sb("wbs", [128, EXP, HW])
        hb = sb("hb", [128, 4, T])
        mes = sb("mes", [128, 4, HW])
        acc = sb("accs", [128, 2, HW])

        def within(buf, at, shape):
            n = 1
            for d in shape:
                n *= d
            names = "abcd"[:len(shape)]
            view = buf[:, at:at + n]
            if len(shape) > 1:
                view = view.rearrange("p (" + " ".join(names) + ") -> p " + " ".join(names), **dict(zip(names[1:], shape[1:])))
            return view, at + n

        gn = hs[:, :, :, :].rearrange("p a b t -> p (a b t)")[:, 0:HALF * HW].rearrange("p (b f) -> p b f", b=HALF)
        buf0 = av[:, 0].rearrange("p m t -> p (m t)")
        buf1 = av[:, 1].rearrange("p m t -> p (m t)")
        Wrs_raw, at = within(buf0, 0, [NE, 2, HID])
        Wls, at = within(buf0, at, [NE, 2, HID])
        hT, at = within(buf0, at, [2, B, NODES])
        W1g, at = within(buf1, 0, [EXP, FH])
        W1r, at = within(buf1, at, [EXP, FH])
        Wrsum, at = within(buf1, at, [3, 2, HID])
        rT, at = within(buf1, at, [B, NODES])
        selWf, at = within(buf1[0:32], at, [EXP, 2, 64])

        Wfs, at = within(buf1, at, [HW])
        bfs, at = within(buf1, at, [HW])
        Wcv, at = within(buf1, at, [INNER])
        Asel, at = within(buf1, at, [ST, BLK])
        cb1s, at = within(buf1, at, [NODES])
        cW1bd, at = within(buf1, at, [2 * NODES])
        rows, at = within(buf1[0:NROWS], at, [128])
        assert at <= NBLK * T

        P = ctx.enter_context(nc.psum_tensor("P", [128, 8, 512], fp32))
        UB = 3
        XD, XA, XB, XC, YS = 3, 4, 5, 6, 7

        v = nc.vector
        a_ = nc.scalar
        pe = nc.tensor
        gp = nc.gpsimd

        def node_edges(t):
            return [i for i, (_, d) in enumerate(EDGES) if d == t]

        def block_of(m):
            return 4 * (m % 4) + m // 4

        xv = x.rearrange("(h b) d l w -> h d b (l w)", h=2)
        ov = out.rearrange("(h b) d l w -> h d b (l w)", h=2)

        block = ctx.enter_context(nc.Block())

        def sp_dt(sp_, g, p):
            since(sp_, "dt", g + 1)
            sp_.dma_start(dt_dram[p], dts[:, p, :]).then_inc(S["dt_out"], 16)
            sp_.wait_ge(S["dt_out"], 16 * (g + 1))
            since(sp_, "scan", NBLK * (g - 1))
            if isinstance(g, int) and g < 2:
                sp_.wait_ge(S["k_col0"], g + 1)
            src = dt_dram[p].rearrange("(q k e) (h f) -> k q e h f", k=4, e=BLK, h=2)
            for k in range(4):
                for q in range(4):
                    sp_.dma_start(av[:, p, 4 * k + q, :].rearrange("p (h f) -> p h f", h=2)[:, :, 1:HW],
                                  rep(src[k, q, :, :, 1:HW], 0, ST)).then_inc(S[f"dt_in{k}"], 16)

        def sp_out(sp_, g, p):
            sp_.wait_ge(S["acc"], EXP * (g + 1))
            for h in range(2):
                sp_.dma_start(ov[h, :, bass.ds(g, 1), :], acc[64 * h:64 * h + 64, p:p + 1, :]).then_inc(S["out_sem"], 16)

        @block.sync
        def _(sp_):
            for b in (0, HALF // 2):
                for h in range(2):
                    sp_.dma_start(res[64 * h:64 * h + 64, HW * b:HW * (b + HALF // 2)].rearrange("p (b f) -> p b f", f=HW),
                                  xv[h][:, b:b + HALF // 2, :]).then_inc(S["ld_x%d" % (b // (HALF // 2))], 16)
            sp_.wait_ge(S["k_cw1"], 1)
            for h in range(2):
                sp_.dma_start(cW1bd[64 * h:64 * h + 64, NODES * h:NODES * h + NODES], cW1).then_inc(S["ld_wgn"], 16)
            sp_.dma_start(cb1s[:, :], rep(cb1, 0, 128)).then_inc(S["ld_wgn"], 16)
            for fh in range(2):
                sp_.dma_start(Wrs_raw[:, :, fh, :], Wr[:, 128 * fh:128 * fh + 128, :].rearrange("i f n -> f i n")).then_inc(S["ld_wr"], 16)
            for fh in range(2):
                sp_.dma_start(Wls[:, :, fh, :], Wl[:, 128 * fh:128 * fh + 128, :].rearrange("i f n -> f i n")).then_inc(S["ld_wl"], 16)
            sp_.dma_start(Wfs[:, :], Wf).then_inc(S["ld_wf"], 16)
            sp_.dma_start(bfs[:, :], rep(bf, 0, 128)).then_inc(S["ld_wf"], 16)
            def row(name, ap, off=0):
                sp_.dma_start(rows[R[name] + off:R[name] + off + ap.shape[0], 0:ap.shape[-1]], ap).then_inc(S["ld_rows"], 16)
            row("b1", b1.rearrange("e (k f) -> (e k) f", f=128))
            row("bl", bl)
            row("b_in", b_in.rearrange("(a f) -> a f", f=128))
            row("b_conv", b_conv.unsqueeze(0))
            row("b_dt", b_dt.unsqueeze(0))
            sp_.dma_start(bbc[:, :], b_bc.rearrange("(a s) -> a s", a=2)).then_inc(S["ld_rows"], 16)
            for h in range(2):
                for name, ap in (("b_out", b_out.unsqueeze(0)), ("b2", b2), ("cb2", cb2.unsqueeze(0)), ("ln_g", ln_g), ("ln_b", ln_b)):
                    n = ap.shape[0]
                    sp_.dma_start(rows[R[name]:R[name] + n, 64 * h:64 * h + 64], ap).then_inc(S["ld_rows"], 16)
            sp_.wait_ge(S["k_zero"], 8)
            for h in range(2):
                sp_.dma_start(cW2bd[64 * h:64 * h + 64, 64 * h:64 * h + 64], cW2).then_inc(S["ld_wf"], 16)
            for h in range(2):
                sp_.dma_start(W1r[64 * h:64 * h + 64, :, :], W1.rearrange("e d n -> d e n")).then_inc(S["ld_ffn"], 16)
            sp_.dma_start(W2s[:, :, :, :], W2.rearrange("e (k p) d -> p e k d", p=128)).then_inc(S["ld_dup"], 16)
            for h in range(2):
                sp_.dma_start(Wrt[64 * h:64 * h + 64, h, :], fWr).then_inc(S["ld_dup"], 16)
            sp_.dma_start(brs[:, :], rep(fbr, 0, 128)).then_inc(S["ld_dup"], 16)
            for g in range(3):
                sp_dt(sp_, g, g % 2)
            sp_out(sp_, 0, 0)
            with sp_.Fori(0, LOOPS) as it:
                for par in range(2):
                    i = it * 2 + (2 + par)
                    sp_dt(sp_, i + 1, 1 - par)
                    sp_out(sp_, i - 1, 1 - par)
            sp_dt(sp_, G - 1, 1)
            sp_out(sp_, G - 3, 1)
            sp_out(sp_, G - 2, 0)
            sp_out(sp_, G - 1, 1)
            sp_.wait_ge(S["out_sem"], 32 * G)

        def step_input(eng, by, g, p):
            eng.wait_ge(S["sp_ln"], g + 1)
            eng.wait_ge(S["sp_relu"], g + 1)
            since(eng, "dt_out", 16 * (g - 1))
            by.tensor_tensor(dts[:, p, :], rl[:, :], sp[:, :], ALU.add).then_inc(S["dt"], 1)
            eng.wait_ge(S["dt"], g + 1)
            by.tensor_tensor(u[:, :], dts[:, p, :], xc[:, :], ALU.mult).then_inc(S["u"], 1)

        def pool_slot(eng, g, p, n):
            eng.wait_ge(S["scan"], NBLK * g + 2 * n + 2)
            if n == 0:
                eng.wait_ge(S["cs"], g + 1)
            gp.tensor_tensor(hs[:, n % 4, :, :], hs[:, n % 4, :, :],
                             rep(Cs[:, p, :], 1, 2), ALU.mult).then_inc(S["cm"], 1)

        def pool_acc(eng, g, p, e):
            eng.wait_ge(S["me"], EXP * g + e + 1)
            if e == 0:
                since(eng, "out_sem", 32 * g)
                prev = t1[:, p, :]
            else:
                eng.wait_ge(S["acc"], EXP * g + e)
                prev = acc[:, p, :]
            gp.tensor_tensor(acc[:, p, :], prev, mes[:, e % 4, :], ALU.add).then_inc(S["acc"], 1)

        @block.gpsimd
        def _(eng):
            gp.memset(cW1bd[:, :], 0.0).then_inc(S["k_cw1"], 1)
            gp.memset(ident[:, :], 0.0).then_inc(S["k_zero"], 1)
            gp.memset(avg_m[:, :], 0.0).then_inc(S["k_zero"], 1)
            gp.memset(cW2bd[:, :], 0.0).then_inc(S["k_zero"], 1)
            gp.memset(Wrt[:, :, :], 0.0).then_inc(S["k_zero"], 1)
            gp.memset(pair_m[:, :], 0.5).then_inc(S["k_zero"], 1)
            gp.memset(gsel[:, :], 1.0).then_inc(S["k_zero"], 1)
            gp.memset(selWf[:, :, :, :], 0.0).then_inc(S["k_zero"], 1)
            gp.memset(selS[:, :, :], 0.0).then_inc(S["k_zero"], 1)
            eng.wait_ge(S["k_zero"], 8)
            for h in range(2):
                gp.memset(avg_m[64 * h:64 * h + 64, 64 * h:64 * h + 64], 1.0 / D).then_inc(S["k_misc"], 1)
            eng.wait_ge(S["k_misc"], 2)
            gp.affine_select(out=ident[:, :], in_=ident[:, :], compare_op=ALU.not_equal, fill=1.0, base=0,
                             pattern=[[-1, 128]], channel_multiplier=1).then_inc(S["k_ident"], 1)
            pv = pair_m[:, :].rearrange("p (a b) -> p a b", b=2)
            gp.affine_select(out=pv, in_=pv, compare_op=ALU.is_ge, fill=0.0, base=0,
                             pattern=[[-2, 64], [0, 2]], channel_multiplier=1).then_inc(S["k_sel"], 1)
            gp.affine_select(out=gsel[:, :], in_=gsel[:, :], compare_op=ALU.is_ge, fill=0.0, base=0,
                             pattern=[[-BLK, NBLK]], channel_multiplier=1).then_inc(S["k_sel"], 1)
            gp.affine_select(out=selWf[:, :, :, :], in_=selWf[:, :, :, :], compare_op=ALU.not_equal, fill=1.0, base=0,
                             pattern=[[-1, EXP], [-2 * EXP, 2], [0, 64]], channel_multiplier=1).then_inc(S["k_sel"], 1)
            eng.wait_ge(S["k_sel"], 3)
            gp.affine_select(out=pv, in_=pv, compare_op=ALU.is_ge, fill=0.0, base=1,
                             pattern=[[2, 64], [0, 2]], channel_multiplier=-1).then_inc(S["k_sel"], 1)
            gp.affine_select(out=gsel[:, :], in_=gsel[:, :], compare_op=ALU.is_ge, fill=0.0, base=BLK - 1,
                             pattern=[[BLK, NBLK]], channel_multiplier=-1).then_inc(S["k_sel"], 1)
            gp.affine_select(out=selWf[:, :, :, :], in_=selWf[:, :, :, :], compare_op=ALU.not_equal, fill=1.0, base=-EXP,
                             pattern=[[-1, EXP], [-2 * EXP, 2], [0, 64]], channel_multiplier=1).then_inc(S["k_sel"], 1)
            gp.memset(epst[:, :], EPS).then_inc(S["k_misc"], 1)
            gp.memset(onet[:, :], 1.0).then_inc(S["k_misc"], 1)
            for e in range(EXP):
                gp.memset(rank[:, :, e:e + 1], float(EXP - e)).then_inc(S["k_misc"], 1)
            eng.wait_ge(S["k_ident"], 1)
            gp.tensor_tensor(cen_m[:, :], ident[:, :], avg_m[:, :], ALU.subtract).then_inc(S["k_misc"], 1)
            eng.wait_ge(S["ld_wr"], 32)
            for ti, t in enumerate("ABC"):
                e0, e1, e2 = node_edges(t)
                gp.tensor_tensor(Wrsum[:, ti], Wrs_raw[:, e0], Wrs_raw[:, e1], ALU.add).then_inc(S["wrs_ready"], 1)
            eng.wait_ge(S["wrs_ready"], 3)
            for ti, t in enumerate("ABC"):
                gp.tensor_tensor(Wrsum[:, ti], Wrsum[:, ti], Wrs_raw[:, node_edges(t)[2]], ALU.add).then_inc(S["wrs_ready"], 1)
            eng.wait_ge(S["ld_ffn"], 32)
            eng.wait_ge(S["cols_ev"], 1)
            gp.tensor_tensor(W1g[:, :, :], W1r[:, :, :], rep(cols[:, R["ln_g"]:R["ln_g"] + EXP], 2, FH),
                             ALU.mult).then_inc(S["ffn_g"], 1)
            eng.wait_ge(S["ffn_h"], 1)
            gp.tensor_tensor(W1L[:, :, :], W1g[:, :, :], W1H[:, :, :], ALU.subtract).then_inc(S["ffn_l"], 1)

            eng.wait_ge(S["res_ready"], 4)
            gp.memset(av[:, 0, :, :].rearrange("p m (h f) -> p m h f", h=2)[:, :, :, 0:1], 0.0).then_inc(S["k_col0"], 1)
            eng.wait_ge(S["ffn_l"], 1)
            eng.wait_ge(S["prep2"], 3)
            eng.wait_ge(S["k_selw"], 1)
            gp.memset(av[:, 1, :, :].rearrange("p m (h f) -> p m h f", h=2)[:, :, :, 0:1], 0.0).then_inc(S["k_col0"], 1)

            def body(i, p, nxt, nxt2, prev):
                q = 1 - p
                if nxt is not None:
                    step_input(eng, gp, nxt, q)
                for n in range(0, 6):
                    pool_slot(eng, i, p, n)
                if prev is not None:
                    for e in range(0, 2):
                        pool_acc(eng, prev, q, e)
                pool_slot(eng, i, p, 6)
                if prev is not None:
                    for e in range(2, 4):
                        pool_acc(eng, prev, q, e)
                pool_slot(eng, i, p, 7)
                if prev is not None:
                    for e in range(4, 8):
                        pool_acc(eng, prev, q, e)

            body(0, 0, 1, 2, None)
            body(1, 1, 2, 3, 0)
            with eng.Fori(0, LOOPS) as it:
                for par in range(2):
                    i = it * 2 + (2 + par)
                    body(i, par, i + 1, i + 2, i - 1)
            body(G - 2, 0, G - 1, None, G - 3)
            body(G - 1, 1, None, None, G - 2)
            for e in range(EXP):
                pool_acc(eng, G - 1, 1, e)

        def act_lnA1(eng, g, bank=XD):
            eng.wait_ge(S["cen1"], g + 1)
            since(eng, "var1", g)
            a_.activation(sq[:, :], P[:, bank, 0:HW], ACT.Square).then_inc(S["sq1"], 1)

        def act_lnA2(eng, g, bank=XD):
            eng.wait_ge(S["var1"], g + 1)
            since(eng, "xn1", 2 * g)
            a_.activation(rs[:, :], P[:, bank, HW:T], ACT.Ln, bias=epst[:, 0:1]).then_inc(S["ln1"], 1)
            eng.wait_ge(S["ln1"], g + 1)
            a_.activation(rs[:, :], rs[:, :], ACT.Exp, scale=-0.5).then_inc(S["rs1"], 1)

        def act_siluz(eng, g):
            eng.wait_ge(S["z_mm"], g + 1)
            since(eng, "c_rep_mm", g)
            since(eng, "u", g)
            a_.activation(xc[:, :], P[:, XA, :], ACT.Silu, bias=bz[:, 0:1]).then_inc(S["xc"], 1)

        def act_silug(eng, g):
            eng.wait_ge(S["g_mm"], g + 1)
            since(eng, "sgc", g)
            a_.activation(sg0[:, :], P[:, XC, :], ACT.Silu, bias=cols[:, R["b_in"] + 1:R["b_in"] + 2]).then_inc(S["sg"], 1)

        def act_abs(eng, g):
            eng.wait_ge(S["dtz_mm"], g + 1)
            since(eng, "ul", 2 * g)
            a_.activation(sp[:, :], P[:, XA, :], ACT.Abs, bias=cols[:, R["b_dt"]:R["b_dt"] + 1]).then_inc(S["sp_abs"], 1)

        def act_softplus(eng, g):
            eng.wait_ge(S["sp_abs"], g + 1)
            a_.activation(sp[:, :], sp[:, :], ACT.Exp, scale=-1.0).then_inc(S["sp_exp"], 1)
            eng.wait_ge(S["sp_exp"], g + 1)
            a_.activation(sp[:, :], sp[:, :], ACT.Ln, bias=onet[:, 0:1]).then_inc(S["sp_ln"], 1)

        def act_b(eng, g, p):
            eng.wait_ge(S["b_mm"], g + 1)
            since(eng, "bm", NBLK * (g - 1))
            a_.activation(Bs[:, p, :], P[:, XC, :], ACT.Identity, bias=bbcol[:, 0:1]).then_inc(S["bs"], 1)

        def act_decay(eng, g, p, lo, hi):
            for m in range(lo, hi):
                if m % 4 == 0:
                    eng.wait_ge(S[f"dt_in{m // 4}"], 64 * (g + 1))
                j = block_of(m)
                steps = av[:, p, m, :].rearrange("p (h f) -> p h f", h=2)[:, :, 1:HW]
                a_.activation(steps, steps, ACT.Exp, scale=Aneg[:, j:j + 1]).then_inc(S["aexp"], 1)

        def act_lnF1(eng, g):
            eng.wait_ge(S["cen2"], g + 1)
            since(eng, "var2", g)
            a_.activation(sq2[:, :], P[:, XB, 0:HW], ACT.Square).then_inc(S["sq2"], 1)

        def act_lnF2(eng, g):
            eng.wait_ge(S["var2"], g + 1)
            since(eng, "tn", g)
            since(eng, "r2", g)
            a_.activation(rs2[:, :], P[:, XB, HW:T], ACT.Ln, bias=epst[:, 0:1]).then_inc(S["ln2"], 1)
            eng.wait_ge(S["ln2"], g + 1)
            a_.activation(rs2[:, :], rs2[:, :], ACT.Exp, scale=-0.5).then_inc(S["rs2"], 1)
            eng.wait_ge(S["rs2"], g + 1)
            since(eng, "vq", g)
            a_.activation(r2s[:, :], rs2[:, :], ACT.Square).then_inc(S["r2"], 1)

        def act_lnF3(eng, g):
            eng.wait_ge(S["vq"], g + 1)
            since(eng, "xn2", 2 * g)
            a_.activation(rqs[:, :], vqs[:, :], ACT.Ln, bias=epst[:, 0:1]).then_inc(S["lnq"], 1)
            eng.wait_ge(S["lnq"], g + 1)
            a_.activation(rqs[:, :], rqs[:, :], ACT.Exp, scale=-0.5).then_inc(S["rq"], 1)

        def act_router(eng, g):
            eng.wait_ge(S["dd"], g + 1)
            a_.activation(rt[:, 2], rt[:, 1], ACT.Exp).then_inc(S["ex"], 1)

        def act_wt(eng, g):
            eng.wait_ge(S["wtr"], 2 * (g + 1))
            since(eng, "wb_mm", EXP * g)
            a_.activation(wT[:, :], P[0:32, XB, 0:HW], ACT.Copy).then_inc(S["wtc"], 1)

        def act_wb(eng, g, lo, hi):
            for r in range(lo, hi):
                eng.wait_ge(S["wb_mm"], EXP * g + 2 * r + 2)
                if r == 0:
                    since(eng, "me", EXP * g)
                a_.activation(wbs[:, 2 * r:2 * r + 2, :].rearrange("p e f -> p (e f)"), P[:, (XB, XD)[r > 0], :], ACT.Copy).then_inc(S["wb"], 1)

        def act_gelu(eng, g):
            for r in range(EXP * KC):
                eng.wait_ge(S["f1"], EXP * KC * g + r + 1)
                since(eng, "f2", EXP * KC * g + max(r - 3, 0))
                a_.activation(hb[:, r % 4, :], P[:, (XA, XB)[r % 2], :], ACT.Gelu, bias=b1c[:, r:r + 1]).then_inc(S["gl"], 1)
                if r < EXP // 2 - 1:
                    act_wb(eng, g, r + 1, r + 2)

        @block.scalar
        def _(eng):
            for ap, src, sem in ((Wcv[:, :], W_conv, "ld_wssm"), (Als[:, :], A_log, "ld_wssm"), (Wins[0:64, :], W_in, "ld_wssm"),
                                 (Wins[64:128, :], W_in, "ld_wssm"), (Wbcs[:, :], W_bc, "ld_wssm"), (Wdts[:, :], W_dt, "ld_wssm"),
                                 (Wouts[:, :], W_out, "ld_wssm")):
                eng.dma_start(ap, src).then_inc(S[sem], 16)
            a_.preload_act_table_set("natural_log_exp_and_others")
            eng.wait_ge(S["k_misc"], 3)
            eng.wait_ge(S["gn_var"], 1)
            a_.activation(gvar[:, :], P[:, 0, 2 * HALF:3 * HALF], ACT.Ln, bias=epst[:, 0:1]).then_inc(S["gn_ln"], 1)
            eng.wait_ge(S["gn_ln"], 1)
            a_.activation(grs[:, :], gvar[:, :], ACT.Exp, scale=-0.5).then_inc(S["gn_rs"], 1)
            eng.wait_ge(S["prep1"], 4)
            eng.wait_ge(S["wmt_ev"], 2)
            a_.activation(Aexp[:, :], P[:, 7, 192:192 + NBLK], ACT.Exp).then_inc(S["a_exp"], 1)
            eng.wait_ge(S["ffn_g"], 1)
            a_.activation(W1H[:, :, :], W1g[:, :, :], ACT.Copy).then_inc(S["ffn_h"], 1)
            eng.wait_ge(S["r_add"], 3)
            for b in (0, HALF // 2):
                part = rT[:, :, :].rearrange("p (h b) n -> p h b n", h=2)[:, :, b:b + HALF // 2, :]
                a_.activation(part, part, ACT.Relu, scale=1.0 / 3.0).then_inc(S["r_ready"], 1)

            def body(i, p, nxt, nxt2, prev):
                q = 1 - p
                if nxt2 is not None:
                    act_lnA1(eng, nxt2)
                act_decay(eng, i, p, 1, 2)
                if nxt is not None:
                    act_abs(eng, nxt)
                if nxt2 is not None:
                    act_lnA2(eng, nxt2)
                if prev is not None:
                    act_lnF1(eng, prev)
                if nxt is not None:
                    act_softplus(eng, nxt)
                if prev is not None:
                    act_lnF2(eng, prev)
                if nxt is not None:
                    act_b(eng, nxt, q)
                act_decay(eng, i, p, 2, 3)
                if prev is not None:
                    act_lnF3(eng, prev)
                act_decay(eng, i, p, 3, 4)
                if prev is not None:
                    act_router(eng, prev)
                act_decay(eng, i, p, 4, 12)
                if prev is not None:
                    act_wt(eng, prev)
                    act_wb(eng, prev, 0, 1)
                act_decay(eng, i, p, 12, NBLK)
                if prev is not None:
                    a_.preload_act_table_set("gelu_and_others")
                    act_gelu(eng, prev)
                if nxt2 is not None:
                    a_.preload_act_table_set("silu_and_others")
                    act_siluz(eng, nxt2)
                    act_silug(eng, nxt2)
                a_.preload_act_table_set("natural_log_exp_and_others")
                if nxt is not None:
                    act_decay(eng, nxt, q, 0, 1)

            act_lnA1(eng, 0, XA)
            act_lnA2(eng, 0, XA)
            a_.preload_act_table_set("silu_and_others")
            act_siluz(eng, 0)
            act_silug(eng, 0)
            a_.preload_act_table_set("natural_log_exp_and_others")
            act_abs(eng, 0)
            act_b(eng, 0, 0)
            act_softplus(eng, 0)
            act_lnA1(eng, 1)
            act_lnA2(eng, 1)
            a_.preload_act_table_set("silu_and_others")
            act_siluz(eng, 1)
            act_silug(eng, 1)
            a_.preload_act_table_set("natural_log_exp_and_others")
            act_decay(eng, 0, 0, 0, 1)
            body(0, 0, 1, 2, None)
            body(1, 1, 2, 3, 0)
            with eng.Fori(0, LOOPS) as it:
                for par in range(2):
                    i = it * 2 + (2 + par)
                    body(i, par, i + 1, i + 2, i - 1)
            body(G - 2, 0, G - 1, None, G - 3)
            body(G - 1, 1, None, None, G - 2)
            act_lnF1(eng, G - 1)
            act_lnF2(eng, G - 1)
            act_lnF3(eng, G - 1)
            act_router(eng, G - 1)
            a_.preload_act_table_set("gelu_and_others")
            act_wt(eng, G - 1)
            act_wb(eng, G - 1, 0, 1)
            act_gelu(eng, G - 1)

        def dve_bm(eng, g, p, b):
            ub = P[:, b % UB, :]
            eng.wait_ge(S["ub"], NBLK * g + b + 1)
            if b == 0:
                eng.wait_ge(S["bs"], g + 1)
            v.tensor_tensor(ub, ub, Bs[:, p, :], ALU.mult).then_inc(S["bm"], 1)

        def dve_scan(eng, g, p, b):
            n = b // 2
            eng.wait_ge(S["bm"], NBLK * g + b + 1)
            eng.wait_ge(S["aexp"], NBLK * g + b + 1)
            if b % 2 == 0:
                since(eng, "ysum", 4 * g + n // 2 - 1)
            v.tensor_tensor_scan(hs[:, n % 4, b % 2, :], av[:, p, b, :], P[:, b % UB, :],
                                 0.0, ALU.mult, ALU.add).then_inc(S["scan"], 1)

        def dve_step(eng, g, p, b):
            if b + 1 < NBLK:
                dve_bm(eng, g, p, b + 1)
            dve_scan(eng, g, p, b)

        def dve_xn(eng, g, bank=XD):
            eng.wait_ge(S["rs1"], g + 1)
            since(eng, "xl1", g)
            for h in range(2):
                q = slice(64 * h, 64 * h + 64)
                v.tensor_tensor(xnt[:, HW * h:HW * h + HW], P[q, bank, 0:HW], rs[q, :], ALU.mult).then_inc(S["xn1"], 1)
            eng.wait_ge(S["xn1"], 2 * (g + 1))
            since(eng, "g_mm", g)
            v.tensor_copy(Xs[0:64, :], xnt[:, :]).then_inc(S["xh1"], 1)
            eng.wait_ge(S["xh1"], g + 1)
            v.tensor_tensor(Xs[64:128, :], xnt[:, :], Xs[0:64, :], ALU.subtract).then_inc(S["xl1"], 1)

        def dve_c(eng, g, p):
            eng.wait_ge(S["c_rep_mm"], g + 1)
            since(eng, "cm", SLOTS * (g - 1))
            v.tensor_scalar(Cs[:, p, :], P[:, XC, :], bbcol[:, 1:2], None, ALU.add).then_inc(S["cs"], 1)

        def dve_relu(eng, g):
            bdt = cols[:, R["b_dt"]:R["b_dt"] + 1]
            eng.wait_ge(S["sp_abs"], g + 1)
            v.tensor_scalar(rl[:, :], P[:, XA, :], bdt, 0.0, ALU.add, ALU.max).then_inc(S["sp_relu"], 1)

        def dve_keep_gate(eng, g, p):
            eng.wait_ge(S["sg"], g + 1)
            since(eng, "yg", g - 1)
            v.tensor_copy(sg[:, p, :], sg0[:, :]).then_inc(S["sgc"], 1)

        def dve_split(eng, g, p):
            eng.wait_ge(S["u"], g + 1)
            since(eng, "ub", NBLK * (g - 1))
            for half in range(2):
                hi = slice(64 * half, 64 * half + 64)
                v.tensor_copy(us[hi, p, half, :], u[hi, :]).then_inc(S["uh"], 1)
            eng.wait_ge(S["uh"], 2 * (g + 1))
            for half in range(2):
                hi, lo = slice(64 * half, 64 * half + 64), slice(64 - 64 * half, 128 - 64 * half)
                v.tensor_tensor(us[lo, p, half, :], u[hi, :], us[hi, p, half, :], ALU.subtract).then_inc(S["ul"], 1)

        def dve_gate(eng, g, p):
            eng.wait_ge(S["ysum"], 4 * (g + 1))
            eng.wait_ge(S["sgc"], g + 1)
            since(eng, "po", g)
            v.tensor_tensor(ygs[:, :], P[:, YS, :], sg[:, p, :], ALU.mult).then_inc(S["yg"], 1)

        def dve_t1(eng, g, p):
            eng.wait_ge(S["po"], g + 1)
            v.scalar_tensor_tensor(out=t1[:, p, :], in0=P[:, XC, 0:HW], scalar=cols[:, R["b_out"]:R["b_out"] + 1],
                                   in1=res[:, bass.ds(g * HW, HW)], op0=ALU.add, op1=ALU.add).then_inc(S["t1"], 1)

        def dve_lnF(eng, g):
            eng.wait_ge(S["rs2"], g + 1)
            since(eng, "lg", g)
            since(eng, "xn2", 2 * g)
            v.tensor_tensor(tns[:, :], P[:, XB, 0:HW], rs2[:, :], ALU.mult).then_inc(S["tn"], 1)
            eng.wait_ge(S["r2"], g + 1)
            since(eng, "lnq", g)
            v.tensor_tensor(vqs[:, :], P[:, XB, HW:T], r2s[:, :], ALU.mult).then_inc(S["vq"], 1)

        def dve_xn2(eng, g):
            eng.wait_ge(S["rq"], g + 1)
            eng.wait_ge(S["tn"], g + 1)
            since(eng, "xl2", g)
            for h in range(2):
                q = slice(64 * h, 64 * h + 64)
                v.tensor_tensor(xnt2[:, HW * h:HW * h + HW], tns[q, :], rqs[q, :], ALU.mult).then_inc(S["xn2"], 1)
            eng.wait_ge(S["xn2"], 2 * (g + 1))
            since(eng, "f1", EXP * KC * g)
            v.tensor_copy(X2[0:64, :], xnt2[:, :]).then_inc(S["xh2"], 1)
            eng.wait_ge(S["xh2"], g + 1)
            v.tensor_tensor(X2[64:128, :], xnt2[:, :], X2[0:64, :], ALU.subtract).then_inc(S["xl2"], 1)

        def dve_router1(eng, g):
            eng.wait_ge(S["lg"], 2 * (g + 1))
            since(eng, "dd", g)
            v.tensor_tensor(rt[:, 0], P[:, XB, 0:4 * EXP].rearrange("p (c e) -> p c e", e=EXP),
                            rep(brs[:, :], 1, 4), ALU.add).then_inc(S["lgb"], 1)
            eng.wait_ge(S["lgb"], g + 1)
            v.tensor_reduce(rv[:, 0], rt[:, 0], AX, ALU.max).then_inc(S["m1"], 1)
            eng.wait_ge(S["m1"], g + 1)
            since(eng, "ex", g)
            v.tensor_tensor(rt[:, 1], rt[:, 0], rep(rv[:, 0], 2, EXP), ALU.subtract).then_inc(S["dd"], 1)

        def dve_router2(eng, g):
            bc = lambda k: rep(rv[:, k], 2, EXP)
            eng.wait_ge(S["ex"], g + 1)
            v.scalar_tensor_tensor(out=rt[:, 3], in0=rt[:, 2], scalar=1.0, in1=rank[:, :, :], op0=ALU.is_ge, op1=ALU.mult).then_inc(S["s1"], 1)
            eng.wait_ge(S["s1"], g + 1)
            v.tensor_reduce(rv[:, 1], rt[:, 3], AX, ALU.max).then_inc(S["ms1"], 1)
            eng.wait_ge(S["ms1"], g + 1)
            v.tensor_tensor(rt[:, 4], rt[:, 3], bc(1), ALU.is_equal).then_inc(S["o1"], 1)
            eng.wait_ge(S["o1"], g + 1)
            v.scalar_tensor_tensor(out=rt[:, 5], in0=rt[:, 4], scalar=-2.0, in1=rt[:, 2], op0=ALU.mult, op1=ALU.add).then_inc(S["e2"], 1)
            eng.wait_ge(S["e2"], g + 1)
            v.tensor_reduce(rv[:, 2], rt[:, 5], AX, ALU.max).then_inc(S["m2"], 1)
            eng.wait_ge(S["m2"], g + 1)
            v.tensor_tensor(rt[:, 6], rt[:, 5], bc(2), ALU.is_equal).then_inc(S["s2"], 1)
            v.tensor_scalar(rv[:, 4], rv[:, 2], 1.0, None, ALU.add).then_inc(S["den"], 1)
            eng.wait_ge(S["s2"], g + 1)
            v.tensor_tensor(rt[:, 7], rt[:, 6], rank[:, :, :], ALU.mult).then_inc(S["s2r"], 1)
            eng.wait_ge(S["den"], g + 1)
            v.reciprocal(rv[:, 5], rv[:, 4]).then_inc(S["rden"], 1)
            eng.wait_ge(S["s2r"], g + 1)
            v.tensor_reduce(rv[:, 3], rt[:, 7], AX, ALU.max).then_inc(S["ms2"], 1)
            eng.wait_ge(S["ms2"], g + 1)
            v.tensor_tensor(rt[:, 8], rt[:, 7], bc(3), ALU.is_equal).then_inc(S["o2"], 1)
            eng.wait_ge(S["o2"], g + 1)
            v.tensor_tensor(rt[:, 9], rt[:, 8], bc(2), ALU.mult).then_inc(S["num"], 1)
            eng.wait_ge(S["num"], g + 1)
            v.tensor_tensor(rt[:, 10], rt[:, 9], rt[:, 4], ALU.add).then_inc(S["wt"], 1)
            eng.wait_ge(S["wt"], g + 1)
            eng.wait_ge(S["rden"], g + 1)
            v.tensor_tensor(rt[:, 11], rt[:, 10], bc(5), ALU.mult).then_inc(S["vhi"], 1)
            eng.wait_ge(S["vhi"], 2 * g + 1)
            w4 = rt[:, 11].rearrange("p (q h) e -> p q h e", h=2)
            since(eng, "wtr", 2 * g)
            v.tensor_copy(vv[:, :, :, 0, :].bitcast(f32r), w4).then_inc(S["vhi"], 1)
            eng.wait_ge(S["vhi"], 2 * g + 2)
            v.tensor_tensor(vv[:, :, :, 1, :], w4, vv[:, :, :, 0, :], ALU.subtract).then_inc(S["vlo"], 1)

        def dve_expert(eng, g, e):
            if e % 2 == 0:
                eng.wait_ge(S["f2"], EXP * KC * g + 2 * KC * (e // 2 + 1))
                eng.wait_ge(S["wb"], EXP // 2 * g + e // 2 + 1)
            since(eng, "acc", EXP * g + max(e - 3, 0))
            v.scalar_tensor_tensor(out=mes[:, e % 4, :], in0=P[:, (XC, XD)[e // 2 % 2], HW * (e % 2):HW * (e % 2) + HW],
                                   scalar=cols[:, R["b2"] + e:R["b2"] + e + 1], in1=wbs[:, e, :],
                                   op0=ALU.add, op1=ALU.mult).then_inc(S["me"], 1)

        @block.vector
        def _(eng):
            rv3 = res[:, :].rearrange("p (b f) -> p b f", b=HALF)
            for b in range(HALF):
                if b % (HALF // 2) == 0:
                    eng.wait_ge(S["ld_x%d" % (b // (HALF // 2))], 32)
                v.bn_stats(stats[:, b, :], rv3[:, b, :]).then_inc(S["gn_stat"], 1)
            eng.wait_ge(S["gn_stat"], HALF)
            for b in range(HALF):
                v.bn_aggr(mv[:, b, :], stats[:, b, :]).then_inc(S["gn_agg"], 1)
            eng.wait_ge(S["gn_agg"], HALF)
            eng.wait_ge(S["gn_avg"], 1)
            v.tensor_copy(gmean[:, :], P[:, 0, 0:HALF]).then_inc(S["gn_dev"], 1)
            eng.wait_ge(S["gn_dev"], 1)
            v.tensor_tensor(gdev[:, 0, :], mv[:, :, 0], gmean[:, :], ALU.subtract).then_inc(S["gn_dev"], 1)
            eng.wait_ge(S["gn_dev"], 2)
            v.tensor_tensor(gdev[:, 0, :], gdev[:, 0, :], gdev[:, 0, :], ALU.mult).then_inc(S["gn_dsq"], 1)
            eng.wait_ge(S["gn_dsq"], 1)
            v.tensor_tensor(gdev[:, 1, :], gdev[:, 0, :], mv[:, :, 1], ALU.add).then_inc(S["gn_dsq"], 1)
            eng.wait_ge(S["gn_rs"], 1)
            for b in range(HALF):
                v.tensor_scalar(gn[:, b, :], rv3[:, b, :], gmean[:, b:b + 1], grs[:, b:b + 1], ALU.subtract, ALU.mult).then_inc(S["gn_out"], 1)
            eng.wait_ge(S["k_ident"], 1)
            v.tensor_reduce(mask8[:, :], ident[:, :].rearrange("p (j e) -> p e j", e=BLK), AX, ALU.add).then_inc(S["k_mask"], 1)
            eng.wait_ge(S["ld_wssm"], 112)
            eng.wait_ge(S["k_mask"], 1)
            v.tensor_tensor(Asel[:, :, :], rep(Als[:, :], 2, BLK), rep(mask8[:, :], 1, ST), ALU.mult).then_inc(S["a_selx"], 1)

            def features(fh):
                for c in range(2):
                    eng.wait_ge(S["ht_mm"], 2 * fh + c + 1)
                    v.tensor_tensor(hT[:, fh].rearrange("p (h b) n -> p b h n", h=2)[:, 4 * c:4 * c + 4],
                                    P[:, 2 * fh + c, :].rearrange("p (b h n) -> p b h n", h=2, n=NODES),
                                    rep(rep(cb1s[:, :], 1, 2), 1, 4), ALU.add).then_inc(S["ht_ev"], 1)

            eng.wait_ge(S["ld_wgn"], 48)
            features(0)
            features(1)
            eng.wait_ge(S["ld_rows"], 16 * 16)
            v.tensor_copy(bbx[:, :, :], rep(bbc[:, :], 2, BLK)).then_inc(S["bbx"], 1)
            eng.wait_ge(S["ht_ev"], 4)
            for ti, t in enumerate("ABC"):
                lo, hi = NODE[t]
                for fh in range(2):
                    v.tensor_reduce(mu[:, ti, fh, :], hT[:, fh, :, lo:hi], AX, ALU.add).then_inc(S["mu_ready"], 1)
            eng.wait_ge(S["mu_ready"], 6)
            for ti, t in enumerate("ABC"):
                lo, hi = NODE[t]
                v.tensor_scalar(mu[:, ti], mu[:, ti], 1.0 / (hi - lo), None, ALU.mult).then_inc(S["mu_ready"], 1)
            eng.wait_ge(S["prep1"], 4)
            v.tensor_copy(bbcol[:, :], P[:, 7, 208:210]).then_inc(S["bbcol"], 1)
            v.tensor_copy(cols[:, :], P[:, 7, 0:NROWS]).then_inc(S["cols_ev"], 1)
            for h in range(2):
                v.tensor_copy(WmT2[:, h, :], P[:, 7, 128:192]).then_inc(S["wmt_ev"], 1)
            eng.wait_ge(S["cols_ev"], 1)
            for ti, t in enumerate("ABC"):
                e0, e1, e2 = (R["bl"] + i for i in node_edges(t))
                v.tensor_tensor(blsum[:, ti:ti + 1], cols[:, e0:e0 + 1], cols[:, e1:e1 + 1], ALU.add).then_inc(S["bls_ready"], 1)
            eng.wait_ge(S["bls_ready"], 3)
            for ti, t in enumerate("ABC"):
                e2 = R["bl"] + node_edges(t)[2]
                v.tensor_tensor(blsum[:, ti:ti + 1], blsum[:, ti:ti + 1], cols[:, e2:e2 + 1], ALU.add).then_inc(S["bls_ready"], 1)
            eng.wait_ge(S["bls_ready"], 6)
            eng.wait_ge(S["prep2"], 2)
            v.tensor_copy(WzH[:, :], P[:, 7, 0:128]).then_inc(S["wz_hi"], 1)
            v.tensor_copy(WgH[:, :], Wins[:, INNER:2 * INNER]).then_inc(S["wz_hi"], 1)
            eng.wait_ge(S["wz_hi"], 2)
            v.tensor_tensor(WzL[:, :], P[:, 7, 0:128], WzH[:, :], ALU.subtract).then_inc(S["wz_lo"], 1)
            v.tensor_tensor(WgL[:, :], Wins[:, INNER:2 * INNER], WgH[:, :], ALU.subtract).then_inc(S["wz_lo"], 1)
            v.tensor_tensor(bz[:, :], P[:, 7, 128:129], cols[:, R["b_conv"]:R["b_conv"] + 1], ALU.add).then_inc(S["bz"], 1)
            eng.wait_ge(S["a_exp"], 1)
            v.tensor_scalar(Aneg[:, :], Aexp[:, :], -1.0, None, ALU.mult).then_inc(S["a_neg"], 1)
            for i in range(2):
                v.tensor_copy(Wrep[:, i], rep(Wbcs[:, ST * i:ST * i + ST], 2, BLK)).then_inc(S["wbr"], 1)
            for ti, t in enumerate("ABC"):
                eng.wait_ge(S["c_mm"], 3)
                v.tensor_scalar(cT[:, ti, :], P[:, 6, B * ti:B * ti + B], blsum[:, ti:ti + 1], None, ALU.add).then_inc(S["c_ev"], 1)
            eng.wait_ge(S["c_ev"], 3)
            eng.wait_ge(S["o_mm"], 3)
            for ti, t in enumerate("ABC"):
                lo, hi = NODE[t]
                n = hi - lo
                bank, at = ((4, 0), (5, 0), (5, B * n))[ti]
                v.tensor_tensor(rT[:, :, lo:hi], P[:, bank, at:at + B * n].rearrange("p (b n) -> p b n", n=n),
                                rep(cT[:, ti, :], 2, n), ALU.add).then_inc(S["r_add"], 1)
            both = [rep(ident[:, 64 * half:64 * half + 64].rearrange("p (j e) -> p j e", e=BLK), 2, ST) for half in range(2)]
            v.tensor_tensor(selU[:, :, :].rearrange("p j (s e) -> p j s e", e=BLK), both[0], both[1], ALU.add).then_inc(S["k_selu"], 1)
            eng.wait_ge(S["k_zero"], 8)
            for k in range(4):
                v.tensor_copy(selS[:, k, BLK * k:BLK * k + BLK], mask8[:, :]).then_inc(S["k_selu"], 1)
            eng.wait_ge(S["k_sel"], 6)
            v.tensor_copy(selW[:, :, :], selWf[:, :, :, :].rearrange("p e h d -> p e (h d)")).then_inc(S["k_selw"], 1)
            eng.wait_ge(S["ld_wf"], 64)
            eng.wait_ge(S["ht_mm"], 4)

            def outputs(c):
                eng.wait_ge(S["out_mm"], c + 1)
                v.tensor_tensor(gn[:, 2 * c:2 * c + 2, :], P[:, c, :].rearrange("p (b f) -> p b f", f=HW),
                                rep(bfs[:, :], 1, 2), ALU.add).then_inc(S["out_ev"], 1)

            def residual(c):
                eng.wait_ge(S["y_mm"], c + 1)
                v.scalar_tensor_tensor(out=res[:, 512 * c:512 * c + 512], in0=P[:, 4 + c, :], scalar=cols[:, R["cb2"]:R["cb2"] + 1],
                                       in1=res[:, 512 * c:512 * c + 512], op0=ALU.add, op1=ALU.add).then_inc(S["res_ready"], 1)

            outputs(0)
            outputs(1)
            residual(0)
            outputs(2)
            residual(1)
            outputs(3)
            residual(2)
            residual(3)

            def body(i, p, nxt, nxt2, prev):
                q = 1 - p
                if prev is not None:
                    dve_gate(eng, prev, q)
                dve_step(eng, i, p, 0)
                if prev is not None:
                    dve_t1(eng, prev, q)
                if nxt is not None:
                    dve_keep_gate(eng, nxt, q)
                    dve_relu(eng, nxt)
                if nxt2 is not None:
                    dve_xn(eng, nxt2)
                dve_step(eng, i, p, 1)
                if prev is not None:
                    dve_lnF(eng, prev)
                dve_step(eng, i, p, 2)
                if prev is not None:
                    dve_router1(eng, prev)
                dve_step(eng, i, p, 3)
                if prev is not None:
                    dve_router2(eng, prev)
                if nxt is not None:
                    dve_c(eng, nxt, q)
                for b in range(4, 6):
                    dve_step(eng, i, p, b)
                if prev is not None:
                    dve_xn2(eng, prev)
                for b in range(6, 8):
                    dve_step(eng, i, p, b)
                if nxt is not None:
                    dve_split(eng, nxt, q)
                for b in range(8, 13):
                    dve_step(eng, i, p, b)
                if prev is not None:
                    dve_expert(eng, prev, 0)
                    dve_expert(eng, prev, 1)
                dve_step(eng, i, p, 13)
                if prev is not None:
                    dve_expert(eng, prev, 2)
                    dve_expert(eng, prev, 3)
                for b in range(14, 16):
                    dve_step(eng, i, p, b)
                if prev is not None:
                    for e in range(4, 8):
                        dve_expert(eng, prev, e)
                if nxt is not None:
                    dve_bm(eng, nxt, q, 0)

            dve_xn(eng, 0, XA)
            dve_keep_gate(eng, 0, 0)
            dve_relu(eng, 0)
            dve_c(eng, 0, 0)
            step_input(eng, v, 0, 0)
            dve_split(eng, 0, 0)
            dve_xn(eng, 1)
            dve_bm(eng, 0, 0, 0)
            body(0, 0, 1, 2, None)
            eng.wait_ge(S["prep2"], 3)
            v.tensor_tensor(b1c[:, :], P[:, XB, 0:EXP * KC], cols[:, R["b1"]:R["b1"] + EXP * KC], ALU.add).then_inc(S["b1c"], 1)
            body(1, 1, 2, 3, 0)
            with eng.Fori(0, LOOPS) as it:
                for par in range(2):
                    i = it * 2 + (2 + par)
                    body(i, par, i + 1, i + 2, i - 1)
            body(G - 2, 0, G - 1, None, G - 3)
            body(G - 1, 1, None, None, G - 2)
            dve_gate(eng, G - 1, 1)
            dve_t1(eng, G - 1, 1)
            dve_lnF(eng, G - 1)
            dve_router1(eng, G - 1)
            dve_xn2(eng, G - 1)
            dve_router2(eng, G - 1)
            for e in range(EXP):
                dve_expert(eng, G - 1, e)

        def pe_ub(eng, g, p, b):
            if b == 0:
                eng.wait_ge(S["ul"], 2 * (g + 1))
                since(eng, "scan", NBLK * g)
            if b >= UB:
                eng.wait_ge(S["scan"], NBLK * g + b - UB + 1)
            half, j = divmod(block_of(b), NBLK // 2)
            pe.matmul(P[:, b % UB, :], selU[:, j, :], us[:, p, half, :], start=True, stop=True).then_inc(S["ub"], 1)

        def pe_sum(eng, g, k):
            eng.wait_ge(S["cm"], SLOTS * g + 2 * k + 2)
            if k == 0:
                since(eng, "yg", g)
            for q in range(4):
                n = 2 * k + q // 2
                last = pe.matmul(P[32 * q:32 * q + 32, YS, :], selS[:, k, :], hs[:, n % 4, q % 2, :],
                                 start=(k == 0), stop=(k == 3))
            last.then_inc(S["ysum"], 1)

        def pe_cenA(eng, g, bank=XD):
            since(eng, "me", EXP * (g - 3))
            pe.matmul(P[:, bank, 0:HW], cen_m[:, :], res[:, bass.ds(g * HW, HW)], start=True, stop=True).then_inc(S["cen1"], 1)

        def pe_varA(eng, g, bank=XD):
            eng.wait_ge(S["sq1"], g + 1)
            pe.matmul(P[:, bank, HW:T], avg_m[:, :], sq[:, :], start=True, stop=True).then_inc(S["var1"], 1)

        def pe_projz(eng, g):
            eng.wait_ge(S["xl1"], g + 1)
            since(eng, "sp_relu", g)
            since(eng, "gl", EXP * KC * (g - 2) - 1)
            pe.matmul(P[:, XA, :], WzH[:, :], Xs[:, :], start=True, stop=False)
            pe.matmul(P[:, XA, :], WzL[:, :], Xs[:, :], start=False, stop=True).then_inc(S["z_mm"], 1)

        def pe_projg(eng, g):
            since(eng, "cs", g)
            since(eng, "me", EXP * (g - 2) - 2)
            pe.matmul(P[:, XC, :], WgH[:, :], Xs[:, :], start=True, stop=False)
            pe.matmul(P[:, XC, :], WgL[:, :], Xs[:, :], start=False, stop=True).then_inc(S["g_mm"], 1)

        def pe_dtz(eng, g):
            eng.wait_ge(S["xc"], g + 1)
            pe.matmul(P[:, XA, :], Wdts[:, :], xc[:, :], start=True, stop=True).then_inc(S["dtz_mm"], 1)

        def pe_b(eng, g):
            eng.wait_ge(S["sg"], g + 1)
            since(eng, "t1", g - 1)
            pe.matmul(P[:, XC, :], Wrep[:, 0].rearrange("p s e -> p (s e)"), xc[:, :], start=True, stop=True).then_inc(S["b_mm"], 1)

        def pe_c(eng, g):
            eng.wait_ge(S["bs"], g + 1)
            pe.matmul(P[:, XC, :], Wrep[:, 1].rearrange("p s e -> p (s e)"), xc[:, :], start=True, stop=True).then_inc(S["c_rep_mm"], 1)

        def pe_po(eng, g):
            eng.wait_ge(S["yg"], g + 1)
            since(eng, "me", EXP * g)
            eng.wait_ge(S["sg"], so_far(g, 3))
            for h in range(2):
                last = pe.matmul(P[64 * h:64 * h + 64, XC, 0:HW], Wouts[:, :], ygs[:, HW * h:HW * h + HW], start=True, stop=True)
            last.then_inc(S["po"], 1)

        def pe_cenF(eng, g, p):
            eng.wait_ge(S["t1"], g + 1)
            since(eng, "gl", EXP * KC * g)
            pe.matmul(P[:, XB, 0:HW], cen_m[:, :], t1[:, p, :], start=True, stop=True).then_inc(S["cen2"], 1)

        def pe_varF(eng, g):
            eng.wait_ge(S["sq2"], g + 1)
            pe.matmul(P[:, XB, HW:T], avg_m[:, :], sq2[:, :], start=True, stop=True).then_inc(S["var2"], 1)

        def pe_router(eng, g):
            eng.wait_ge(S["tn"], g + 1)
            eng.wait_ge(S["vq"], g + 1)
            for q in range(2):
                pe.matmul(P[:, XB, 2 * EXP * q:2 * EXP * q + 2 * EXP], tns[:, 128 * q:128 * q + 128],
                          Wrt[:, :, :].rearrange("p h e -> p (h e)"), start=True, stop=True).then_inc(S["lg"], 1)

        def pe_wt(eng, g):
            eng.wait_ge(S["vlo"], g + 1)
            for q in range(2):
                pe.transpose(P[0:32, XB, 128 * q:128 * q + 128], vv[:, q].rearrange("p h r e -> p (h r e)"), ident[:, :]).then_inc(S["wtr"], 1)
            eng.wait_ge(S["wtc"], g + 1)

        def pe_wb(eng, g, lo, hi):
            for r in range(lo, hi):
                if r == 1:
                    since(eng, "me", EXP * g)
                    eng.wait_ge(S["xn1"], 2 * so_far(g, 4))
                if r >= 2:
                    eng.wait_ge(S["wb"], EXP // 2 * g + r)
                for e in (2 * r, 2 * r + 1):
                    pe.matmul(P[:, (XB, XD)[r > 0], HW * (e % 2):HW * (e % 2) + HW], selW[:, e, :], wT[:, :],
                              start=True, stop=True).then_inc(S["wb_mm"], 1)

        def pe_f1(eng, g, r):
            e, k = r // KC, r % KC
            if r == 0:
                eng.wait_ge(S["xl2"], g + 1)
                eng.wait_ge(S["sp_relu"], so_far(g, 2))
            if r == 1:
                eng.wait_ge(S["wb"], EXP // 2 * g + 1)
            if r >= 2:
                eng.wait_ge(S["gl"], EXP * KC * g + r - 1)
            bank = (XA, XB)[r % 2]
            pe.matmul(P[:, bank, :], W1H[:, e, 128 * k:128 * k + 128], X2[:, :], start=True, stop=False)
            pe.matmul(P[:, bank, :], W1L[:, e, 128 * k:128 * k + 128], X2[:, :], start=False, stop=True).then_inc(S["f1"], 1)

        def pe_f2(eng, g, r):
            e, k = r // KC, r % KC
            eng.wait_ge(S["gl"], EXP * KC * g + r + 1)
            pair = r // (2 * KC)
            if r == 0:
                eng.wait_ge(S["cs"], so_far(g, 2))
            if r == 2 * KC:
                eng.wait_ge(S["wb"], EXP // 2 * (g + 1))
            if r % (2 * KC) == 0 and pair >= 2:
                eng.wait_ge(S["me"], EXP * g + 2 * (pair - 1))
            for h in range(2):
                last = pe.matmul(P[64 * h:64 * h + 64, (XC, XD)[pair % 2], HW * (e % 2):HW * (e % 2) + HW], W2s[:, e, k, :],
                                 hb[:, r % 4, HW * h:HW * h + HW], start=(k == 0), stop=(k == KC - 1))
            last.then_inc(S["f2"], 1)

        def pe_ffn(eng, g, lo, hi):
            for r in range(lo, hi):
                if r < EXP * KC:
                    pe_f1(eng, g, r)
                if r >= 2:
                    pe_f2(eng, g, r - 2)
                if r in (2, 3):
                    pe_wb(eng, g, r, r + 1)

        @block.tensor
        def _(eng):
            eng.wait_ge(S["k_sel"], 6)
            eng.wait_ge(S["gn_agg"], HALF)
            pe.matmul(P[:, 0, 0:HALF], pair_m[:, :], mv[:, :, 0], start=True, stop=True).then_inc(S["gn_avg"], 1)
            eng.wait_ge(S["gn_dsq"], 2)
            pe.matmul(P[:, 0, 2 * HALF:3 * HALF], pair_m[:, :], gdev[:, 1, :], start=True, stop=True).then_inc(S["gn_var"], 1)
            eng.wait_ge(S["ld_wgn"], 48)
            eng.wait_ge(S["gn_ln"], 1)

            def features(fh):
                for b in range(HALF):
                    if fh == 0:
                        eng.wait_ge(S["gn_out"], b + 1)
                    last = pe.matmul(P[:, 2 * fh + b // 4, 128 * (b % 4):128 * (b % 4) + 128], gn[:, b, 128 * fh:128 * fh + 128],
                                     cW1bd[:, :], start=True, stop=True)
                    if b % 4 == 3:
                        last.then_inc(S["ht_mm"], 1)

            features(0)
            features(1)
            eng.wait_ge(S["k_ident"], 1)
            eng.wait_ge(S["ld_rows"], 16 * 16)
            pe.transpose(P[:, 7, 0:NROWS], rows[:, :], ident[0:NROWS, 0:NROWS]).then_inc(S["prep1"], 1)
            eng.wait_ge(S["ld_wssm"], 112)
            pe.transpose(P[:, 7, 128:192], Wins[0:64, 0:128], ident[0:64, 0:64]).then_inc(S["prep1"], 1)
            eng.wait_ge(S["a_selx"], 1)
            pe.matmul(P[:, 7, 192:192 + NBLK], Asel[:, :, :].rearrange("p s e -> p (s e)"), gsel[:, :], start=True, stop=True).then_inc(S["prep1"], 1)
            eng.wait_ge(S["bbx"], 1)
            pe.transpose(P[:, 7, 208:210], bbx[:, :, :].rearrange("p s e -> p (s e)"), ident[0:2, 0:2]).then_inc(S["prep1"], 1)
            eng.wait_ge(S["wrs_ready"], 6)
            eng.wait_ge(S["ht_ev"], 4)
            for ti, t in enumerate("ABC"):
                lo, hi = NODE[t]
                n = hi - lo
                bank, at = ((4, 0), (5, 0), (5, B * n))[ti]
                for fh in range(2):
                    last = pe.matmul(P[:, bank, at:at + B * n], Wrsum[:, ti, fh, :], hT[:, fh, :, lo:hi], start=(fh == 0), stop=(fh == 1))
                last.then_inc(S["o_mm"], 1)
            eng.wait_ge(S["wmt_ev"], 2)
            eng.wait_ge(S["a_exp"], 1)
            pe.matmul(P[:, 7, 0:128], WmT2[:, :, :].rearrange("p h d -> p (h d)"), Wcv[:, :], start=True, stop=True).then_inc(S["prep2"], 1)
            pe.matmul(P[:, 7, 128:129], Wcv[:, :], cols[:, R["b_in"]:R["b_in"] + 1], start=True, stop=True).then_inc(S["prep2"], 1)
            eng.wait_ge(S["ld_wl"], 32)
            eng.wait_ge(S["mu_ready"], 9)
            for ti, t in enumerate("ABC"):
                todo = [(i, fh) for i in node_edges(t) for fh in range(2)]
                for n, (i, fh) in enumerate(todo):
                    last = pe.matmul(P[:, 6, B * ti:B * ti + B], Wls[:, i, fh, :], mu[:, "ABC".index(EDGES[i][0]), fh, :],
                                     start=(n == 0), stop=(n == len(todo) - 1))
                last.then_inc(S["c_mm"], 1)
            eng.wait_ge(S["ld_wf"], 64)

            def outputs(c):
                eng.wait_ge(S["r_ready"], c // 2 + 1)
                for b in range(2 * c, 2 * c + 2):
                    for h in range(2):
                        last = pe.matmul(P[64 * h:64 * h + 64, c, HW * (b % 2):HW * (b % 2) + HW], rT[:, HALF * h + b, :], Wfs[:, :],
                                         start=True, stop=True)
                last.then_inc(S["out_mm"], 1)

            def mixed(c):
                eng.wait_ge(S["out_ev"], c + 1)
                pe.matmul(P[:, 4 + c, :], cW2bd[:, :], gn[:, 2 * c:2 * c + 2, :].rearrange("p b f -> p (b f)"), start=True, stop=True).then_inc(S["y_mm"], 1)

            outputs(0)
            outputs(1)
            eng.wait_ge(S["c_ev"], 3)
            eng.wait_ge(S["r_add"], 3)
            eng.wait_ge(S["wz_lo"], 2)
            eng.wait_ge(S["bz"], 1)
            mixed(0)
            outputs(2)
            mixed(1)
            outputs(3)
            eng.wait_ge(S["k_misc"], 13)
            eng.wait_ge(S["res_ready"], 1)
            pe_cenA(eng, 0, XA)
            mixed(2)
            mixed(3)
            pe_varA(eng, 0, XA)
            pe_projz(eng, 0)
            eng.wait_ge(S["res_ready"], 4)
            pe_projg(eng, 0)
            pe_cenA(eng, 1)
            pe_dtz(eng, 0)
            eng.wait_ge(S["wbr"], 2)
            pe_b(eng, 0)
            pe_c(eng, 0)
            pe_varA(eng, 1)
            eng.wait_ge(S["ld_ffn"], 32)
            for e in range(EXP):
                for k in range(KC):
                    last = pe.matmul(P[:, XB, KC * e + k:KC * e + k + 1], W1r[0:64, e, 128 * k:128 * k + 128],
                                     cols[0:64, R["ln_b"] + e:R["ln_b"] + e + 1], start=True, stop=True)
            last.then_inc(S["prep2"], 1)
            pe_projz(eng, 1)
            pe_projg(eng, 1)
            eng.wait_ge(S["k_selu"], 5)

            def body(i, p, nxt, nxt2, prev):
                q = 1 - p
                if nxt2 is not None:
                    pe_cenA(eng, nxt2)
                if nxt is not None:
                    pe_dtz(eng, nxt)
                if prev is not None:
                    pe_po(eng, prev)
                if nxt2 is not None:
                    pe_varA(eng, nxt2)
                pe_ub(eng, i, p, 3)
                if prev is not None:
                    pe_cenF(eng, prev, q)
                if nxt is not None:
                    pe_b(eng, nxt)
                if prev is not None:
                    pe_varF(eng, prev)
                    pe_router(eng, prev)
                for b in range(4, 7):
                    pe_ub(eng, i, p, b)
                if nxt is not None:
                    pe_c(eng, nxt)
                if prev is not None:
                    pe_wt(eng, prev)
                    pe_wb(eng, prev, 0, 2)
                pe_sum(eng, i, 0)
                for b in range(7, 9):
                    pe_ub(eng, i, p, b)
                if prev is not None:
                    pe_ffn(eng, prev, 0, 2)
                pe_ub(eng, i, p, 9)
                if prev is not None:
                    pe_ffn(eng, prev, 2, 4)
                pe_ub(eng, i, p, 10)
                if prev is not None:
                    pe_ffn(eng, prev, 4, 5)
                pe_sum(eng, i, 1)
                pe_ub(eng, i, p, 11)
                if prev is not None:
                    pe_ffn(eng, prev, 5, 6)
                pe_ub(eng, i, p, 12)
                if prev is not None:
                    pe_ffn(eng, prev, 6, 8)
                pe_ub(eng, i, p, 13)
                if prev is not None:
                    pe_ffn(eng, prev, 8, 10)
                pe_ub(eng, i, p, 14)
                if prev is not None:
                    pe_ffn(eng, prev, 10, 11)
                pe_ub(eng, i, p, 15)
                if prev is not None:
                    pe_ffn(eng, prev, 11, 12)
                pe_sum(eng, i, 2)
                if prev is not None:
                    pe_ffn(eng, prev, 12, 17)
                if nxt2 is not None:
                    pe_projz(eng, nxt2)
                if prev is not None:
                    pe_ffn(eng, prev, 17, 18)
                if nxt2 is not None:
                    pe_projg(eng, nxt2)
                if nxt is not None:
                    for b in range(0, 2):
                        pe_ub(eng, nxt, q, b)
                pe_sum(eng, i, 3)
                if nxt is not None:
                    pe_ub(eng, nxt, q, 2)

            for b in range(UB):
                pe_ub(eng, 0, 0, b)
            body(0, 0, 1, 2, None)
            eng.wait_ge(S["k_selw"], 1)
            eng.wait_ge(S["ld_dup"], 64)
            eng.wait_ge(S["ffn_l"], 1)
            eng.wait_ge(S["b1c"], 1)
            body(1, 1, 2, 3, 0)
            with eng.Fori(0, LOOPS) as it:
                for par in range(2):
                    i = it * 2 + (2 + par)
                    body(i, par, i + 1, i + 2, i - 1)
            body(G - 2, 0, G - 1, None, G - 3)
            body(G - 1, 1, None, None, G - 2)
            pe_po(eng, G - 1)
            pe_cenF(eng, G - 1, 1)
            pe_varF(eng, G - 1)
            pe_router(eng, G - 1)
            pe_wt(eng, G - 1)
            pe_wb(eng, G - 1, 0, 2)
            pe_ffn(eng, G - 1, 0, 18)


_INS = [('x', 'x'), ('L0_conv_W1', 'cW1'), ('L0_conv_b1', 'cb1'), ('L0_conv_Wl', 'Wl'), ('L0_conv_bl', 'bl'),
        ('L0_conv_Wr', 'Wr'), ('L0_conv_Wf', 'Wf'), ('L0_conv_bf', 'bf'), ('L0_conv_W2', 'cW2'), ('L0_conv_b2', 'cb2'),
        ('L1_attn_W_in', 'W_in'), ('L1_attn_b_in', 'b_in'), ('L1_attn_W_conv', 'W_conv'), ('L1_attn_b_conv', 'b_conv'),
        ('L1_attn_A_log', 'A_log'), ('L1_attn_W_bc', 'W_bc'), ('L1_attn_b_bc', 'b_bc'), ('L1_attn_W_dt', 'W_dt'),
        ('L1_attn_b_dt', 'b_dt'), ('L1_attn_W_out', 'W_out'), ('L1_attn_b_out', 'b_out'), ('L1_ffn_Wr', 'fWr'),
        ('L1_ffn_br', 'fbr'), ('L1_ffn_ln_g', 'ln_g'), ('L1_ffn_ln_b', 'ln_b'), ('L1_ffn_W1', 'W1'), ('L1_ffn_b1', 'b1'),
        ('L1_ffn_W2', 'W2'), ('L1_ffn_b2', 'b2')]


def kernel(**inputs):
    import numpy as _np
    import concourse.bacc as _bacc
    from concourse import mybir as _mybir
    from concourse.bass_utils import run_bass_kernel_spmd as _run

    nc = _bacc.Bacc("TRN2", target_bir_lowering=False, num_devices=1)
    arrays, args = {}, {}
    for name, short in _INS:
        a = _np.ascontiguousarray(inputs[name])
        arrays[f"in_{name}"] = a
        args[short] = nc.dram_tensor(f"in_{name}", a.shape, _mybir.dt.from_np(a.dtype), kind="ExternalInput").ap()
    args["out"] = nc.dram_tensor("out_0", (B, D, 16, 16), _mybir.dt.float32, kind="ExternalOutput").ap()
    build(nc, **args)
    r = _run(nc, [arrays], core_ids=[0])
    return r.results[0]["out_0"]
```
